# Optimizing a Trainium2 kernel written in Bass

```python
import numpy as np
import jax
import jax.numpy as jnp

def _softmax(x, axis=-1):
    return jax.nn.softmax(x, axis=axis)

def _gelu(x):
    return jax.nn.gelu(x, approximate=True)

def _silu(x):
    return jax.nn.silu(x)

def _sigmoid(x):
    return jax.nn.sigmoid(x)

def _layernorm(x, axis=-1, eps=1e-05):
    m = jnp.mean(x, axis=axis, keepdims=True)
    v = jnp.var(x, axis=axis, keepdims=True)
    return (x - m) / jnp.sqrt(v + eps)

def _scatter_add(tgt, idx, src, axis=0):
    return tgt.at[idx].add(src)

def _segment_sum(src, seg, n):
    return jax.ops.segment_sum(src, seg, n)
kernel_name = 'mk_decoder_preln_d1_seqx_r8_15249b'

def setup_inputs(seed: int=0):
    np.random.seed(seed)
    _w = jnp.asarray

    def _rec_inputs():
        import jax
        import jax.numpy as jnp
        _rk = jax.random.key(seed)
        x = -0.0002928 + 1 * jax.random.normal(jax.random.fold_in(_rk, 1), (16, 64, 128), jnp.float32)
        _lenS = 64 - jax.random.randint(jax.random.fold_in(_rk, 7), (16,), 0, max(1, 64 // 4) + 1, jnp.int32)
        _lenS2 = 64 - jax.random.randint(jax.random.fold_in(_rk, 8), (16,), 0, max(1, 64 // 4) + 1, jnp.int32)
        _ctx_1024P = jax.random.normal(jax.random.fold_in(_rk, 11), (16, 16, 128), jnp.float32)
        _ctx_1024c = jax.random.dirichlet(jax.random.fold_in(_rk, 511), 0.3 * jnp.ones((16,), jnp.float32), (16, 64))
        _ctx_1024t = jnp.einsum('bsk,bkd->bsd', _ctx_1024c, _ctx_1024P)
        _ctx_1024t = _ctx_1024t * jax.lax.rsqrt(jnp.mean(jnp.square(_ctx_1024t)) + 1e-12) * 0.953939
        ctx_1024 = -1.39393e-06 + 0.999914 * (_ctx_1024t + 0.3 * jax.random.normal(jax.random.fold_in(_rk, 611), (16, 64, 128), jnp.float32))
        return (x, ctx_1024)
    x, ctx_1024 = _rec_inputs()

    def _L0_attn_setup():
        import jax, jax.numpy as jnp
        import numpy as np
        D_MODEL = 128
        D_STATE = 16
        D_CONV = 4
        D_INNER = 2 * D_MODEL
        DT_MIN, DT_MAX = (0.001, 0.1)
        BATCH, SEQ = (2, 128)
        LN_EPS = 1e-05

        def _silu(v):
            return v * jax.nn.sigmoid(v)
        key = jax.random.key(seed)
        ks = jax.random.split(key, 8)
        x = jax.random.normal(ks[0], (BATCH, SEQ, D_MODEL), jnp.float32)
        in_proj_w = jax.random.normal(ks[1], (2 * D_INNER, D_MODEL), jnp.float32) / np.sqrt(D_MODEL)
        conv_w = jax.random.normal(ks[2], (D_INNER, 1, D_CONV), jnp.float32) / np.sqrt(D_CONV)
        conv_b = jnp.zeros((D_INNER,), jnp.float32)
        x_proj_w = jax.random.normal(ks[3], (2 * D_STATE + 1, D_INNER), jnp.float32) / np.sqrt(D_INNER)
        dt_proj_w = jax.random.normal(ks[4], (D_INNER, 1), jnp.float32) * 0.001
        dt = jnp.exp(jax.random.uniform(ks[5], (D_INNER,), jnp.float32) * (np.log(DT_MAX) - np.log(DT_MIN)) + np.log(DT_MIN))
        dt_proj_b = dt + jnp.log(-jnp.expm1(-dt))
        log_A = jnp.log(jnp.broadcast_to(jnp.arange(1, D_STATE + 1, dtype=jnp.float32), (D_INNER, D_STATE)))
        D_param = jnp.ones((D_INNER,), jnp.float32)
        norm_w = jnp.ones((D_INNER,), jnp.float32)
        norm_b = jnp.zeros((D_INNER,), jnp.float32)
        out_proj_w = jax.random.normal(ks[6], (D_MODEL, D_INNER), jnp.float32) / np.sqrt(D_INNER)
        return dict(x=x, in_proj_w=in_proj_w, conv_w=conv_w, conv_b=conv_b, x_proj_w=x_proj_w, dt_proj_w=dt_proj_w, dt_proj_b=dt_proj_b, log_A=log_A, D_param=D_param, norm_w=norm_w, norm_b=norm_b, out_proj_w=out_proj_w)
    _L0_attn_all = _L0_attn_setup()
    _L0_attn_in = {k: v for k, v in _L0_attn_all.items() if k in ('in_proj_w', 'conv_w', 'conv_b', 'x_proj_w', 'dt_proj_w', 'dt_proj_b', 'log_A', 'D_param', 'norm_w', 'norm_b', 'out_proj_w')}
    del _L0_attn_all

    def _L0_xattn_setup():
        import jax, jax.numpy as jnp
        import numpy as np
        B, S, D = (2, 256, 128)
        H = 16
        CHUNK = 32
        NEG_INF = -1000000000.0
        key = jax.random.key(seed)
        ks = jax.random.split(key, 11)
        std = 1.0 / np.sqrt(D)
        return {'query': jax.random.normal(ks[0], (B, S, D), jnp.float32), 'key': jax.random.normal(ks[1], (B, S, D), jnp.float32), 'value': jax.random.normal(ks[2], (B, S, D), jnp.float32), 'Wq': jax.random.normal(ks[3], (D, D), jnp.float32) * std, 'bq': jax.random.normal(ks[4], (D,), jnp.float32) * 0.01, 'Wk': jax.random.normal(ks[5], (D, D), jnp.float32) * std, 'bk': jax.random.normal(ks[6], (D,), jnp.float32) * 0.01, 'Wv': jax.random.normal(ks[7], (D, D), jnp.float32) * std, 'bv': jax.random.normal(ks[8], (D,), jnp.float32) * 0.01, 'Wo': jax.random.normal(ks[9], (D, D), jnp.float32) * std, 'bo': jax.random.normal(ks[10], (D,), jnp.float32) * 0.01}
    _L0_xattn_all = _L0_xattn_setup()
    _L0_xattn_in = {k: v for k, v in _L0_xattn_all.items() if k in ('Wq', 'bq', 'Wk', 'bk', 'Wv', 'bv', 'Wo', 'bo')}
    del _L0_xattn_all

    def _L0_ffn_setup():
        import jax, jax.numpy as jnp
        import numpy as np
        B, S, H, D, E = (4, 128, 128, 512, 8)
        key = jax.random.key(seed)
        ks = jax.random.split(key, 12)

        def init(k, shape, fan_in):
            return jax.random.normal(k, shape, jnp.float32) / np.float32(np.sqrt(fan_in))
        return {'x': jax.random.normal(ks[0], (B, S, H), jnp.float32), 'Wq': init(ks[1], (H, H), H), 'bq': jnp.zeros((H,), jnp.float32), 'Wk': init(ks[2], (H, H), H), 'bk': jnp.zeros((H,), jnp.float32), 'Wv': init(ks[3], (H, H), H), 'bv': jnp.zeros((H,), jnp.float32), 'Wo': init(ks[4], (H, H), H), 'bo': jnp.zeros((H,), jnp.float32), 'Wg': init(ks[5], (H, E), H), 'bg': jnp.zeros((E,), jnp.float32), 'W1': init(ks[6], (E, H, D), H), 'b1': jnp.zeros((E, D), jnp.float32), 'W2': init(ks[7], (E, D, H), D), 'b2': jnp.zeros((E, H), jnp.float32)}
    _L0_ffn_all = _L0_ffn_setup()
    _L0_ffn_in = {k: v for k, v in _L0_ffn_all.items() if k in ('Wq', 'bq', 'Wk', 'bk', 'Wv', 'bv', 'Wo', 'bo', 'Wg', 'bg', 'W1', 'b1', 'W2', 'b2')}
    del _L0_ffn_all
    return {'x': x, 'ctx_1024': ctx_1024, 'L0_attn_in_proj_w': _L0_attn_in['in_proj_w'], 'L0_attn_conv_w': _L0_attn_in['conv_w'], 'L0_attn_conv_b': _L0_attn_in['conv_b'], 'L0_attn_x_proj_w': _L0_attn_in['x_proj_w'], 'L0_attn_dt_proj_w': _L0_attn_in['dt_proj_w'], 'L0_attn_dt_proj_b': _L0_attn_in['dt_proj_b'], 'L0_attn_log_A': _L0_attn_in['log_A'], 'L0_attn_D_param': _L0_attn_in['D_param'], 'L0_attn_norm_w': _L0_attn_in['norm_w'], 'L0_attn_norm_b': _L0_attn_in['norm_b'], 'L0_attn_out_proj_w': _L0_attn_in['out_proj_w'], 'L0_xattn_Wq': _L0_xattn_in['Wq'], 'L0_xattn_bq': _L0_xattn_in['bq'], 'L0_xattn_Wk': _L0_xattn_in['Wk'], 'L0_xattn_bk': _L0_xattn_in['bk'], 'L0_xattn_Wv': _L0_xattn_in['Wv'], 'L0_xattn_bv': _L0_xattn_in['bv'], 'L0_xattn_Wo': _L0_xattn_in['Wo'], 'L0_xattn_bo': _L0_xattn_in['bo'], 'L0_ffn_Wq': _L0_ffn_in['Wq'], 'L0_ffn_bq': _L0_ffn_in['bq'], 'L0_ffn_Wk': _L0_ffn_in['Wk'], 'L0_ffn_bk': _L0_ffn_in['bk'], 'L0_ffn_Wv': _L0_ffn_in['Wv'], 'L0_ffn_bv': _L0_ffn_in['bv'], 'L0_ffn_Wo': _L0_ffn_in['Wo'], 'L0_ffn_bo': _L0_ffn_in['bo'], 'L0_ffn_Wg': _L0_ffn_in['Wg'], 'L0_ffn_bg': _L0_ffn_in['bg'], 'L0_ffn_W1': _L0_ffn_in['W1'], 'L0_ffn_b1': _L0_ffn_in['b1'], 'L0_ffn_W2': _L0_ffn_in['W2'], 'L0_ffn_b2': _L0_ffn_in['b2']}

def reference(x, ctx_1024, L0_attn_in_proj_w, L0_attn_conv_w, L0_attn_conv_b, L0_attn_x_proj_w, L0_attn_dt_proj_w, L0_attn_dt_proj_b, L0_attn_log_A, L0_attn_D_param, L0_attn_norm_w, L0_attn_norm_b, L0_attn_out_proj_w, L0_xattn_Wq, L0_xattn_bq, L0_xattn_Wk, L0_xattn_bk, L0_xattn_Wv, L0_xattn_bv, L0_xattn_Wo, L0_xattn_bo, L0_ffn_Wq, L0_ffn_bq, L0_ffn_Wk, L0_ffn_bk, L0_ffn_Wv, L0_ffn_bv, L0_ffn_Wo, L0_ffn_bo, L0_ffn_Wg, L0_ffn_bg, L0_ffn_W1, L0_ffn_b1, L0_ffn_W2, L0_ffn_b2):
    import jax
    import jax.numpy as jnp

    def _L0_attn_ref(x, in_proj_w, conv_w, conv_b, x_proj_w, dt_proj_w, dt_proj_b, log_A, D_param, norm_w, norm_b, out_proj_w):
        import jax, jax.numpy as jnp
        import numpy as np
        D_MODEL = 128
        D_STATE = 16
        D_CONV = 4
        D_INNER = 2 * D_MODEL
        DT_MIN, DT_MAX = (0.001, 0.1)
        BATCH, SEQ = (2, 128)
        LN_EPS = 1e-05

        def _silu(v):
            return v * jax.nn.sigmoid(v)
        xz = x @ in_proj_w.T
        xp, z = jnp.split(xz, 2, axis=-1)
        xc = jnp.transpose(xp, (0, 2, 1))
        xc = jax.lax.conv_general_dilated(xc, conv_w, window_strides=(1,), padding=[(D_CONV - 1, 0)], feature_group_count=D_INNER, dimension_numbers=('NCH', 'OIH', 'NCH'))
        xc = xc + conv_b[None, :, None]
        xc = _silu(jnp.transpose(xc, (0, 2, 1)))
        ssm = xc @ x_proj_w.T
        Bp = ssm[..., :D_STATE]
        Cp = ssm[..., D_STATE:2 * D_STATE]
        delta_raw = ssm[..., 2 * D_STATE:]
        delta = jax.nn.softplus(delta_raw @ dt_proj_w.T + dt_proj_b)
        delta = jnp.clip(delta, DT_MIN, DT_MAX)
        A = -jnp.exp(log_A)
        u = xc

        def step(state, inp):
            u_t, d_t, B_t, C_t = inp
            dA = jnp.exp(d_t[:, :, None] * A[None])
            dB = d_t[:, :, None] * B_t[:, None, :]
            state = dA * state + dB * u_t[:, :, None]
            y_t = jnp.einsum('bn,bdn->bd', C_t, state)
            return (state, y_t)
        x0 = jnp.zeros((x.shape[0], D_INNER, D_STATE), u.dtype)
        seq_inputs = (jnp.swapaxes(u, 0, 1), jnp.swapaxes(delta, 0, 1), jnp.swapaxes(Bp, 0, 1), jnp.swapaxes(Cp, 0, 1))
        _, ys = jax.lax.scan(step, x0, seq_inputs)
        y = jnp.swapaxes(ys, 0, 1)
        y = y + u * D_param
        mu = jnp.mean(y, axis=-1, keepdims=True)
        var = jnp.var(y, axis=-1, keepdims=True)
        y = (y - mu) * jax.lax.rsqrt(var + LN_EPS) * norm_w + norm_b
        y = y * _silu(z)
        return y @ out_proj_w.T

    def _L0_xattn_ref(query, key, value, Wq, bq, Wk, bk, Wv, bv, Wo, bo):
        import jax, jax.numpy as jnp
        import numpy as np
        B, S, D = (2, 256, 128)
        H = 16
        CHUNK = 32
        NEG_INF = -1000000000.0
        b, s, d = query.shape
        hd = d // H
        scale = 1.0 / jnp.sqrt(jnp.asarray(hd, query.dtype))
        q = (query @ Wq + bq).reshape(b, s, H, hd)
        k = (key @ Wk + bk).reshape(b, s, H, hd)
        v = (value @ Wv + bv).reshape(b, s, H, hd)
        scores = jnp.einsum('bqhd,bkhd->bhqk', q, k) * scale
        pos = jnp.arange(s)
        block_end = (pos // CHUNK + 1) * CHUNK
        mask = pos[None, :] < block_end[:, None]
        scores = jnp.where(mask[None, None], scores, NEG_INF)
        attn = jax.nn.softmax(scores, axis=-1)
        out = jnp.einsum('bhqk,bkhd->bqhd', attn, v).reshape(b, s, d)
        return out @ Wo + bo

    def _L0_ffn_ref(x, Wq, bq, Wk, bk, Wv, bv, Wo, bo, Wg, bg, W1, b1, W2, b2):
        import jax, jax.numpy as jnp
        import numpy as np
        B, S, H, D, E = (4, 128, 128, 512, 8)
        q = x @ Wq + bq
        k = x @ Wk + bk
        v = x @ Wv + bv
        scale = jnp.asarray(1.0 / np.sqrt(H), x.dtype)
        scores = jnp.einsum('bqh,bkh->bqk', q, k) * scale
        attn = jax.nn.softmax(scores, axis=-1)
        a = jnp.einsum('bqk,bkh->bqh', attn, v) @ Wo + bo
        x = x + a
        gates = jax.nn.softmax(x @ Wg + bg, axis=-1)
        hmid = jax.nn.relu(jnp.einsum('bsh,ehd->bsed', x, W1) + b1)
        eout = jnp.einsum('bsed,edh->bseh', hmid, W2) + b2
        y = jnp.einsum('bse,bseh->bsh', gates, eout)
        return x + y
    x = x + _L0_attn_ref(_layernorm(x, axis=-1), L0_attn_in_proj_w, L0_attn_conv_w, L0_attn_conv_b, L0_attn_x_proj_w, L0_attn_dt_proj_w, L0_attn_dt_proj_b, L0_attn_log_A, L0_attn_D_param, L0_attn_norm_w, L0_attn_norm_b, L0_attn_out_proj_w)
    x = x + _L0_xattn_ref(_layernorm(x, axis=-1), ctx_1024, ctx_1024, L0_xattn_Wq, L0_xattn_bq, L0_xattn_Wk, L0_xattn_bk, L0_xattn_Wv, L0_xattn_bv, L0_xattn_Wo, L0_xattn_bo)
    x = x + _L0_ffn_ref(_layernorm(x, axis=-1), L0_ffn_Wq, L0_ffn_bq, L0_ffn_Wk, L0_ffn_bk, L0_ffn_Wv, L0_ffn_bv, L0_ffn_Wo, L0_ffn_bo, L0_ffn_Wg, L0_ffn_bg, L0_ffn_W1, L0_ffn_b1, L0_ffn_W2, L0_ffn_b2)
    return x

_drawn_inputs = setup_inputs


def setup_inputs(seed=0):
    import zlib

    import numpy as np

    out = dict(_drawn_inputs(seed))
    spreads = {'L0_attn_conv_b': (0.0, 0.1),
     'L0_attn_D_param': (1.0, 0.2),
     'L0_attn_norm_w': (1.0, 0.2),
     'L0_attn_norm_b': (0.0, 0.1),
     'L0_ffn_bq': (0.0, 0.8),
     'L0_ffn_bk': (0.0, 2.0),
     'L0_ffn_bv': (0.0, 0.1),
     'L0_ffn_bo': (0.0, 0.1),
     'L0_ffn_bg': (0.0, 0.8),
     'L0_ffn_b1': (0.0, 0.521),
     'L0_ffn_b2': (0.0, 0.377)}
    factors = {'L0_attn_dt_proj_w': 64.0,
     'L0_xattn_bq': 27.06,
     'L0_xattn_bk': 64.0,
     'L0_xattn_bv': 5.804,
     'L0_xattn_bo': 6.247}
    for name, (base, spread) in spreads.items():
        noise = np.random.default_rng([zlib.crc32(name.encode()), seed]).standard_normal(out[name].shape)
        drawn = base * np.exp(spread * noise) if base else spread * noise
        out[name] = jnp.asarray(drawn.astype(out[name].dtype))
    for name, factor in factors.items():
        out[name] = (out[name] * factor).astype(out[name].dtype)
    return out
```

```python
from contextlib import ExitStack

import concourse.bass as bass
from concourse import mybir

F32 = mybir.dt.float32
BF16 = mybir.dt.bfloat16
ALU = mybir.AluOpType
ACT = mybir.ActivationFunctionType
AX_X = mybir.AxisListType.X

P = 128


def columns():
    at, out = 0, {}
    for name, n in (("conv_b", 2), ("dt_b", 2), ("D", 2), ("norm_w", 2), ("norm_b", 2), ("log_A", 32),
                    ("x_bq", 1), ("x_bk", 1), ("f_bq", 1), ("f_bk", 1), ("f_bv", 1), ("b1", 32)):
        out[name] = (at, n)
        at += n
    return out, at


def rows():
    at, out = 0, {}
    for name, n in (("conv_w", 1024), ("x_bv", 128), ("x_bo", 128), ("f_bo", 128), ("bg", 8)):
        out[name] = (at, n)
        at += n
    return out, at


def decoder_layer(nc, x, ctx_t, cols, row, dt_row, w_mamba, w_cross, w_self, W1, W2, b2, out):
    B, S, D = x.shape
    TOK = B * S
    NG = 4
    GB = B // NG
    T = TOK // NG
    NT = T // P
    DI = 256
    NH = DI // P
    N = 16
    TAPS = 4
    PAD = TAPS - 1
    SP = S + PAD
    STEPS = N // 2
    H = 16
    HD = D // H
    CHUNK = 32
    HP = H // 2
    VW = 2 * (HD + 1)
    E = 8
    FT = W1.shape[2] // P
    EPS = 1e-5
    MASKED = -1e30
    X_SCALE = float(HD) ** -0.5
    F_SCALE = float(D) ** -0.5
    COL, NCOL = columns()
    ROW, NROW = rows()

    with ExitStack() as ctx:
        def sb(name, shape, dt=F32):
            return ctx.enter_context(nc.sbuf_tensor(name, shape, dt))

        def pb(name, shape, dt=F32):
            return ctx.enter_context(nc.psum_tensor(name, shape, dt))

        def sem(name):
            return ctx.enter_context(nc.semaphore(name))

        X = sb("X", [P, NG * NT, D])
        CT = sb("CT", [P, TOK])
        cv = sb("cv", [P, NCOL])
        rw = sb("rw", [P, NROW])
        dtw = sb("dtw", [33, DI])
        wm = sb("wm", [P, 512 + 66 + 256])
        wc = sb("wc", [P, 4 * 128])
        ws = sb("ws", [P, 4 * 128 + E])
        w1 = sb("w1", [P, E, FT * P])
        w2 = sb("w2", [P, E * FT, D])
        b2s = sb("b2s", [E, D])
        ident = sb("ident", [P, P])
        mean_w = sb("mean_w", [P, P])
        eps = sb("eps", [P, 1])
        one = sb("one", [P, 1])
        pick = sb("pick", [96, 2 * N, P], BF16)
        head = sb("head", [P, H])
        early_q = sb("early_q", [1, P], BF16)
        late_k = sb("late_k", [1, 512], BF16)
        negA = sb("negA", [P, 2 * N])
        expA = sb("expA", [P, 2 * N])
        ncb = sb("ncb", [P, NH])
        wconv = sb("wconv", [P, TAPS, DI])
        st = sb("st", [P, NG, NT, 6])
        mv = sb("mv", [P, NG, NT, 2])
        lv = sb("lv", [P, NG, NT])
        rs = sb("rs", [P, NG, NT])
        xn = sb("xn", [P, NT, D])
        xp = sb("xp", [P, NG, GB, SP])
        eu = sb("eu", [P, NH, T])
        u = sb("u", [P, 2, NH, T])
        ssm = sb("ssm", [33, 2, T])
        rem = sb("rem", [64, T])
        bc = sb("bc", [96, 2, T], BF16)
        de = sb("de", [P, NH, T])
        dlt = sb("dlt", [P, 2, NH, T])
        du = sb("du", [P, 2, NH, T])
        ez = sb("ez", [P, NH, T])
        sz = sb("sz", [P, 2, NH, T])
        yacc = sb("yacc", [P, 2, NH, T])
        dA = sb("dA", [P, 2, NH, 2, GB, S])
        dBu = sb("dBu", [P, 2, NH, 2, T])
        hs = sb("hs", [P, 2, NH, 2, T])
        pair = sb("pair", [P, NH, T])
        yc = sb("yc", [P, NH, T])
        sq = sb("sq", [P, NH, T])
        lnv = sb("lnv", [P, T])
        rsv = sb("rsv", [P, T])
        yn = sb("yn", [P, NH, T])
        gy = sb("gy", [P, NH, T])
        x1 = sb("x1", [P, 2, NT, D])
        kt = sb("kt", [P, T])
        kx = sb("kx", [P, GB, H, S])
        vx = sb("vx", [P, 2, GB, HP, VW])
        st2 = sb("st2", [P, NG, NT, 6])
        mv2 = sb("mv2", [P, NG, NT, 2])
        lv2 = sb("lv2", [P, NG, NT])
        rs2 = sb("rs2", [P, NG, NT])
        xn2 = sb("xn2", [P, NT, D])
        x2t = sb("x2t", [P, T])
        qt = sb("qt", [P, T])
        x1b = sb("x1b", [P, NT, D])
        mx = sb("mx", [P, H])
        sd = sb("sd", [P, H, S])
        pt = sb("pt", [P, HP, P])
        rc = sb("rc", [P, H])
        ov = sb("ov", [P, H, HD])
        ot = sb("ot", [P, T])
        x2 = sb("x2", [P, 2, NT, D])
        st3 = sb("st3", [P, NG, NT, 6])
        mv3 = sb("mv3", [P, NG, NT, 2])
        lv3 = sb("lv3", [P, NG, NT])
        rs3 = sb("rs3", [P, NG, NT])
        xn3 = sb("xn3", [P, NT, D])
        x3b = sb("x3b", [P, NT, D])
        x3t = sb("x3t", [P, T])
        fq = sb("fq", [P, T])
        fk = sb("fk", [P, T])
        fv = sb("fv", [S, GB, D])
        fm = sb("fm", [P, NT])
        fnb = sb("fnb", [P, NT])
        fp = sb("fp", [P, NT, S])
        fs = sb("fs", [P, NT])
        fr = sb("fr", [P, NT])
        fpn = sb("fpn", [P, NT, S])
        fpt = sb("fpt", [S, T])
        fat = sb("fat", [P, T])
        x4 = sb("x4", [P, NT, D])
        x4t = sb("x4t", [P, 2, T])
        gl = sb("gl", [P, NT, E])
        gm = sb("gm", [P, NT])
        gd = sb("gd", [P, NT, E])
        ge = sb("ge", [P, NT, E])
        gs = sb("gs", [P, NT])
        gr = sb("gr", [P, NT])
        gate = sb("gate", [P, 2, NT, E])
        gt = sb("gt", [E, T])
        x24 = sb("x24", [P, NT, D])
        hid = sb("hid", [P, 4, T])
        acc = sb("acc", [P, NG, NT, D])

        pF = pb("pF", [P, 512])
        pB = pb("pB", [P, 2, T])
        pC = pb("pC", [P, 2, T])
        pX = pb("pX", [P, 512])
        pH = pb("pH", [P, 2, 512])
        pE = pb("pE", [P, 2, 512])

        x_in = [sem(f"x_in{g}") for g in range(NG)]
        ctx_in, vec_in, row_in, wm_in, wc_in, ws_in = (sem(n) for n in ("ctx_in", "vec_in", "row_in", "wm_in", "wc_in", "ws_in"))
        w1_in, w2_in, b2_in, out_done = (sem(n) for n in ("w1_in", "w2_in", "b2_in", "out_done"))
        dve_const, pool_const, pool_step, expA_ready, consts_ready = (sem(n) for n in (
            "dve_const", "pool_const", "pool_step", "expA_ready", "consts_ready"))
        (stats, mean_var, ln_var, rstd, normed, normed_t, padded, inner, exp_u, den_u, sig_u, u_ready, ssm_ps, ssm_ready,
         split, dt_ps, exp_dt, dt_min, ln_dt, delta, du_ready, z_ps, exp_z, den_z, sig_z, sz_ready) = (sem(n) for n in (
            "stats", "mean_var", "ln_var", "rstd", "normed", "normed_t", "padded", "inner", "exp_u", "den_u", "sig_u",
            "u_ready", "ssm_ps", "ssm_ready", "split", "dt_ps", "exp_dt", "dt_min", "ln_dt", "delta", "du_ready", "z_ps",
            "exp_z", "den_z", "sig_z", "sz_ready"))
        split_step = sem("split_step")
        b_ps, c_ps, decay, dbu_ready, state, weighted, paired, summed, skip = (sem(n) for n in (
            "b_ps", "c_ps", "decay", "dbu_ready", "state", "weighted", "paired", "summed", "skip"))
        mean_ps, centred, squared, var_ps, ln_y, rstd_y, scaled, gated, back_ps, x1_ready = (sem(n) for n in (
            "mean_ps", "centred", "squared", "var_ps", "ln_y", "rstd_y", "scaled", "gated", "back_ps", "x1_ready"))
        (k_ps, k_ready, kx_ready, v_ps, vx_ready, stats2, mean_var2, ln_var2, rstd2, normed2, normed2_t, x2t_ready, q_ps,
         q_ready, scores, maxed, shifted, probs, probs_t, pt_ready, pv_ps, recip, ov_ready, ov_t, ot_ready, cross_ps,
         x1b_ready, x2_ready) = (sem(n) for n in (
            "k_ps", "k_ready", "kx_ready", "v_ps", "vx_ready", "stats2", "mean_var2", "ln_var2", "rstd2", "normed2",
            "normed2_t", "x2t_ready", "q_ps", "q_ready", "scores", "maxed", "shifted", "probs", "probs_t", "pt_ready",
            "pv_ps", "recip", "ov_ready", "ov_t", "ot_ready", "cross_ps", "x1b_ready", "x2_ready"))
        (stats3, mean_var3, ln_var3, rstd3, normed3, x3b_ready, normed3_t, x3t_ready, fqk_ps, fqk_ready, fv_ps, fv_ready,
         fscores, fmaxed, fneg, fprobs, frecip, fpn_ready, fp_t, fpt_ready, fat_ps, fat_ready, self_ps, x4_ready, x4_t,
         x4t_ready) = (sem(n) for n in (
            "stats3", "mean_var3", "ln_var3", "rstd3", "normed3", "x3b_ready", "normed3_t", "x3t_ready", "fqk_ps",
            "fqk_ready", "fv_ps", "fv_ready", "fscores", "fmaxed", "fneg", "fprobs", "frecip", "fpn_ready", "fp_t",
            "fpt_ready", "fat_ps", "fat_ready", "self_ps", "x4_ready", "x4_t", "x4t_ready"))
        (gate_ps, logits, gmaxed, gshifted, gexp, gsummed, grecip, gate_ready, gate_t, gt_ready, bias_ps, x24_ready,
         acc_first, hid_ps, hid_ready, exp_ps, expert) = (sem(n) for n in (
            "gate_ps", "logits", "gmaxed", "gshifted", "gexp", "gsummed", "grecip", "gate_ready", "gate_t", "gt_ready",
            "bias_ps", "x24_ready", "acc_first", "hid_ps", "hid_ready", "exp_ps", "expert"))

        block = ctx.enter_context(nc.Block())

        def col(name, i=0, n=1):
            return cv[:, COL[name][0] + i:COL[name][0] + i + n]

        def bcast(name):
            return rw[:, ROW[name][0]:ROW[name][0] + ROW[name][1]]

        w_in_t = wm[:, 0:512]
        w_x = wm[:, 512:512 + 66].rearrange("p (h m) -> p h m", h=NH)
        w_out = wm[:, 578:578 + 256].rearrange("p (h m) -> p h m", h=NH)
        xwq, xwk, xwv, xwo = (wc[:, i * 128:(i + 1) * 128] for i in range(4))
        fwq, fwk, fwv, fwo = (ws[:, i * 128:(i + 1) * 128] for i in range(4))
        wg = ws[:, 512:512 + E]
        x_tiles = x.rearrange("b s d -> (b s) d").rearrange("(n p) d -> p n d", p=P)
        out_tiles = out.rearrange("b s d -> (b s) d").rearrange("(n p) d -> p n d", p=P)

        def halves(ap):
            return ap.rearrange("p (h t) -> p h t", h=NH)

        @block.sync
        def _(sp):
            sp.dma_start(X[:, 0:NT, :], x_tiles[:, 0:NT, :]).then_inc(x_in[0], 16)
            sp.dma_start(cv[:, :], cols).then_inc(vec_in, 16)
            sp.dma_start(wm[:, :], w_mamba).then_inc(wm_in, 16)
            sp.dma_start(rw[:, :], row.to_broadcast([P, NROW])).then_inc(row_in, 16)
            sp.dma_start(dtw[32:33, :], dt_row).then_inc(row_in, 16)
            sp.dma_start(CT[:, :], ctx_t).then_inc(ctx_in, 16)
            sp.dma_start(wc[:, :], w_cross).then_inc(wc_in, 16)
            for g in range(1, NG):
                sp.dma_start(X[:, g * NT:(g + 1) * NT, :], x_tiles[:, g * NT:(g + 1) * NT, :]).then_inc(x_in[g], 16)
            sp.dma_start(ws[:, :], w_self).then_inc(ws_in, 16)
            sp.dma_start(b2s[:, :], b2).then_inc(b2_in, 16)
            sp.dma_start(w1[:, :, :], W1.rearrange("e h f -> h e f")).then_inc(w1_in, 16)
            sp.dma_start(w2[:, :, :], W2.rearrange("e (t p) h -> p (e t) h", p=P)).then_inc(w2_in, 16)
            for g in range(NG):
                sp.wait_ge(expert, E * (g + 1))
                sp.dma_start(out_tiles[:, g * NT:(g + 1) * NT, :], acc[:, g, :, :]).then_inc(out_done, 16)
            sp.wait_ge(out_done, 16 * NG)

        @block.gpsimd
        def _(pool):
            done = [0]

            def step(ins):
                done[0] += 1
                ins.then_inc(pool_step, 1)
                pool.wait_ge(pool_step, done[0])

            step(nc.gpsimd.memset(ident[:, :], 0.0))
            nc.gpsimd.affine_select(out=ident[:, :], in_=ident[:, :], compare_op=ALU.not_equal, fill=1.0, base=0,
                                    pattern=[[-1, P]], channel_multiplier=1).then_inc(pool_const, 1)
            step(nc.gpsimd.memset(head[:, :], 1.0))
            step(nc.gpsimd.affine_select(out=head[:, :], in_=head[:, :], compare_op=ALU.is_ge, fill=0.0, base=0,
                                         pattern=[[-HD, H]], channel_multiplier=1))
            step(nc.gpsimd.affine_select(out=head[:, :], in_=head[:, :], compare_op=ALU.is_ge, fill=0.0, base=HD - 1,
                                         pattern=[[HD, H]], channel_multiplier=-1))
            step(nc.gpsimd.memset(pick[:, :, :], 0.0))
            for j in range(3):
                last = nc.gpsimd.affine_select(out=pick[:, :, :], in_=pick[:, :, :], compare_op=ALU.not_equal, fill=1.0,
                                               base=-2 * N * j, pattern=[[-1, 2 * N], [0, P]], channel_multiplier=1)
                if j < 2:
                    step(last)
            last.then_inc(pool_const, 1)

            def keys(g):
                pool.wait_ge(k_ready, g + 1)
                if g:
                    pool.wait_ge(scores, NT * g)
                for b in range(GB):
                    last = nc.gpsimd.tensor_tensor(
                        kx[:, b, :, :],
                        kt[:, b * S:(b + 1) * S].unsqueeze(1).to_broadcast([P, H, S]),
                        head[:, :].unsqueeze(2).to_broadcast([P, H, S]), ALU.mult)
                last.then_inc(kx_ready, 1)

            def scan(g):
                for p in range(STEPS):
                    i = STEPS * g + p
                    if p == 0:
                        pool.wait_ge(skip, g + 1)
                    if i:
                        pool.wait_ge(summed, i)
                    pool.wait_ge(weighted, i + 1)
                    nc.gpsimd.tensor_tensor(pair[:, :, :], hs[:, i % 2, :, 0, :], hs[:, i % 2, :, 1, :],
                                            ALU.add).then_inc(paired, 1)
                    pool.wait_ge(paired, i + 1)
                    nc.gpsimd.tensor_tensor(yacc[:, g % 2, :, :], yacc[:, g % 2, :, :], pair[:, :, :],
                                            ALU.add).then_inc(summed, 1)

            for g in range(NG):
                keys(g)
                scan(g)

        @block.scalar
        def _(act):
            act.wait_ge(vec_in, 16)
            nc.scalar.activation(expA[:, :], col("log_A", 0, 2 * N), ACT.Exp).then_inc(expA_ready, 1)
            act.wait_ge(dve_const, 1)

            def rsqrt(g, mv_, lv_, rs_, ready, ln_done, done):
                act.wait_ge(ready, g + 1)
                nc.scalar.activation(lv_[:, g, :], mv_[:, g, :, 1], ACT.Ln, bias=eps[:, :]).then_inc(ln_done, 1)
                act.wait_ge(ln_done, g + 1)
                nc.scalar.activation(rs_[:, g, :], lv_[:, g, :], ACT.Exp, scale=-0.5).then_inc(done, 1)

            def keys(g):
                act.wait_ge(k_ps, g + 1)
                if g:
                    act.wait_ge(kx_ready, g)
                nc.scalar.activation(kt[:, :], pX[:, 0:T], ACT.Identity, bias=col("x_bk")).then_inc(k_ready, 1)

            def front(g):
                rsqrt(g, mv, lv, rs, mean_var, ln_var, rstd)
                act.wait_ge(normed_t, g + 1)
                nc.scalar.activation(xp[:, g, :, PAD:SP], pF[:, 0:T].rearrange("p (b s) -> p b s", b=GB),
                                     ACT.Copy).then_inc(padded, 1)
                act.wait_ge(inner, g + 1)
                if g:
                    act.wait_ge(u_ready, g)
                for h in range(NH):
                    last = nc.scalar.activation(eu[:, h, :], halves(pF[:, :])[:, h, :], ACT.Exp, scale=-1.0,
                                                bias=ncb[:, h:h + 1])
                last.then_inc(exp_u, 1)
                act.wait_ge(ssm_ps, g + 1)
                nc.scalar.activation(ssm[:, g % 2, :], pF[0:33, 0:T], ACT.Copy).then_inc(ssm_ready, 1)
                act.wait_ge(dt_ps, g + 1)
                for h in range(NH):
                    last = nc.scalar.activation(de[:, h, :], halves(pF[:, :])[:, h, :], ACT.Exp,
                                                bias=col("dt_b", h))
                last.then_inc(exp_dt, 1)
                act.wait_ge(dt_min, g + 1)
                nc.scalar.activation(de[:, :, :], de[:, :, :], ACT.Ln, bias=one[:, :]).then_inc(ln_dt, 1)
                act.wait_ge(z_ps, g + 1)
                nc.scalar.activation(ez[:, :, :], halves(pF[:, :]), ACT.Exp, scale=-1.0).then_inc(exp_z, 1)

            def scan(g, p):
                i = STEPS * g + p
                if p == 0:
                    act.wait_ge(delta, g + 1)
                if i >= 2:
                    act.wait_ge(state, i - 1)
                for h in range(NH):
                    for k in range(2):
                        a = h * N + 2 * p + k
                        last = nc.scalar.activation(
                            dA[:, i % 2, h, k, :, 1:S],
                            dlt[:, g % 2, h, :].rearrange("p (b s) -> p b s", b=GB)[:, :, 1:S],
                            ACT.Exp, scale=negA[:, a:a + 1])
                last.then_inc(decay, 1)

            def back(g):
                act.wait_ge(centred, g + 1)
                nc.scalar.activation(sq[:, :, :], yc[:, :, :], ACT.Square).then_inc(squared, 1)
                act.wait_ge(var_ps, g + 1)
                nc.scalar.activation(lnv[:, :], pX[:, 0:T], ACT.Ln, bias=eps[:, :]).then_inc(ln_y, 1)
                act.wait_ge(ln_y, g + 1)
                nc.scalar.activation(rsv[:, :], lnv[:, :], ACT.Exp, scale=-0.5).then_inc(rstd_y, 1)

            def cross(g):
                rsqrt(g, mv2, lv2, rs2, mean_var2, ln_var2, rstd2)
                act.wait_ge(normed2_t, g + 1)
                nc.scalar.activation(x2t[:, :], pX[:, 0:T], ACT.Copy).then_inc(x2t_ready, 1)
                act.wait_ge(q_ps, g + 1)
                nc.scalar.activation(qt[:, :], pX[:, 0:T], ACT.Identity, bias=col("x_bq")).then_inc(q_ready, 1)
                for t in range(NT):
                    j = NT * g + t
                    act.wait_ge(shifted, j + 1)
                    nc.scalar.activation(sd[:, :, :], sd[:, :, :], ACT.Exp, scale=X_SCALE).then_inc(probs, 1)
                    act.wait_ge(probs_t, j + 1)
                    nc.scalar.activation(pt[:, :, :], pE[:, :, :].rearrange("p a (h t) -> p (a h) t", t=P),
                                         ACT.Copy).then_inc(pt_ready, 1)
                    act.wait_ge(ov_t, j + 1)
                    nc.scalar.activation(ot[:, t * P:(t + 1) * P], pX[:, 0:P], ACT.Copy).then_inc(ot_ready, 1)

            def attend(g):
                rsqrt(g, mv3, lv3, rs3, mean_var3, ln_var3, rstd3)
                act.wait_ge(normed3_t, g + 1)
                nc.scalar.activation(x3t[:, :], pX[:, 0:T], ACT.Copy).then_inc(x3t_ready, 1)
                act.wait_ge(fqk_ps, g + 1)
                nc.scalar.activation(fq[:, :], pX[:, 0:T], ACT.Identity, bias=col("f_bq"))
                nc.scalar.activation(fk[:, :], pX[:, T:2 * T], ACT.Identity, bias=col("f_bk")).then_inc(fqk_ready, 1)
                act.wait_ge(fneg, g + 1)
                for t in range(NT):
                    last = nc.scalar.activation(fp[:, t, :], pH[:, 0, t * S:(t + 1) * S], ACT.Exp, scale=F_SCALE,
                                                bias=fnb[:, t:t + 1], accum_out=fs[:, t:t + 1])
                last.then_inc(fprobs, 1)
                act.wait_ge(fp_t, g + 1)
                nc.scalar.activation(fpt[:, :], pH[0:S, 0, 0:T], ACT.Copy).then_inc(fpt_ready, 1)
                act.wait_ge(fat_ps, g + 1)
                nc.scalar.activation(fat[:, :], pX[:, 0:T], ACT.Identity, bias=col("f_bv")).then_inc(fat_ready, 1)
                act.wait_ge(x4_t, g + 1)
                nc.scalar.activation(x4t[:, g % 2, :], pX[:, 0:T], ACT.Copy).then_inc(x4t_ready, 1)
                act.wait_ge(gshifted, g + 1)
                nc.scalar.activation(ge[:, :, :], gd[:, :, :], ACT.Exp).then_inc(gexp, 1)
                act.wait_ge(gate_t, g + 1)
                nc.scalar.activation(gt[:, :], pX[0:E, 0:T], ACT.Copy).then_inc(gt_ready, 1)

            def experts(g):
                for f in range(E * FT):
                    i = E * FT * g + f
                    act.wait_ge(hid_ps, i + 1)
                    if i >= 4:
                        act.wait_ge(exp_ps, i - 3)
                    nc.scalar.activation(hid[:, i % 4, :], pH[:, i % 2, 0:T], ACT.Relu,
                                         bias=col("b1", f)).then_inc(hid_ready, 1)

            for g in range(NG):
                keys(g)
                front(g)
                for p in range(STEPS):
                    scan(g, p)
                back(g)
                cross(g)
                attend(g)
                experts(g)

        @block.tensor
        def _(pe):
            def keys(g):
                if g == 0:
                    pe.wait_ge(ctx_in, 16)
                    pe.wait_ge(wc_in, 16)
                else:
                    pe.wait_ge(acc_first, g)
                nc.tensor.matmul(pX[:, 0:T], xwk, CT[:, g * T:(g + 1) * T], start=True, stop=True).then_inc(k_ps, 1)
                if g:
                    pe.wait_ge(expert, E * g)
                for b in range(GB):
                    for k in range(2):
                        last = nc.tensor.matmul(pE[k * S:(k + 1) * S, 0, b * D:(b + 1) * D],
                                                CT[:, g * T + b * S:g * T + (b + 1) * S], xwv, start=True, stop=True)
                last.then_inc(v_ps, 1)

            def front(g):
                if g == 0:
                    pe.wait_ge(pool_const, 1)
                else:
                    pe.wait_ge(exp_z, g)
                    pe.wait_ge(sz_ready, g)
                pe.wait_ge(normed, g + 1)
                for t in range(NT):
                    last = nc.tensor.transpose(pF[:, t * P:(t + 1) * P], xn[:, t, :], ident[:, :])
                last.then_inc(normed_t, 1)
                if g == 0:
                    pe.wait_ge(dve_const, 2)
                pe.wait_ge(padded, g + 1)
                for h in range(NH):
                    for k in range(TAPS):
                        last = nc.tensor.matmul(halves(pF[:, :])[:, h, :], wconv[:, k, h * P:(h + 1) * P],
                                                xp[:, g, :, k:k + S], start=(k == 0), stop=(k == TAPS - 1))
                last.then_inc(inner, 1)
                pe.wait_ge(exp_u, g + 1)
                pe.wait_ge(u_ready, g + 1)
                for h in range(NH):
                    last = nc.tensor.matmul(pF[0:33, 0:T], w_x[:, h, :], u[:, g % 2, h, :],
                                            start=(h == 0), stop=(h == NH - 1))
                last.then_inc(ssm_ps, 1)
                if g == 0:
                    pe.wait_ge(row_in, 32)
                pe.wait_ge(ssm_ready, g + 1)
                for h in range(NH):
                    last = nc.tensor.matmul(halves(pF[:, :])[:, h, :], dtw[32:33, h * P:(h + 1) * P],
                                            ssm[32:33, g % 2, :], start=True, stop=True)
                last.then_inc(dt_ps, 1)
                pe.wait_ge(exp_dt, g + 1)
                for h in range(NH):
                    last = nc.tensor.matmul(halves(pF[:, :])[:, h, :], w_in_t[:, DI + h * P:DI + (h + 1) * P],
                                            xp[:, g, :, PAD:SP], start=True, stop=True)
                last.then_inc(z_ps, 1)

            def scan(g, p):
                i = STEPS * g + p
                if p == 0:
                    pe.wait_ge(split, g + 1)
                if i == 0:
                    pe.wait_ge(pool_const, 2)
                if i:
                    pe.wait_ge(dbu_ready, i)
                for k in range(2):
                    last = nc.tensor.matmul(pB[:, k, :], pick[:, 2 * p + k, :], bc[:, g % 2, :], start=True, stop=True)
                last.then_inc(b_ps, 1)
                if i:
                    pe.wait_ge(weighted, i)
                for k in range(2):
                    last = nc.tensor.matmul(pC[:, k, :], pick[:, N + 2 * p + k, :], bc[:, g % 2, :], start=True,
                                            stop=True)
                last.then_inc(c_ps, 1)

            def back(g):
                pe.wait_ge(summed, STEPS * (g + 1))
                pe.wait_ge(k_ready, g + 1)
                for h in range(NH):
                    last = nc.tensor.matmul(pX[:, 0:T], mean_w[:, :], yacc[:, g % 2, h, :],
                                            start=(h == 0), stop=(h == NH - 1))
                last.then_inc(mean_ps, 1)
                pe.wait_ge(centred, g + 1)
                pe.wait_ge(squared, g + 1)
                for h in range(NH):
                    last = nc.tensor.matmul(pX[:, 0:T], mean_w[:, :], sq[:, h, :],
                                            start=(h == 0), stop=(h == NH - 1))
                last.then_inc(var_ps, 1)
                pe.wait_ge(ln_y, g + 1)
                pe.wait_ge(gated, g + 1)
                for t in range(NT):
                    for h in range(NH):
                        last = nc.tensor.matmul(pX[:, t * D:(t + 1) * D], gy[:, h, t * P:(t + 1) * P], w_out[:, h, :],
                                                start=(h == 0), stop=(h == NH - 1))
                last.then_inc(back_ps, 1)

            def cross(g):
                pe.wait_ge(x1_ready, g + 1)
                pe.wait_ge(normed2, g + 1)
                for t in range(NT):
                    last = nc.tensor.transpose(pX[:, t * P:(t + 1) * P], xn2[:, t, :], ident[:, :])
                last.then_inc(normed2_t, 1)
                pe.wait_ge(x2t_ready, g + 1)
                nc.tensor.matmul(pX[:, 0:T], xwq, x2t[:, :], start=True, stop=True).then_inc(q_ps, 1)
                pe.wait_ge(q_ready, g + 1)
                pe.wait_ge(kx_ready, g + 1)
                for t in range(NT):
                    j = NT * g + t
                    if t == 0 and g:
                        pe.wait_ge(hid_ready, E * FT * g)
                    if t:
                        pe.wait_ge(shifted, j)
                    for a in range(2):
                        nc.tensor.matmul(pH[:, a, :], early_q[0:1, :], late_k[0:1, :], start=True, stop=False,
                                         skip_group_check=True)
                        for b in range(2):
                            last = nc.tensor.matmul(
                                pH[b * S:(b + 1) * S, a, :], qt[:, t * P + b * S:t * P + (b + 1) * S],
                                kx[:, 2 * t + b, a * 8:a * 8 + 8, :], start=False, stop=True,
                                skip_group_check=True)
                    last.then_inc(scores, 1)
                    if t == 0:
                        pe.wait_ge(vx_ready, g + 1)
                    else:
                        pe.wait_ge(pt_ready, j)
                    pe.wait_ge(probs, j + 1)
                    for q in range(HP):
                        last = nc.tensor.transpose(pE[:, q // 4, (q % 4) * P:(q % 4 + 1) * P],
                                                   sd[:, 2 * q:2 * q + 2, :], ident[:, :])
                    last.then_inc(probs_t, 1)
                    pe.wait_ge(pt_ready, j + 1)
                    if t:
                        pe.wait_ge(ot_ready, j)
                    for b in range(2):
                        for q in range(HP):
                            last = nc.tensor.matmul(pX[b * S:(b + 1) * S, q * VW:(q + 1) * VW],
                                                    pt[:, q, b * S:(b + 1) * S], vx[:, g % 2, 2 * t + b, q, :],
                                                    start=True, stop=True)
                    last.then_inc(pv_ps, 1)
                    pe.wait_ge(ov_ready, j + 1)
                    nc.tensor.transpose(pX[:, 0:P], ov[:, :, :], ident[:, :]).then_inc(ov_t, 1)
                pe.wait_ge(ot_ready, NT * (g + 1))
                for t in range(NT):
                    last = nc.tensor.matmul(pX[:, t * D:(t + 1) * D], ot[:, t * P:(t + 1) * P], xwo,
                                            start=True, stop=True)
                last.then_inc(cross_ps, 1)

            def attend(g):
                pe.wait_ge(x2_ready, g + 1)
                pe.wait_ge(normed3, g + 1)
                for t in range(NT):
                    last = nc.tensor.transpose(pX[:, t * P:(t + 1) * P], xn3[:, t, :], ident[:, :])
                last.then_inc(normed3_t, 1)
                pe.wait_ge(x3t_ready, g + 1)
                if g == 0:
                    pe.wait_ge(ws_in, 16)
                nc.tensor.matmul(pX[:, 0:T], fwq, x3t[:, :], start=True, stop=True)
                nc.tensor.matmul(pX[:, T:2 * T], fwk, x3t[:, :], start=True, stop=True).then_inc(fqk_ps, 1)
                pe.wait_ge(pt_ready, NT * (g + 1))
                for b in range(GB):
                    last = nc.tensor.matmul(pE[0:S, 0, b * D:(b + 1) * D], x3t[:, b * S:(b + 1) * S], fwv,
                                            start=True, stop=True)
                last.then_inc(fv_ps, 1)
                pe.wait_ge(fqk_ready, g + 1)
                pe.wait_ge(shifted, NT * (g + 1))
                for t in range(NT):
                    for b in range(2):
                        c = t * P + b * S
                        last = nc.tensor.matmul(pH[b * S:(b + 1) * S, 0, t * S:(t + 1) * S], fq[:, c:c + S],
                                                fk[:, c:c + S], start=True, stop=True)
                last.then_inc(fscores, 1)
                pe.wait_ge(fpn_ready, g + 1)
                for t in range(NT):
                    last = nc.tensor.transpose(pH[0:S, 0, t * P:(t + 1) * P], fpn[:, t, :], ident[:, :])
                last.then_inc(fp_t, 1)
                pe.wait_ge(fpt_ready, g + 1)
                pe.wait_ge(fv_ready, g + 1)
                for b in range(GB):
                    last = nc.tensor.matmul(pX[:, b * S:(b + 1) * S], fv[:, b, :], fpt[:, b * S:(b + 1) * S],
                                            start=True, stop=True)
                last.then_inc(fat_ps, 1)
                pe.wait_ge(fat_ready, g + 1)
                for t in range(NT):
                    last = nc.tensor.matmul(pX[:, t * D:(t + 1) * D], fat[:, t * P:(t + 1) * P], fwo,
                                            start=True, stop=True)
                last.then_inc(self_ps, 1)
                pe.wait_ge(x4_ready, g + 1)
                for t in range(NT):
                    last = nc.tensor.transpose(pX[:, t * P:(t + 1) * P], x4[:, t, :], ident[:, :])
                last.then_inc(x4_t, 1)
                pe.wait_ge(x4t_ready, g + 1)
                for t in range(NT):
                    last = nc.tensor.matmul(pX[:, t * E:(t + 1) * E], x4t[:, g % 2, t * P:(t + 1) * P], wg,
                                            start=True, stop=True)
                last.then_inc(gate_ps, 1)
                pe.wait_ge(gate_ready, g + 1)
                for t in range(NT):
                    last = nc.tensor.transpose(pX[0:E, t * P:(t + 1) * P], gate[:, g % 2, t, :], ident[:, :])
                last.then_inc(gate_t, 1)
                pe.wait_ge(gt_ready, g + 1)
                if g == 0:
                    pe.wait_ge(b2_in, 16)
                for t in range(NT):
                    last = nc.tensor.matmul(pX[:, t * D:(t + 1) * D], gt[:, t * P:(t + 1) * P], b2s[:, :],
                                            start=True, stop=True)
                last.then_inc(bias_ps, 1)

            def experts(g):
                def second(f):
                    i = E * FT * g + f
                    pe.wait_ge(hid_ready, i + 1)
                    n = E * g + f // FT
                    if f % FT == 0 and n >= 2:
                        pe.wait_ge(expert, n - 1)
                    for t in range(NT):
                        last = nc.tensor.matmul(pE[:, n % 2, t * D:(t + 1) * D], hid[:, i % 4, t * P:(t + 1) * P],
                                                w2[:, f, :], start=(f % FT == 0 and t == 0), stop=(f % FT == FT - 1),
                                                skip_group_check=True)
                    last.then_inc(exp_ps, 1)

                if g == 0:
                    pe.wait_ge(w1_in, 16)
                    pe.wait_ge(w2_in, 16)
                pe.wait_ge(fv_ready, g + 1)
                for f in range(E * FT):
                    i = E * FT * g + f
                    if f >= 2:
                        pe.wait_ge(hid_ready, i - 1)
                    nc.tensor.matmul(pH[:, i % 2, 0:T], w1[:, f // FT, (f % FT) * P:(f % FT + 1) * P],
                                     x4t[:, g % 2, :], start=True, stop=True).then_inc(hid_ps, 1)
                    if f:
                        second(f - 1)
                second(E * FT - 1)

            for g in range(NG):
                keys(g)
                front(g)
                for p in range(STEPS):
                    scan(g, p)
                back(g)
                cross(g)
                attend(g)
                experts(g)

        @block.vector
        def _(dve):
            nc.vector.memset(eps[:, :], EPS)
            nc.vector.memset(one[:, :], 1.0)
            nc.vector.memset(mean_w[:, :], 1.0 / DI)
            nc.vector.memset(early_q[0:1, :].rearrange("p (b s) -> p b s", s=S)[:, :, 0:CHUNK], 1.0)
            nc.vector.memset(early_q[0:1, :].rearrange("p (b s) -> p b s", s=S)[:, :, CHUNK:S], 0.0)
            nc.vector.memset(late_k[0:1, :].rearrange("p (b s) -> p b s", s=S)[:, :, 0:CHUNK], 0.0)
            nc.vector.memset(late_k[0:1, :].rearrange("p (b s) -> p b s", s=S)[:, :, CHUNK:S], MASKED)
            nc.vector.memset(xp[:, :, :, 0:PAD], 0.0)
            nc.vector.memset(dA[:, :, :, :, :, 0:1].rearrange("p a h k b s -> p (a h k b) s"), 0.0)
            dve.wait_ge(vec_in, 16)
            nc.vector.tensor_scalar(ncb[:, :], col("conv_b", 0, NH), -1.0, None, ALU.mult)
            dve.wait_ge(expA_ready, 1)
            nc.vector.tensor_scalar(negA[:, :], expA[:, :], -1.0, None, ALU.mult).then_inc(dve_const, 1)
            dve.wait_ge(row_in, 32)
            dve.wait_ge(wm_in, 16)
            nc.vector.tensor_tensor(wconv[:, :, :], bcast("conv_w").rearrange("p (k c) -> p k c", k=TAPS),
                                    w_in_t[:, 0:DI].unsqueeze(1).to_broadcast([P, TAPS, DI]),
                                    ALU.mult).then_inc(dve_const, 1)
            nc.vector.memset(vx[:, :, :, :, :].rearrange("p a b q w -> p (a b q w)"), 0.0).then_inc(dve_const, 1)
            dve.wait_ge(dve_const, 3)
            vxf = vx[:, :, :, :, :].rearrange("p a b q w -> p (a b q) w")
            nc.vector.memset(vxf[0:S, :, HD:HD + 1], 1.0)
            nc.vector.memset(vxf[S:P, :, VW - 1:VW], 1.0).then_inc(dve_const, 1)

            def layernorm(g, src, st_, mv_, rs_, dst, s_stats, s_mv, s_rstd, s_out):
                for t in range(NT):
                    last = nc.vector.bn_stats(st_[:, g, t, :], src(t))
                last.then_inc(s_stats, 1)
                dve.wait_ge(s_stats, g + 1)
                for t in range(NT):
                    last = nc.vector.bn_aggr(mv_[:, g, t, :], st_[:, g, t, :])
                last.then_inc(s_mv, 1)
                dve.wait_ge(s_mv, g + 1)
                dve.wait_ge(s_rstd, g + 1)
                for t in range(NT):
                    last = nc.vector.tensor_scalar(dst(t), src(t), mv_[:, g, t, 0:1], rs_[:, g, t:t + 1],
                                                   ALU.subtract, ALU.mult)
                last.then_inc(s_out, 1)

            def values(g):
                dve.wait_ge(v_ps, g + 1)
                dve.wait_ge(dve_const, 4)
                if g >= 2:
                    dve.wait_ge(pv_ps, NT * (g - 1))
                for k in range(2):
                    rng = slice(k * S, (k + 1) * S)
                    src = pE[rng, 0, :].rearrange("p (b q k d) -> p k b q d", b=GB, k=2, d=HD)[:, k]
                    bias = bcast("x_bv")[rng].rearrange("p (q k d) -> p k q d", k=2, d=HD)[:, k]
                    for b in range(GB):
                        last = nc.vector.tensor_tensor(vx[rng, g % 2, b, :, k * (HD + 1):k * (HD + 1) + HD],
                                                       src[:, b], bias, ALU.add)
                last.then_inc(vx_ready, 1)

            def front(g):
                dve.wait_ge(x_in[g], 16)
                layernorm(g, lambda t: X[:, g * NT + t, :], st, mv, rs, lambda t: xn[:, t, :],
                          stats, mean_var, rstd, normed)
                dve.wait_ge(exp_u, g + 1)
                nc.vector.tensor_scalar(eu[:, :, :], eu[:, :, :], 1.0, None, ALU.add).then_inc(den_u, 1)
                dve.wait_ge(den_u, g + 1)
                nc.vector.reciprocal(eu[:, :, :], eu[:, :, :]).then_inc(sig_u, 1)
                dve.wait_ge(sig_u, g + 1)
                for h in range(NH):
                    last = nc.vector.scalar_tensor_tensor(
                        out=u[:, g % 2, h, :], in0=halves(pF[:, :])[:, h, :], scalar=col("conv_b", h),
                        in1=eu[:, h, :], op0=ALU.add, op1=ALU.mult)
                last.then_inc(u_ready, 1)
                dve.wait_ge(u_ready, g + 1)
                for h in range(NH):
                    last = nc.vector.tensor_scalar(yacc[:, g % 2, h, :], u[:, g % 2, h, :], col("D", h), None, ALU.mult)
                last.then_inc(skip, 1)
                dve.wait_ge(ssm_ready, g + 1)
                nc.vector.tensor_copy(bc[0:32, g % 2, :], ssm[0:32, g % 2, :]).then_inc(split_step, 1)
                dve.wait_ge(split_step, 3 * g + 1)
                nc.vector.tensor_tensor(rem[32:64, :], ssm[0:32, g % 2, :], bc[0:32, g % 2, :],
                                        ALU.subtract).then_inc(split_step, 1)
                dve.wait_ge(split_step, 3 * g + 2)
                nc.vector.tensor_copy(bc[32:64, g % 2, :], rem[32:64, :]).then_inc(split_step, 1)
                dve.wait_ge(split_step, 3 * g + 3)
                nc.vector.tensor_tensor(bc[64:96, g % 2, :], rem[32:64, :], bc[32:64, g % 2, :],
                                        ALU.subtract).then_inc(split, 1)
                dve.wait_ge(exp_dt, g + 1)
                nc.vector.tensor_scalar(de[:, :, :], de[:, :, :], 1.0, None, ALU.min).then_inc(dt_min, 1)
                dve.wait_ge(ln_dt, g + 1)
                nc.vector.tensor_scalar(dlt[:, g % 2, :, :], de[:, :, :], 0.001, 0.1, ALU.max,
                                        ALU.min).then_inc(delta, 1)
                dve.wait_ge(delta, g + 1)
                nc.vector.tensor_tensor(du[:, g % 2, :, :], dlt[:, g % 2, :, :], u[:, g % 2, :, :],
                                        ALU.mult).then_inc(du_ready, 1)
                dve.wait_ge(exp_z, g + 1)
                nc.vector.tensor_scalar(ez[:, :, :], ez[:, :, :], 1.0, None, ALU.add).then_inc(den_z, 1)
                dve.wait_ge(den_z, g + 1)
                nc.vector.reciprocal(ez[:, :, :], ez[:, :, :]).then_inc(sig_z, 1)
                dve.wait_ge(sig_z, g + 1)
                nc.vector.tensor_tensor(sz[:, g % 2, :, :], ez[:, :, :], halves(pF[:, :]), ALU.mult).then_inc(sz_ready, 1)

            def inject(i):
                g = i // STEPS
                dve.wait_ge(b_ps, i + 1)
                if i % STEPS == 0:
                    dve.wait_ge(du_ready, g + 1)
                if i >= 2:
                    dve.wait_ge(state, i - 1)
                nc.vector.tensor_tensor(
                    dBu[:, i % 2, :, :, :], du[:, g % 2, :, :].unsqueeze(2).to_broadcast([P, NH, 2, T]),
                    pB[:, :, :].unsqueeze(1).to_broadcast([P, NH, 2, T]), ALU.mult).then_inc(dbu_ready, 1)

            def scan(g, p):
                i = STEPS * g + p
                if p == 0:
                    inject(i)
                dve.wait_ge(decay, i + 1)
                dve.wait_ge(dbu_ready, i + 1)
                if i >= 2:
                    dve.wait_ge(paired, i - 1)
                nc.vector.tensor_tensor_scan(
                    hs[:, i % 2, :, :, :].rearrange("p h k t -> p (h k t)"), dA[:, i % 2, :, :, :, :].rearrange("p h k b s -> p (h k b s)"),
                    dBu[:, i % 2, :, :, :].rearrange("p h k t -> p (h k t)"), 0.0, ALU.mult, ALU.add).then_inc(state, 1)
                if p < STEPS - 1:
                    inject(i + 1)
                dve.wait_ge(c_ps, i + 1)
                dve.wait_ge(state, i + 1)
                nc.vector.tensor_tensor(
                    hs[:, i % 2, :, :, :], hs[:, i % 2, :, :, :],
                    pC[:, :, :].unsqueeze(1).to_broadcast([P, NH, 2, T]), ALU.mult).then_inc(weighted, 1)

            def back(g):
                dve.wait_ge(summed, STEPS * (g + 1))
                dve.wait_ge(mean_ps, g + 1)
                nc.vector.tensor_tensor(yc[:, :, :], yacc[:, g % 2, :, :],
                                        pX[:, 0:T].unsqueeze(1).to_broadcast([P, NH, T]),
                                        ALU.subtract).then_inc(centred, 1)
                dve.wait_ge(rstd_y, g + 1)
                for h in range(NH):
                    last = nc.vector.scalar_tensor_tensor(out=yn[:, h, :], in0=yc[:, h, :], scalar=col("norm_w", h),
                                                          in1=rsv[:, :], op0=ALU.mult, op1=ALU.mult)
                last.then_inc(scaled, 1)
                dve.wait_ge(scaled, g + 1)
                for h in range(NH):
                    last = nc.vector.scalar_tensor_tensor(out=gy[:, h, :], in0=yn[:, h, :], scalar=col("norm_b", h),
                                                          in1=sz[:, g % 2, h, :], op0=ALU.add, op1=ALU.mult)
                last.then_inc(gated, 1)
                dve.wait_ge(back_ps, g + 1)
                nc.vector.tensor_tensor(x1[:, g % 2, :, :], X[:, g * NT:(g + 1) * NT, :],
                                        pX[:, 0:NT * D].rearrange("p (t d) -> p t d", t=NT), ALU.add).then_inc(x1_ready, 1)

            def cross(g):
                dve.wait_ge(x1_ready, g + 1)
                layernorm(g, lambda t: x1[:, g % 2, t, :], st2, mv2, rs2, lambda t: xn2[:, t, :],
                          stats2, mean_var2, rstd2, normed2)
                nc.vector.tensor_tensor(x1b[:, :, :], x1[:, g % 2, :, :],
                                        bcast("x_bo").unsqueeze(1).to_broadcast([P, NT, D]), ALU.add).then_inc(x1b_ready, 1)
                for t in range(NT):
                    j = NT * g + t
                    dve.wait_ge(scores, j + 1)
                    sc = pH[:, :, :].rearrange("p a (h k) -> p (a h) k", k=S)
                    nc.vector.tensor_reduce(mx[:, :], sc, AX_X, ALU.max).then_inc(maxed, 1)
                    dve.wait_ge(maxed, j + 1)
                    if j:
                        dve.wait_ge(probs_t, j)
                    nc.vector.tensor_tensor(sd[:, :, :], sc, mx[:, :].unsqueeze(2).to_broadcast([P, H, S]),
                                            ALU.subtract).then_inc(shifted, 1)
                    dve.wait_ge(pv_ps, j + 1)
                    pv = pX[:, 0:HP * VW].rearrange("p (h w) -> p h w", w=HD + 1)
                    nc.vector.reciprocal(rc[:, :].unsqueeze(2), pv[:, :, HD:HD + 1]).then_inc(recip, 1)
                    dve.wait_ge(recip, j + 1)
                    nc.vector.tensor_tensor(ov[:, :, :], pv[:, :, 0:HD], rc[:, :].unsqueeze(2).to_broadcast([P, H, HD]),
                                            ALU.mult).then_inc(ov_ready, 1)
                dve.wait_ge(cross_ps, g + 1)
                dve.wait_ge(x1b_ready, g + 1)
                nc.vector.tensor_tensor(x2[:, g % 2, :, :], x1b[:, :, :],
                                        pX[:, 0:NT * D].rearrange("p (t d) -> p t d", t=NT), ALU.add).then_inc(x2_ready, 1)

            def attend(g):
                dve.wait_ge(x2_ready, g + 1)
                layernorm(g, lambda t: x2[:, g % 2, t, :], st3, mv3, rs3, lambda t: xn3[:, t, :],
                          stats3, mean_var3, rstd3, normed3)
                dve.wait_ge(normed3, g + 1)
                nc.vector.tensor_tensor(x3b[:, :, :], xn3[:, :, :],
                                        bcast("f_bo").unsqueeze(1).to_broadcast([P, NT, D]), ALU.add).then_inc(x3b_ready, 1)
                dve.wait_ge(fv_ps, g + 1)
                nc.vector.tensor_copy(fv[:, :, :], pE[0:S, 0, :].rearrange("p (b d) -> p b d", b=GB)).then_inc(fv_ready, 1)
                dve.wait_ge(fscores, g + 1)
                nc.vector.tensor_reduce(fm[:, :], pH[:, 0, 0:NT * S].rearrange("p (t s) -> p t s", t=NT), AX_X,
                                        ALU.max).then_inc(fmaxed, 1)
                dve.wait_ge(fmaxed, g + 1)
                nc.vector.tensor_scalar(fnb[:, :], fm[:, :], -F_SCALE, None, ALU.mult).then_inc(fneg, 1)
                dve.wait_ge(fprobs, g + 1)
                nc.vector.reciprocal(fr[:, :], fs[:, :]).then_inc(frecip, 1)
                dve.wait_ge(frecip, g + 1)
                nc.vector.tensor_tensor(fpn[:, :, :], fp[:, :, :], fr[:, :].unsqueeze(2).to_broadcast([P, NT, S]),
                                        ALU.mult).then_inc(fpn_ready, 1)
                dve.wait_ge(self_ps, g + 1)
                dve.wait_ge(x3b_ready, g + 1)
                nc.vector.tensor_tensor(x4[:, :, :], x3b[:, :, :], pX[:, 0:NT * D].rearrange("p (t d) -> p t d", t=NT),
                                        ALU.add).then_inc(x4_ready, 1)
                dve.wait_ge(x4_ready, g + 1)
                nc.vector.tensor_tensor(x24[:, :, :], x2[:, g % 2, :, :], x4[:, :, :], ALU.add).then_inc(x24_ready, 1)
                dve.wait_ge(gate_ps, g + 1)
                nc.vector.tensor_tensor(gl[:, :, :], pX[:, 0:NT * E].rearrange("p (t e) -> p t e", t=NT),
                                        bcast("bg").unsqueeze(1).to_broadcast([P, NT, E]), ALU.add).then_inc(logits, 1)
                dve.wait_ge(logits, g + 1)
                nc.vector.tensor_reduce(gm[:, :], gl[:, :, :], AX_X, ALU.max).then_inc(gmaxed, 1)
                dve.wait_ge(gmaxed, g + 1)
                nc.vector.tensor_tensor(gd[:, :, :], gl[:, :, :], gm[:, :].unsqueeze(2).to_broadcast([P, NT, E]),
                                        ALU.subtract).then_inc(gshifted, 1)
                dve.wait_ge(gexp, g + 1)
                nc.vector.tensor_reduce(gs[:, :], ge[:, :, :], AX_X, ALU.add).then_inc(gsummed, 1)
                dve.wait_ge(gsummed, g + 1)
                nc.vector.reciprocal(gr[:, :], gs[:, :]).then_inc(grecip, 1)
                dve.wait_ge(grecip, g + 1)
                nc.vector.tensor_tensor(gate[:, g % 2, :, :], ge[:, :, :], gr[:, :].unsqueeze(2).to_broadcast([P, NT, E]),
                                        ALU.mult).then_inc(gate_ready, 1)
                dve.wait_ge(bias_ps, g + 1)
                dve.wait_ge(x24_ready, g + 1)
                nc.vector.tensor_tensor(acc[:, g, :, :], x24[:, :, :], pX[:, 0:NT * D].rearrange("p (t d) -> p t d", t=NT),
                                        ALU.add).then_inc(acc_first, 1)

            def experts(g):
                for e in range(E):
                    n = E * g + e
                    dve.wait_ge(exp_ps, FT * (n + 1))
                    if e:
                        dve.wait_ge(expert, n)
                    else:
                        dve.wait_ge(acc_first, g + 1)
                    for t in range(NT):
                        last = nc.vector.scalar_tensor_tensor(
                            out=acc[:, g, t, :], in0=pE[:, n % 2, t * D:(t + 1) * D], scalar=gate[:, g % 2, t, e:e + 1],
                            in1=acc[:, g, t, :], op0=ALU.mult, op1=ALU.add)
                    last.then_inc(expert, 1)

            for g in range(NG):
                values(g)
                front(g)
                for p in range(STEPS):
                    scan(g, p)
                back(g)
                cross(g)
                attend(g)
                experts(g)


def kernel(**inputs):
    import numpy as _np
    import concourse.bacc as _bacc
    from concourse import mybir as _mybir
    from concourse.bass_utils import run_bass_kernel_spmd as _run

    a = {k: _np.asarray(v) for k, v in inputs.items()}

    def cols_of(v):
        return v.reshape(-1, P).T

    m, xa, f = "L0_attn_", "L0_xattn_", "L0_ffn_"
    laid = {
        "x": a["x"],
        "ctx_t": a["ctx_1024"].reshape(-1, P).T,
        "cols": _np.concatenate(
            [cols_of(a[m + n]) for n in ("conv_b", "dt_proj_b", "D_param", "norm_w", "norm_b")]
            + [a[m + "log_A"].reshape(2, P, 16).transpose(1, 0, 2).reshape(P, 32)]
            + [cols_of(a[n]) for n in (xa + "bq", xa + "bk", f + "bq", f + "bk", f + "bv")]
            + [cols_of(a[f + "b1"].reshape(-1))], axis=1),
        "row": _np.concatenate([a[m + "conv_w"].reshape(256, 4).T.reshape(-1), a[xa + "bv"], a[xa + "bo"],
                                a[f + "bo"], a[f + "bg"]])[None],
        "dt_row": a[m + "dt_proj_w"].reshape(1, 256),
        "w_mamba": _np.concatenate(
            [a[m + "in_proj_w"].T,
             a[m + "x_proj_w"].T.reshape(2, P, 33).transpose(1, 0, 2).reshape(P, 66),
             a[m + "out_proj_w"].T.reshape(2, P, P).transpose(1, 0, 2).reshape(P, 256)], axis=1),
        "w_cross": _np.concatenate([a[xa + n] for n in ("Wq", "Wk", "Wv", "Wo")], axis=1),
        "w_self": _np.concatenate([a[f + n] for n in ("Wq", "Wk", "Wv", "Wo", "Wg")], axis=1),
        "W1": a[f + "W1"],
        "W2": a[f + "W2"],
        "b2": a[f + "b2"],
    }
    nc = _bacc.Bacc("TRN2", target_bir_lowering=False, num_devices=1)
    arrays, args = {}, []
    for name, v in laid.items():
        arrays[f"in_{name}_dram"] = _np.ascontiguousarray(v)
        args.append(nc.dram_tensor(f"in_{name}_dram", v.shape, _mybir.dt.from_np(v.dtype), kind="ExternalInput").ap())
    args.append(nc.dram_tensor("out_0_dram", a["x"].shape, _mybir.dt.float32, kind="ExternalOutput").ap())
    decoder_layer(nc, *args)
    r = _run(nc, [arrays], core_ids=[0])
    return r.results[0]["out_0_dram"]
```

```python
from contextlib import ExitStack

import concourse.bass as bass
from concourse import mybir

F32 = mybir.dt.float32
BF16 = mybir.dt.bfloat16
ALU = mybir.AluOpType
ACT = mybir.ActivationFunctionType
AX_X = mybir.AxisListType.X

P = 128


def columns():
    at, out = 0, {}
    for name, n in (("conv_b", 2), ("dt_b", 2), ("D", 2), ("norm_w", 2), ("norm_b", 2), ("log_A", 32),
                    ("x_bq", 1), ("x_bk", 1), ("f_bq", 1), ("f_bk", 1), ("f_bv", 1), ("b1", 32)):
        out[name] = (at, n)
        at += n
    return out, at


def rows():
    at, out = 0, {}
    for name, n in (("conv_w", 1024), ("x_bv", 128), ("x_bo", 128), ("f_bo", 128), ("bg", 8)):
        out[name] = (at, n)
        at += n
    return out, at


PERIOD = 1177
FRONT = (("stats", -2166), ("rstd", -1667), ("norm", -1010), ("turn", -884), ("pad", -855), ("conv_0", -791),
         ("conv_1", -747), ("exp_u", -727), ("cap_u", -627), ("sig_u", -586), ("u", -564), ("ssm", -516),
         ("ssm_out", -461), ("dt", -415), ("exp_dt", -375), ("cap_dt", -367), ("ln_dt", -345), ("delta", -238),
         ("exp_z", -219), ("cap_z", -175), ("sig_z", -76), ("silu_z", -9))
MEMORY = (("keys", 1235), ("keys_out", 1296), ("values", 1357), ("values_out", 1401))
SCAN = (((0, "scan"), 21), ((0, "inject"), 22), ((0, "read"), 66), ((1, "scan"), 219), ((1, "inject"), 290),
        ((1, "read"), 342), ((2, "scan"), 394), ((2, "inject"), 394), ((2, "read"), 514), ((3, "scan"), 514),
        ((3, "inject"), 564), ((3, "read"), 567), ((4, "scan"), 613), ((4, "inject"), 640), ((4, "read"), 729),
        ((5, "scan"), 785), ((5, "inject"), 785), ((5, "read"), 842), ((6, "scan"), 934), ((6, "inject"), 955),
        ((6, "read"), 1012), ((7, "scan"), 1051), ((7, "inject"), 1066), ((7, "read"), 1082))
MID = (("mean", 1303), ("centre", 1334), ("square", 1334), ("var", 1373), ("rstd_y", 1373), ("gate_y", 1401),
       ("back", 1472), ("x1", 1482), ("rstd2", 1527), ("norm2", 1530), ("turn2", 1564), ("turn2_out", 1588),
       ("query", 1606), ("query_out", 1623), ("scores 0", 1647), ("shift 0", 1710), ("exp 0", 1724),
       ("turn 0", 1728), ("turn_out 0", 1730), ("apply 0", 1734), ("divide 0", 1742), ("scores 2", 1756),
       ("shift 2", 1762), ("exp 2", 1772), ("turn 2", 1786), ("turn_out 2", 1806), ("apply 2", 1806),
       ("divide 2", 1808), ("divide 3", 1815), ("heads", 1826), ("heads_out", 1830), ("cross", 1833), ("x2", 1874),
       ("rstd3", 1909), ("norm3", 1912), ("turn3", 1950), ("turn3_out", 1959), ("fqk", 1984), ("fqk_out", 2000),
       ("fscores", 2000), ("fmax", 2007), ("fexp", 2026), ("fdivide", 2058), ("fturn", 2058), ("fturn_out", 2058),
       ("fapply", 2115), ("fapply_out", 2142), ("self", 2174), ("x4", 2197), ("turn4", 2212), ("turn4_out", 2252),
       ("gates", 2320), ("logits", 2330), ("gexp", 2366), ("gate", 2366), ("gturn", 2383), ("gturn_out", 2383),
       ("bias", 2459), ("first", 2459))
TILES_AT = ((0, 2307), (1, 2372), (2, 2379), (3, 2424), (4, 2469), (5, 2546), (6, 2593), (7, 2593), (8, 2607),
            (9, 2661), (10, 2685), (11, 2706), (12, 2737), (13, 2770), (14, 2816), (15, 2859), (16, 2903),
            (17, 2911), (18, 2954), (19, 2999), (20, 3009), (21, 3078), (22, 3101), (23, 3109), (24, 3155),
            (25, 3198), (26, 3216), (27, 3218), (28, 3346), (29, 3357), (30, 3357), (31, 3449))
TILES = len(TILES_AT)


def timetable(groups):
    threads = (("experts", TILES_AT), ("mid", MID), ("scan", SCAN), ("front", FRONT + MEMORY))
    work = []
    for rank, (what, pieces) in enumerate(threads):
        for g in range(groups):
            for i, (piece, tick) in enumerate(pieces):
                work.append((g * PERIOD + tick, rank, g, i, what, piece))
    for _, _, g, _, what, piece in sorted(work):
        yield what, g, piece


def decoder_layer(nc, x, ctx_t, cols, row, dt_row, w_mamba, w_cross, w_self, W1, W2, b2, out):
    B, S, D = x.shape
    TOK = B * S
    NG = 4
    GB = B // NG
    T = TOK // NG
    NT = T // P
    DI = 256
    NH = DI // P
    N = 16
    TAPS = 4
    PAD = TAPS - 1
    SP = S + PAD
    STEPS = N // 2
    H = 16
    HG = H // 2
    HD = D // H
    CHUNK = 32
    HP = H // 2
    VW = 2 * (HD + 1)
    E = 8
    FT = W1.shape[2] // P
    EPS = 1e-5
    MASKED = -1e30
    CAP = 1e18
    X_SCALE = float(HD) ** -0.5
    F_SCALE = float(D) ** -0.5
    COL, NCOL = columns()
    ROW, NROW = rows()

    with ExitStack() as ctx:
        def sb(name, shape, dt=F32):
            return ctx.enter_context(nc.sbuf_tensor(name, shape, dt))

        def pb(name, shape, dt=F32):
            return ctx.enter_context(nc.psum_tensor(name, shape, dt))

        def sem(name):
            return ctx.enter_context(nc.semaphore(name))

        X = sb("X", [P, NG * NT, D])
        CT = sb("CT", [P, B, 2, S])
        cv = sb("cv", [P, NCOL])
        rw = sb("rw", [P, NROW])
        dtw = sb("dtw", [33, DI])
        wm = sb("wm", [P, 512 + 66 + 256])
        wc = sb("wc", [P, 4 * 128])
        ws = sb("ws", [P, 4 * 128 + E])
        w1 = sb("w1", [P, E, FT * P])
        w2 = sb("w2", [P, E * FT, D])
        b2s = sb("b2s", [E, D])
        ident = sb("ident", [P, P])
        mean_w = sb("mean_w", [P, P])
        eps = sb("eps", [P, 1])
        one = sb("one", [P, 1])
        pick = sb("pick", [96, 2 * N], BF16)
        head = sb("head", [P, HG])
        early_q = sb("early_q", [1, P], BF16)
        late_k = sb("late_k", [1, 512], BF16)
        negA = sb("negA", [P, 2 * N])
        expA = sb("expA", [P, 2 * N])
        ncb = sb("ncb", [P, NH])
        wconv = sb("wconv", [P, TAPS, DI])
        st = sb("st", [P, NG, NT, 6])
        mv = sb("mv", [P, NG, NT, 2])
        lv = sb("lv", [P, NG, NT])
        rs = sb("rs", [P, NG, NT])
        xn = sb("xn", [P, NT, D])
        xp = sb("xp", [P, NG, GB, SP])
        eu = sb("eu", [P, NH, T])
        u = sb("u", [P, 2, NH, T])
        ssm = sb("ssm", [33, 2, T])
        rem = sb("rem", [64, T])
        bc = sb("bc", [96, 2, T], BF16)
        de = sb("de", [P, NH, T])
        dlt = sb("dlt", [P, 2, NH, T])
        du = sb("du", [P, 2, NH, T])
        ez = sb("ez", [P, NH, T])
        sz = sb("sz", [P, 2, NH, T])
        yacc = sb("yacc", [P, 2, NH, T])
        dA = sb("dA", [P, 2, NH, 2, GB, S])
        dBu = sb("dBu", [P, 2, NH, 2, T])
        hs = sb("hs", [P, 2, NH, 2, T])
        pair = sb("pair", [P, NH, T])
        yc = sb("yc", [P, NH, T])
        sq = sb("sq", [P, NH, T])
        lnv = sb("lnv", [P, T])
        rsv = sb("rsv", [P, T])
        yn = sb("yn", [P, NH, T])
        gy = sb("gy", [P, NH, T])
        x1 = sb("x1", [P, 2, NT, D])
        kt = sb("kt", [P, T])
        kx = sb("kx", [P, GB, HG, S])
        vx = sb("vx", [P, 2, GB, HP, VW])
        st2 = sb("st2", [P, NG, NT, 6])
        mv2 = sb("mv2", [P, NG, NT, 2])
        lv2 = sb("lv2", [P, NG, NT])
        rs2 = sb("rs2", [P, NG, NT])
        xn2 = sb("xn2", [P, NT, D])
        x2t = sb("x2t", [P, T])
        qt = sb("qt", [P, GB, 2, S])
        x1b = sb("x1b", [P, NT, D])
        mx = sb("mx", [P, 2, H // 2])
        sd = sb("sd", [P, 2, H // 2, S])
        pt = sb("pt", [P, 2, HP // 2, P])
        rc = sb("rc", [P, H])
        ov = sb("ov", [P, NT, H, HD])
        ot = sb("ot", [P, T])
        x2 = sb("x2", [P, 2, NT, D])
        st3 = sb("st3", [P, NG, NT, 6])
        mv3 = sb("mv3", [P, NG, NT, 2])
        lv3 = sb("lv3", [P, NG, NT])
        rs3 = sb("rs3", [P, NG, NT])
        xn3 = sb("xn3", [P, NT, D])
        x3b = sb("x3b", [P, NT, D])
        x3t = sb("x3t", [P, T])
        fq = sb("fq", [P, T])
        fk = sb("fk", [P, T])
        fv = sb("fv", [S, GB, D])
        fm = sb("fm", [P, NT])
        fnb = sb("fnb", [P, NT])
        fp = sb("fp", [P, NT, S])
        fs = sb("fs", [P, NT])
        fr = sb("fr", [P, NT])
        fpn = sb("fpn", [P, NT, S])
        fpt = sb("fpt", [S, T])
        fat = sb("fat", [P, T])
        x4 = sb("x4", [P, NT, D])
        x4t = sb("x4t", [P, 2, T])
        gl = sb("gl", [P, NT, E])
        gm = sb("gm", [P, NT])
        gd = sb("gd", [P, NT, E])
        ge = sb("ge", [P, NT, E])
        gs = sb("gs", [P, NT])
        gr = sb("gr", [P, NT])
        gate = sb("gate", [P, 2, NT, E])
        gt = sb("gt", [E, T])
        x24 = sb("x24", [P, NT, D])
        hid = sb("hid", [P, 4, T])
        acc = sb("acc", [P, NG, NT, D])

        pF = pb("pF", [P, 512])
        pB = pb("pB", [P, 2, T])
        pC = pb("pC", [P, 2, T])
        pX = pb("pX", [P, 512])
        pY = pb("pY", [P, 512])
        pH = pb("pH", [P, 2, 512])
        pE = pb("pE", [P, 512])

        x_in = [sem(f"x_in{g}") for g in range(NG)]
        ctx_in, vec_in, row_in, wm_in, wc_in, ws_in = (sem(n) for n in ("ctx_in", "vec_in", "row_in", "wm_in", "wc_in", "ws_in"))
        w1_in, w2_in, b2_in, out_done = (sem(n) for n in ("w1_in", "w2_in", "b2_in", "out_done"))
        dve_const, pool_const, pool_step, expA_ready, consts_ready = (sem(n) for n in (
            "dve_const", "pool_const", "pool_step", "expA_ready", "consts_ready"))
        (stats, mean_var, ln_var, rstd, normed, normed_t, padded, inner, exp_u, den_u, sig_u, u_ready, ssm_ps, ssm_ready,
         split, dt_ps, exp_dt, dt_min, ln_dt, delta, du_ready, z_ps, exp_z, den_z, sig_z, sz_ready) = (sem(n) for n in (
            "stats", "mean_var", "ln_var", "rstd", "normed", "normed_t", "padded", "inner", "exp_u", "den_u", "sig_u",
            "u_ready", "ssm_ps", "ssm_ready", "split", "dt_ps", "exp_dt", "dt_min", "ln_dt", "delta", "du_ready", "z_ps",
            "exp_z", "den_z", "sig_z", "sz_ready"))
        split_step = sem("split_step")
        b_ps, c_ps, decay, dbu_ready, state, weighted, paired, summed, skip = (sem(n) for n in (
            "b_ps", "c_ps", "decay", "dbu_ready", "state", "weighted", "paired", "summed", "skip"))
        cap_u, ln_u, cap_z, ln_z = (sem(n) for n in ("cap_u", "ln_u", "cap_z", "ln_z"))
        mean_ps, centred, squared, var_ps, ln_y, rstd_y, scaled, gated, back_ps, x1_ready = (sem(n) for n in (
            "mean_ps", "centred", "squared", "var_ps", "ln_y", "rstd_y", "scaled", "gated", "back_ps", "x1_ready"))
        (k_ps, k_ready, kx_ready, v_ps, vx_ready, stats2, mean_var2, ln_var2, rstd2, normed2, normed2_t, x2t_ready, q_ps,
         q_ready, scores, maxed, shifted, probs, probs_t, pt_ready, pv_ps, recip, ov_ready, ov_t, ot_ready, cross_ps,
         x1b_ready, x2_ready) = (sem(n) for n in (
            "k_ps", "k_ready", "kx_ready", "v_ps", "vx_ready", "stats2", "mean_var2", "ln_var2", "rstd2", "normed2",
            "normed2_t", "x2t_ready", "q_ps", "q_ready", "scores", "maxed", "shifted", "probs", "probs_t", "pt_ready",
            "pv_ps", "recip", "ov_ready", "ov_t", "ot_ready", "cross_ps", "x1b_ready", "x2_ready"))
        (stats3, mean_var3, ln_var3, rstd3, normed3, x3b_ready, normed3_t, x3t_ready, fqk_ps, fqk_ready, fv_ps, fv_ready,
         fscores, fmaxed, fneg, fprobs, frecip, fpn_ready, fp_t, fpt_ready, fat_ps, fat_ready, self_ps, x4_ready, x4_t,
         x4t_ready) = (sem(n) for n in (
            "stats3", "mean_var3", "ln_var3", "rstd3", "normed3", "x3b_ready", "normed3_t", "x3t_ready", "fqk_ps",
            "fqk_ready", "fv_ps", "fv_ready", "fscores", "fmaxed", "fneg", "fprobs", "frecip", "fpn_ready", "fp_t",
            "fpt_ready", "fat_ps", "fat_ready", "self_ps", "x4_ready", "x4_t", "x4t_ready"))
        (gate_ps, logits, gmaxed, gshifted, gexp, gsummed, grecip, gate_ready, gate_t, gt_ready, bias_ps, x24_ready,
         acc_first, hid_ps, hid_ready, exp_ps, expert) = (sem(n) for n in (
            "gate_ps", "logits", "gmaxed", "gshifted", "gexp", "gsummed", "grecip", "gate_ready", "gate_t", "gt_ready",
            "bias_ps", "x24_ready", "acc_first", "hid_ps", "hid_ready", "exp_ps", "expert"))

        block = ctx.enter_context(nc.Block())

        def col(name, i=0, n=1):
            return cv[:, COL[name][0] + i:COL[name][0] + i + n]

        def bcast(name):
            return rw[:, ROW[name][0]:ROW[name][0] + ROW[name][1]]

        w_in_t = wm[:, 0:512]
        w_x = wm[:, 512:512 + 66].rearrange("p (h m) -> p h m", h=NH)
        w_out = wm[:, 578:578 + 256].rearrange("p (h m) -> p h m", h=NH)
        xwq, xwk, xwv, xwo = (wc[:, i * 128:(i + 1) * 128] for i in range(4))
        fwq, fwk, fwv, fwo = (ws[:, i * 128:(i + 1) * 128] for i in range(4))
        wg = ws[:, 512:512 + E]
        x_tiles = x.rearrange("b s d -> (b s) d").rearrange("(n p) d -> p n d", p=P)
        out_tiles = out.rearrange("b s d -> (b s) d").rearrange("(n p) d -> p n d", p=P)

        def halves(ap):
            return ap.rearrange("p (h t) -> p h t", h=NH)

        @block.sync
        def _(sp):
            sp.dma_start(X[:, 0:NT, :], x_tiles[:, 0:NT, :]).then_inc(x_in[0], 16)
            sp.dma_start(cv[:, :], cols).then_inc(vec_in, 16)
            sp.dma_start(wm[:, :], w_mamba).then_inc(wm_in, 16)
            sp.dma_start(rw[:, :], row.to_broadcast([P, NROW])).then_inc(row_in, 16)
            sp.dma_start(dtw[32:33, :], dt_row).then_inc(row_in, 16)
            for k in range(2):
                sp.dma_start(CT[:, :, k, :], ctx_t.rearrange("d (b s) -> d b s", b=B)).then_inc(ctx_in, 16)
            sp.dma_start(wc[:, :], w_cross).then_inc(wc_in, 16)
            for g in range(1, NG):
                sp.dma_start(X[:, g * NT:(g + 1) * NT, :], x_tiles[:, g * NT:(g + 1) * NT, :]).then_inc(x_in[g], 16)
            sp.dma_start(ws[:, :], w_self).then_inc(ws_in, 16)
            sp.dma_start(b2s[:, :], b2).then_inc(b2_in, 16)
            sp.dma_start(w1[:, :, :], W1.rearrange("e h f -> h e f")).then_inc(w1_in, 16)
            sp.dma_start(w2[:, :, :], W2.rearrange("e (t p) h -> p (e t) h", p=P)).then_inc(w2_in, 16)
            for g in range(NG):
                sp.wait_ge(expert, E * (g + 1))
                sp.dma_start(out_tiles[:, g * NT:(g + 1) * NT, :], acc[:, g, :, :]).then_inc(out_done, 16)
            sp.wait_ge(out_done, 16 * NG)

        @block.gpsimd
        def _(pool):
            done = [0]

            def step(ins):
                done[0] += 1
                ins.then_inc(pool_step, 1)
                pool.wait_ge(pool_step, done[0])

            step(nc.gpsimd.memset(ident[:, :], 0.0))
            nc.gpsimd.affine_select(out=ident[:, :], in_=ident[:, :], compare_op=ALU.not_equal, fill=1.0, base=0,
                                    pattern=[[-1, P]], channel_multiplier=1).then_inc(pool_const, 1)
            step(nc.gpsimd.memset(head[:, :], 1.0))
            for k in range(2):
                part = head[k * S:(k + 1) * S, :]
                step(nc.gpsimd.affine_select(out=part, in_=part, compare_op=ALU.is_ge, fill=0.0, base=0,
                                             pattern=[[-HD, HG]], channel_multiplier=1))
                step(nc.gpsimd.affine_select(out=part, in_=part, compare_op=ALU.is_ge, fill=0.0, base=HD - 1,
                                             pattern=[[HD, HG]], channel_multiplier=-1))
            step(nc.gpsimd.memset(pick[:, :], 0.0))
            for j in range(3):
                last = nc.gpsimd.affine_select(out=pick[:, :], in_=pick[:, :], compare_op=ALU.not_equal, fill=1.0,
                                               base=-2 * N * j, pattern=[[-1, 2 * N]], channel_multiplier=1)
                if j < 2:
                    step(last)
            last.then_inc(pool_const, 1)

            def keys(g):
                pool.wait_ge(k_ready, g + 1)
                if g:
                    pool.wait_ge(scores, 2 * NT * g)
                for b in range(GB):
                    last = nc.gpsimd.tensor_tensor(
                        kx[:, b, :, :],
                        kt[:, b * S:(b + 1) * S].unsqueeze(1).to_broadcast([P, HG, S]),
                        head[:, :].unsqueeze(2).to_broadcast([P, HG, S]), ALU.mult)
                last.then_inc(kx_ready, 1)

            def scan(g, p):
                i = STEPS * g + p
                if p == 0:
                    pool.wait_ge(skip, g + 1)
                if i:
                    pool.wait_ge(summed, i)
                pool.wait_ge(weighted, i + 1)
                nc.gpsimd.tensor_tensor(pair[:, :, :], hs[:, i % 2, :, 0, :], hs[:, i % 2, :, 1, :],
                                        ALU.add).then_inc(paired, 1)
                pool.wait_ge(paired, i + 1)
                nc.gpsimd.tensor_tensor(yacc[:, g % 2, :, :], yacc[:, g % 2, :, :], pair[:, :, :],
                                        ALU.add).then_inc(summed, 1)

            for what, g, piece in timetable(NG):
                if what == "scan" and piece[1] == "read":
                    scan(g, piece[0])
                if what == "front" and piece == "keys_out":
                    keys(g)

        @block.scalar
        def _(act):
            nc.scalar.preload_act_table_set("natural_log_exp_and_others")
            act.wait_ge(vec_in, 16)
            nc.scalar.activation(expA[:, :], col("log_A", 0, 2 * N), ACT.Exp).then_inc(expA_ready, 1)
            act.wait_ge(dve_const, 1)

            def rsqrt(g, mv_, lv_, rs_, ready, ln_done, done):
                act.wait_ge(ready, g + 1)
                nc.scalar.activation(lv_[:, g, :], mv_[:, g, :, 1], ACT.Ln, bias=eps[:, :]).then_inc(ln_done, 1)
                act.wait_ge(ln_done, g + 1)
                nc.scalar.activation(rs_[:, g, :], lv_[:, g, :], ACT.Exp, scale=-0.5).then_inc(done, 1)

            def front(g, piece):
                if piece == "rstd":
                    rsqrt(g, mv, lv, rs, mean_var, ln_var, rstd)
                elif piece == "pad":
                    act.wait_ge(normed_t, g + 1)
                    nc.scalar.activation(xp[:, g, :, PAD:SP], pF[:, 0:T].rearrange("p (b s) -> p b s", b=GB),
                                         ACT.Copy).then_inc(padded, 1)
                elif piece == "exp_u":
                    act.wait_ge(inner, g + 1)
                    if g:
                        act.wait_ge(u_ready, g)
                    for h in range(NH):
                        last = nc.scalar.activation(eu[:, h, :], halves(pF[:, :])[:, h, :], ACT.Exp, scale=-1.0,
                                                    bias=ncb[:, h:h + 1])
                    last.then_inc(exp_u, 1)
                elif piece == "sig_u":
                    act.wait_ge(cap_u, g + 1)
                    nc.scalar.activation(eu[:, :, :], eu[:, :, :], ACT.Ln, bias=one[:, :]).then_inc(ln_u, 1)
                    act.wait_ge(ln_u, g + 1)
                    nc.scalar.activation(eu[:, :, :], eu[:, :, :], ACT.Exp, scale=-1.0).then_inc(sig_u, 1)
                elif piece == "ssm_out":
                    act.wait_ge(ssm_ps, g + 1)
                    nc.scalar.activation(ssm[:, g % 2, :], pF[0:33, 0:T], ACT.Copy).then_inc(ssm_ready, 1)
                elif piece == "exp_dt":
                    act.wait_ge(dt_ps, g + 1)
                    if g:
                        act.wait_ge(delta, g)
                    for h in range(NH):
                        last = nc.scalar.activation(de[:, h, :], halves(pF[:, :])[:, h, :], ACT.Exp,
                                                    bias=col("dt_b", h))
                    last.then_inc(exp_dt, 1)
                elif piece == "ln_dt":
                    act.wait_ge(dt_min, g + 1)
                    nc.scalar.activation(de[:, :, :], de[:, :, :], ACT.Ln, bias=one[:, :]).then_inc(ln_dt, 1)
                elif piece == "exp_z":
                    act.wait_ge(z_ps, g + 1)
                    if g:
                        act.wait_ge(sz_ready, g)
                    nc.scalar.activation(ez[:, :, :], halves(pF[:, :]), ACT.Exp, scale=-1.0).then_inc(exp_z, 1)
                elif piece == "sig_z":
                    act.wait_ge(cap_z, g + 1)
                    nc.scalar.activation(ez[:, :, :], ez[:, :, :], ACT.Ln, bias=one[:, :]).then_inc(ln_z, 1)
                    act.wait_ge(ln_z, g + 1)
                    nc.scalar.activation(ez[:, :, :], ez[:, :, :], ACT.Exp, scale=-1.0).then_inc(sig_z, 1)
                elif piece == "keys_out":
                    act.wait_ge(k_ps, g + 1)
                    if g:
                        act.wait_ge(kx_ready, g)
                    nc.scalar.activation(kt[:, :], pF[:, 0:T], ACT.Identity, bias=col("x_bk")).then_inc(k_ready, 1)

            def decays(g, p):
                i = STEPS * g + p
                if p == 0:
                    act.wait_ge(delta, g + 1)
                if i >= 2:
                    act.wait_ge(state, i - 1)
                for h in range(NH):
                    for k in range(2):
                        a = h * N + 2 * p + k
                        last = nc.scalar.activation(
                            dA[:, i % 2, h, k, :, 1:S],
                            dlt[:, g % 2, h, :].rearrange("p (b s) -> p b s", b=GB)[:, :, 1:S],
                            ACT.Exp, scale=negA[:, a:a + 1])
                last.then_inc(decay, 1)

            def scan(g, piece):
                p, op = piece
                if p == 0 and op == "scan":
                    decays(g, 0)
                if op == "inject" and p + 1 < STEPS:
                    decays(g, p + 1)

            def weights(j):
                act.wait_ge(shifted, j + 1)
                nc.scalar.activation(sd[:, j % 2, :, :], sd[:, j % 2, :, :], ACT.Exp, scale=X_SCALE).then_inc(probs, 1)

            def weights_t(j):
                act.wait_ge(probs_t, j + 1)
                nc.scalar.activation(pt[:, j % 2, :, :], (pX, pY)[j % 2][:, :].rearrange("p (h t) -> p h t", t=P),
                                     ACT.Copy).then_inc(pt_ready, 1)

            def mid(g, piece):
                j = 2 * NT * g + 2 * (piece[-1] == "2" and piece[-2] == " ")
                if piece == "square":
                    act.wait_ge(centred, g + 1)
                    nc.scalar.activation(sq[:, :, :], yc[:, :, :], ACT.Square).then_inc(squared, 1)
                elif piece == "rstd_y":
                    act.wait_ge(var_ps, g + 1)
                    nc.scalar.activation(lnv[:, :], pX[:, 0:T], ACT.Ln, bias=eps[:, :]).then_inc(ln_y, 1)
                    act.wait_ge(ln_y, g + 1)
                    nc.scalar.activation(rsv[:, :], lnv[:, :], ACT.Exp, scale=-0.5).then_inc(rstd_y, 1)
                elif piece == "rstd2":
                    rsqrt(g, mv2, lv2, rs2, mean_var2, ln_var2, rstd2)
                elif piece == "turn2_out":
                    act.wait_ge(normed2_t, g + 1)
                    nc.scalar.activation(x2t[:, :], pX[:, 0:T], ACT.Copy).then_inc(x2t_ready, 1)
                elif piece == "query_out":
                    act.wait_ge(q_ps, g + 1)
                    if g == 0:
                        act.wait_ge(dve_const, 4)
                    for k in range(2):
                        rng = slice(k * S, (k + 1) * S)
                        last = nc.scalar.activation(qt[rng, :, k, :], pX[rng, 0:T].rearrange("p (b s) -> p b s", b=GB),
                                                    ACT.Identity, bias=col("x_bq")[rng])
                    last.then_inc(q_ready, 1)
                elif piece in ("exp 0", "exp 2"):
                    weights(j)
                elif piece in ("turn 0", "turn 2"):
                    weights(j + 1)
                elif piece in ("turn_out 0", "turn_out 2"):
                    weights_t(j)
                elif piece in ("apply 0", "apply 2"):
                    weights_t(j + 1)
                elif piece == "heads_out":
                    act.wait_ge(ov_t, g + 1)
                    nc.scalar.activation(ot[:, :], pX[:, 0:T], ACT.Copy).then_inc(ot_ready, 1)
                elif piece == "rstd3":
                    rsqrt(g, mv3, lv3, rs3, mean_var3, ln_var3, rstd3)
                elif piece == "turn3_out":
                    act.wait_ge(normed3_t, g + 1)
                    nc.scalar.activation(x3t[:, :], pX[:, 0:T], ACT.Copy).then_inc(x3t_ready, 1)
                elif piece == "fqk_out":
                    act.wait_ge(fqk_ps, g + 1)
                    nc.scalar.activation(fq[:, :], pX[:, 0:T], ACT.Identity, bias=col("f_bq"))
                    nc.scalar.activation(fk[:, :], pX[:, T:2 * T], ACT.Identity, bias=col("f_bk")).then_inc(fqk_ready, 1)
                elif piece == "fexp":
                    act.wait_ge(fneg, g + 1)
                    for t in range(NT):
                        last = nc.scalar.activation(fp[:, t, :], pX[:, t * S:(t + 1) * S], ACT.Exp, scale=F_SCALE,
                                                    bias=fnb[:, t:t + 1], accum_out=fs[:, t:t + 1])
                    last.then_inc(fprobs, 1)
                elif piece == "fturn_out":
                    act.wait_ge(fp_t, g + 1)
                    nc.scalar.activation(fpt[:, :], pY[0:S, 0:T], ACT.Copy).then_inc(fpt_ready, 1)
                elif piece == "fapply_out":
                    act.wait_ge(fat_ps, g + 1)
                    nc.scalar.activation(fat[:, :], pX[:, 0:T], ACT.Identity, bias=col("f_bv")).then_inc(fat_ready, 1)
                elif piece == "turn4_out":
                    act.wait_ge(x4_t, g + 1)
                    if g >= 2:
                        act.wait_ge(hid_ps, TILES * (g - 1))
                    nc.scalar.activation(x4t[:, g % 2, :], pX[:, 0:T], ACT.Copy).then_inc(x4t_ready, 1)
                elif piece == "gexp":
                    act.wait_ge(gshifted, g + 1)
                    nc.scalar.activation(ge[:, :, :], gd[:, :, :], ACT.Exp).then_inc(gexp, 1)
                elif piece == "gturn_out":
                    act.wait_ge(gate_t, g + 1)
                    nc.scalar.activation(gt[:, :], pX[0:E, 0:T], ACT.Copy).then_inc(gt_ready, 1)

            def experts(g, f):
                i = TILES * g + f
                act.wait_ge(hid_ps, i + 1)
                if i >= 4:
                    act.wait_ge(exp_ps, i - 3)
                nc.scalar.activation(hid[:, i % 4, :], pH[:, i % 2, 0:T], ACT.Relu,
                                     bias=col("b1", f)).then_inc(hid_ready, 1)

            for what, g, piece in timetable(NG):
                {"front": front, "scan": scan, "mid": mid, "experts": experts}[what](g, piece)

        @block.tensor
        def _(pe):
            def front(g, piece):
                if piece == "turn":
                    if g == 0:
                        pe.wait_ge(pool_const, 1)
                    elif g == 1:
                        pe.wait_ge(sz_ready, g)
                    else:
                        pe.wait_ge(vx_ready, g - 1)
                    pe.wait_ge(normed, g + 1)
                    for t in range(NT):
                        last = nc.tensor.transpose(pF[:, t * P:(t + 1) * P], xn[:, t, :], ident[:, :])
                    last.then_inc(normed_t, 1)
                elif piece in ("conv_0", "conv_1"):
                    h = int(piece[-1])
                    if h == 0:
                        if g == 0:
                            pe.wait_ge(dve_const, 2)
                        pe.wait_ge(padded, g + 1)
                    for k in range(TAPS):
                        last = nc.tensor.matmul(halves(pF[:, :])[:, h, :], wconv[:, k, h * P:(h + 1) * P],
                                                xp[:, g, :, k:k + S], start=(k == 0), stop=(k == TAPS - 1))
                    if h == NH - 1:
                        last.then_inc(inner, 1)
                elif piece == "ssm":
                    pe.wait_ge(exp_u, g + 1)
                    pe.wait_ge(u_ready, g + 1)
                    for h in range(NH):
                        last = nc.tensor.matmul(pF[0:33, 0:T], w_x[:, h, :], u[:, g % 2, h, :],
                                                start=(h == 0), stop=(h == NH - 1))
                    last.then_inc(ssm_ps, 1)
                elif piece == "dt":
                    if g == 0:
                        pe.wait_ge(row_in, 32)
                    pe.wait_ge(ssm_ready, g + 1)
                    for h in range(NH):
                        last = nc.tensor.matmul(halves(pF[:, :])[:, h, :], dtw[32:33, h * P:(h + 1) * P],
                                                ssm[32:33, g % 2, :], start=True, stop=True)
                    last.then_inc(dt_ps, 1)
                elif piece == "cap_dt":
                    pe.wait_ge(exp_dt, g + 1)
                    for h in range(NH):
                        last = nc.tensor.matmul(halves(pF[:, :])[:, h, :], w_in_t[:, DI + h * P:DI + (h + 1) * P],
                                                xp[:, g, :, PAD:SP], start=True, stop=True)
                    last.then_inc(z_ps, 1)
                elif piece == "keys":
                    if g == 0:
                        pe.wait_ge(ctx_in, 32)
                        pe.wait_ge(wc_in, 16)
                    pe.wait_ge(sz_ready, min(g + 2, NG))
                    nc.tensor.matmul(pF[:, 0:T], xwk, CT[:, g * GB:(g + 1) * GB, 0, :], start=True, stop=True).then_inc(k_ps, 1)
                elif piece == "values":
                    pe.wait_ge(k_ready, g + 1)
                    for b in range(GB):
                        last = nc.tensor.matmul(pF[:, b * D:(b + 1) * D], CT[:, g * GB + b, :, :], xwv,
                                                start=True, stop=True)
                    last.then_inc(v_ps, 1)

            def spread_b(i):
                g, p = divmod(i, STEPS)
                if i % STEPS == 0:
                    pe.wait_ge(split, g + 1)
                if i == 0:
                    pe.wait_ge(pool_const, 2)
                else:
                    pe.wait_ge(dbu_ready, i)
                for k in range(2):
                    last = nc.tensor.matmul(pB[:, k, :], pick[:, 2 * p + k:2 * p + k + 1].to_broadcast([96, P]), bc[:, g % 2, :], start=True, stop=True)
                last.then_inc(b_ps, 1)

            def scan(g, piece):
                p, op = piece
                i = STEPS * g + p
                if op == "scan":
                    if p == 0:
                        spread_b(i)
                    if i:
                        pe.wait_ge(weighted, i)
                    for k in range(2):
                        last = nc.tensor.matmul(pC[:, k, :], pick[:, N + 2 * p + k:N + 2 * p + k + 1].to_broadcast([96, P]), bc[:, g % 2, :], start=True,
                                                stop=True)
                    last.then_inc(c_ps, 1)
                    if p + 1 < STEPS:
                        spread_b(i + 1)

            def score(g, j):
                b = j % GB
                bank = (pX, pY)[j % 2]
                nc.tensor.matmul(bank[:, :], early_q[0:1, :], late_k[0:1, :], start=True, stop=False,
                                 skip_group_check=True)
                nc.tensor.matmul(bank[:, :], qt[:, b, :, :], kx[:, b, :, :], start=False, stop=True,
                                 skip_group_check=True).then_inc(scores, 1)

            def turn(j):
                pe.wait_ge(probs, j + 1)
                for q in range(HP // 2):
                    last = nc.tensor.transpose((pX, pY)[j % 2][:, q * P:(q + 1) * P],
                                               sd[:, j % 2, 2 * q:2 * q + 2, :], ident[:, :])
                last.then_inc(probs_t, 1)

            def apply(g, j):
                b, rows_ = j % GB, slice((j % 2) * S, (j % 2 + 1) * S)
                pe.wait_ge(pt_ready, j + 1)
                for k in range(2):
                    for q in range(HG // 2):
                        at = k * (HG // 2) + q
                        last = nc.tensor.matmul((pX, pY)[j % 2][rows_, at * VW:(at + 1) * VW],
                                                pt[:, j % 2, q, k * S:(k + 1) * S], vx[:, g % 2, b, at, :],
                                                start=True, stop=True)
                last.then_inc(pv_ps, 1)

            def mid(g, piece):
                j = 2 * NT * g + 2 * (piece[-1] == "2" and piece[-2] == " ")
                if piece == "mean":
                    pe.wait_ge(summed, STEPS * (g + 1))
                    if g:
                        pe.wait_ge(acc_first, g)
                    for h in range(NH):
                        last = nc.tensor.matmul(pX[:, 0:T], mean_w[:, :], yacc[:, g % 2, h, :],
                                                start=(h == 0), stop=(h == NH - 1))
                    last.then_inc(mean_ps, 1)
                elif piece == "var":
                    pe.wait_ge(centred, g + 1)
                    pe.wait_ge(squared, g + 1)
                    for h in range(NH):
                        last = nc.tensor.matmul(pX[:, 0:T], mean_w[:, :], sq[:, h, :],
                                                start=(h == 0), stop=(h == NH - 1))
                    last.then_inc(var_ps, 1)
                elif piece == "back":
                    pe.wait_ge(ln_y, g + 1)
                    pe.wait_ge(gated, g + 1)
                    for t in range(NT):
                        for h in range(NH):
                            last = nc.tensor.matmul(pX[:, t * D:(t + 1) * D], gy[:, h, t * P:(t + 1) * P],
                                                    w_out[:, h, :], start=(h == 0), stop=(h == NH - 1))
                    last.then_inc(back_ps, 1)
                elif piece == "turn2":
                    pe.wait_ge(x1_ready, g + 1)
                    pe.wait_ge(normed2, g + 1)
                    for t in range(NT):
                        last = nc.tensor.transpose(pX[:, t * P:(t + 1) * P], xn2[:, t, :], ident[:, :])
                    last.then_inc(normed2_t, 1)
                elif piece == "query":
                    pe.wait_ge(x2t_ready, g + 1)
                    nc.tensor.matmul(pX[:, 0:T], xwq, x2t[:, :], start=True, stop=True).then_inc(q_ps, 1)
                elif piece == "scores 0":
                    pe.wait_ge(q_ready, g + 1)
                    pe.wait_ge(kx_ready, g + 1)
                    score(g, j)
                    score(g, j + 1)
                elif piece == "scores 2":
                    pe.wait_ge(ov_ready, j - 1)
                    score(g, j)
                elif piece == "shift 2":
                    pe.wait_ge(ov_ready, j)
                    score(g, j + 1)
                elif piece in ("turn 0", "turn 2"):
                    turn(j)
                elif piece in ("turn_out 0", "turn_out 2"):
                    turn(j + 1)
                elif piece in ("apply 0", "apply 2"):
                    apply(g, j)
                elif piece in ("divide 0", "divide 2"):
                    apply(g, j + 1)
                elif piece == "heads":
                    pe.wait_ge(ov_ready, 2 * NT * (g + 1))
                    for t in range(NT):
                        last = nc.tensor.transpose(pX[:, t * P:(t + 1) * P], ov[:, t, :, :], ident[:, :])
                    last.then_inc(ov_t, 1)
                elif piece == "cross":
                    pe.wait_ge(ot_ready, g + 1)
                    for t in range(NT):
                        last = nc.tensor.matmul(pX[:, t * D:(t + 1) * D], ot[:, t * P:(t + 1) * P], xwo,
                                                start=True, stop=True)
                    last.then_inc(cross_ps, 1)
                elif piece == "turn3":
                    pe.wait_ge(x2_ready, g + 1)
                    pe.wait_ge(normed3, g + 1)
                    for t in range(NT):
                        last = nc.tensor.transpose(pX[:, t * P:(t + 1) * P], xn3[:, t, :], ident[:, :])
                    last.then_inc(normed3_t, 1)
                elif piece == "fqk":
                    pe.wait_ge(x3t_ready, g + 1)
                    if g == 0:
                        pe.wait_ge(ws_in, 16)
                    nc.tensor.matmul(pX[:, 0:T], fwq, x3t[:, :], start=True, stop=True)
                    nc.tensor.matmul(pX[:, T:2 * T], fwk, x3t[:, :], start=True, stop=True).then_inc(fqk_ps, 1)
                    for b in range(GB):
                        last = nc.tensor.matmul(pY[0:S, b * D:(b + 1) * D], x3t[:, b * S:(b + 1) * S], fwv,
                                                start=True, stop=True)
                    last.then_inc(fv_ps, 1)
                elif piece == "fscores":
                    pe.wait_ge(fqk_ready, g + 1)
                    for t in range(NT):
                        for b in range(2):
                            c = t * P + b * S
                            last = nc.tensor.matmul(pX[b * S:(b + 1) * S, t * S:(t + 1) * S], fq[:, c:c + S],
                                                    fk[:, c:c + S], start=True, stop=True)
                    last.then_inc(fscores, 1)
                elif piece == "fturn":
                    pe.wait_ge(fv_ready, g + 1)
                    pe.wait_ge(fpn_ready, g + 1)
                    for t in range(NT):
                        last = nc.tensor.transpose(pY[0:S, t * P:(t + 1) * P], fpn[:, t, :], ident[:, :])
                    last.then_inc(fp_t, 1)
                elif piece == "fapply":
                    pe.wait_ge(fpt_ready, g + 1)
                    for b in range(GB):
                        last = nc.tensor.matmul(pX[:, b * S:(b + 1) * S], fv[:, b, :], fpt[:, b * S:(b + 1) * S],
                                                start=True, stop=True)
                    last.then_inc(fat_ps, 1)
                elif piece == "self":
                    pe.wait_ge(fat_ready, g + 1)
                    for t in range(NT):
                        last = nc.tensor.matmul(pX[:, t * D:(t + 1) * D], fat[:, t * P:(t + 1) * P], fwo,
                                                start=True, stop=True)
                    last.then_inc(self_ps, 1)
                elif piece == "turn4":
                    pe.wait_ge(x4_ready, g + 1)
                    for t in range(NT):
                        last = nc.tensor.transpose(pX[:, t * P:(t + 1) * P], x4[:, t, :], ident[:, :])
                    last.then_inc(x4_t, 1)
                elif piece == "gates":
                    pe.wait_ge(x4t_ready, g + 1)
                    for t in range(NT):
                        last = nc.tensor.matmul(pX[:, t * E:(t + 1) * E], x4t[:, g % 2, t * P:(t + 1) * P], wg,
                                                start=True, stop=True)
                    last.then_inc(gate_ps, 1)
                elif piece == "gturn":
                    pe.wait_ge(gate_ready, g + 1)
                    for t in range(NT):
                        last = nc.tensor.transpose(pX[0:E, t * P:(t + 1) * P], gate[:, g % 2, t, :], ident[:, :])
                    last.then_inc(gate_t, 1)
                elif piece == "bias":
                    pe.wait_ge(gt_ready, g + 1)
                    if g == 0:
                        pe.wait_ge(b2_in, 16)
                    for t in range(NT):
                        last = nc.tensor.matmul(pX[:, t * D:(t + 1) * D], gt[:, t * P:(t + 1) * P], b2s[:, :],
                                                start=True, stop=True)
                    last.then_inc(bias_ps, 1)

            def second(g, f):
                i = TILES * g + f
                pe.wait_ge(hid_ready, i + 1)
                n = E * g + f // FT
                if f % FT == 0 and n:
                    pe.wait_ge(expert, n)
                for t in range(NT):
                    last = nc.tensor.matmul(pE[:, t * D:(t + 1) * D], hid[:, i % 4, t * P:(t + 1) * P],
                                            w2[:, f, :], start=(f % FT == 0 and t == 0), stop=(f % FT == FT - 1),
                                            skip_group_check=True)
                last.then_inc(exp_ps, 1)

            def experts(g, f):
                i = TILES * g + f
                if i == 0:
                    pe.wait_ge(w1_in, 16)
                    pe.wait_ge(w2_in, 16)
                if f == 0:
                    pe.wait_ge(x4t_ready, g + 1)
                if i >= 2:
                    pe.wait_ge(hid_ready, i - 1)
                nc.tensor.matmul(pH[:, i % 2, 0:T], w1[:, f // FT, (f % FT) * P:(f % FT + 1) * P],
                                 x4t[:, g % 2, :], start=True, stop=True).then_inc(hid_ps, 1)
                if f:
                    second(g, f - 1)
                if f == TILES - 1:
                    second(g, f)

            for what, g, piece in timetable(NG):
                {"front": front, "scan": scan, "mid": mid, "experts": experts}[what](g, piece)

        @block.vector
        def _(dve):
            nc.vector.memset(eps[:, :], EPS)
            nc.vector.memset(one[:, :], 1.0)
            nc.vector.memset(mean_w[:, :], 1.0 / DI)
            nc.vector.memset(early_q[0:1, :].rearrange("p (b s) -> p b s", s=S)[:, :, 0:CHUNK], 1.0)
            nc.vector.memset(early_q[0:1, :].rearrange("p (b s) -> p b s", s=S)[:, :, CHUNK:S], 0.0)
            nc.vector.memset(late_k[0:1, :].rearrange("p (b s) -> p b s", s=S)[:, :, 0:CHUNK], 0.0)
            nc.vector.memset(late_k[0:1, :].rearrange("p (b s) -> p b s", s=S)[:, :, CHUNK:S], MASKED)
            nc.vector.memset(xp[:, :, :, 0:PAD], 0.0)
            nc.vector.memset(dA[:, :, :, :, :, 0:1].rearrange("p a h k b s -> p (a h k b) s"), 0.0)
            dve.wait_ge(vec_in, 16)
            nc.vector.tensor_scalar(ncb[:, :], col("conv_b", 0, NH), -1.0, None, ALU.mult)
            dve.wait_ge(expA_ready, 1)
            nc.vector.tensor_scalar(negA[:, :], expA[:, :], -1.0, None, ALU.mult).then_inc(dve_const, 1)
            dve.wait_ge(row_in, 32)
            dve.wait_ge(wm_in, 16)
            nc.vector.tensor_tensor(wconv[:, :, :], bcast("conv_w").rearrange("p (k c) -> p k c", k=TAPS),
                                    w_in_t[:, 0:DI].unsqueeze(1).to_broadcast([P, TAPS, DI]),
                                    ALU.mult).then_inc(dve_const, 1)
            nc.vector.memset(vx[:, :, :, :, :].rearrange("p a b q w -> p (a b q w)"), 0.0).then_inc(dve_const, 1)
            dve.wait_ge(dve_const, 3)
            nc.vector.memset(qt[:, :, :, :], 0.0)
            vxf = vx[:, :, :, :, :].rearrange("p a b q w -> p (a b q) w")
            nc.vector.memset(vxf[0:S, :, HD:HD + 1], 1.0)
            nc.vector.memset(vxf[S:P, :, VW - 1:VW], 1.0).then_inc(dve_const, 1)

            def statistics(g, src, st_, mv_, s_stats, s_mv):
                for t in range(NT):
                    last = nc.vector.bn_stats(st_[:, g, t, :], src(t))
                last.then_inc(s_stats, 1)
                dve.wait_ge(s_stats, g + 1)
                for t in range(NT):
                    last = nc.vector.bn_aggr(mv_[:, g, t, :], st_[:, g, t, :])
                last.then_inc(s_mv, 1)

            def normalise(g, src, mv_, rs_, dst, s_mv, s_rstd, s_out):
                dve.wait_ge(s_mv, g + 1)
                dve.wait_ge(s_rstd, g + 1)
                for t in range(NT):
                    last = nc.vector.tensor_scalar(dst(t), src(t), mv_[:, g, t, 0:1], rs_[:, g, t:t + 1],
                                                   ALU.subtract, ALU.mult)
                last.then_inc(s_out, 1)

            def front(g, piece):
                src = lambda t: X[:, g * NT + t, :]
                if piece == "stats":
                    dve.wait_ge(x_in[g], 16)
                    statistics(g, src, st, mv, stats, mean_var)
                elif piece == "norm":
                    if g:
                        dve.wait_ge(normed_t, g)
                    normalise(g, src, mv, rs, lambda t: xn[:, t, :], mean_var, rstd, normed)
                elif piece == "cap_u":
                    dve.wait_ge(exp_u, g + 1)
                    nc.vector.tensor_scalar(eu[:, :, :], eu[:, :, :], CAP, None, ALU.min).then_inc(cap_u, 1)
                elif piece == "u":
                    dve.wait_ge(sig_u, g + 1)
                    for h in range(NH):
                        last = nc.vector.scalar_tensor_tensor(
                            out=u[:, g % 2, h, :], in0=halves(pF[:, :])[:, h, :], scalar=col("conv_b", h),
                            in1=eu[:, h, :], op0=ALU.add, op1=ALU.mult)
                    last.then_inc(u_ready, 1)
                elif piece == "ssm":
                    dve.wait_ge(u_ready, g + 1)
                    if g >= 2:
                        dve.wait_ge(mean_ps, g - 1)
                        dve.wait_ge(centred, g - 1)
                    for h in range(NH):
                        last = nc.vector.tensor_scalar(yacc[:, g % 2, h, :], u[:, g % 2, h, :], col("D", h), None,
                                                       ALU.mult)
                    last.then_inc(skip, 1)
                elif piece == "dt":
                    dve.wait_ge(ssm_ready, g + 1)
                    nc.vector.tensor_copy(bc[0:32, g % 2, :], ssm[0:32, g % 2, :]).then_inc(split_step, 1)
                    dve.wait_ge(split_step, 3 * g + 1)
                    nc.vector.tensor_tensor(rem[32:64, :], ssm[0:32, g % 2, :], bc[0:32, g % 2, :],
                                            ALU.subtract).then_inc(split_step, 1)
                elif piece == "exp_dt":
                    dve.wait_ge(split_step, 3 * g + 2)
                    nc.vector.tensor_copy(bc[32:64, g % 2, :], rem[32:64, :]).then_inc(split_step, 1)
                    dve.wait_ge(split_step, 3 * g + 3)
                    nc.vector.tensor_tensor(bc[64:96, g % 2, :], rem[32:64, :], bc[32:64, g % 2, :],
                                            ALU.subtract).then_inc(split, 1)
                elif piece == "cap_dt":
                    dve.wait_ge(exp_dt, g + 1)
                    nc.vector.tensor_scalar(de[:, :, :], de[:, :, :], 1.0, None, ALU.min).then_inc(dt_min, 1)
                elif piece == "delta":
                    dve.wait_ge(ln_dt, g + 1)
                    nc.vector.tensor_scalar(dlt[:, g % 2, :, :], de[:, :, :], 0.001, 0.1, ALU.max,
                                            ALU.min).then_inc(delta, 1)
                    dve.wait_ge(delta, g + 1)
                    nc.vector.tensor_tensor(du[:, g % 2, :, :], dlt[:, g % 2, :, :], u[:, g % 2, :, :],
                                            ALU.mult).then_inc(du_ready, 1)
                elif piece == "cap_z":
                    dve.wait_ge(exp_z, g + 1)
                    nc.vector.tensor_scalar(ez[:, :, :], ez[:, :, :], CAP, None, ALU.min).then_inc(cap_z, 1)
                elif piece == "silu_z":
                    dve.wait_ge(sig_z, g + 1)
                    nc.vector.tensor_tensor(sz[:, g % 2, :, :], ez[:, :, :], halves(pF[:, :]),
                                            ALU.mult).then_inc(sz_ready, 1)
                elif piece == "values_out":
                    dve.wait_ge(v_ps, g + 1)
                    dve.wait_ge(dve_const, 4)
                    if g >= 2:
                        dve.wait_ge(pv_ps, 2 * NT * (g - 1))
                    for k in range(2):
                        rng = slice(k * S, (k + 1) * S)
                        val = pF[rng, :].rearrange("p (b q k d) -> p k b q d", b=GB, k=2, d=HD)[:, k]
                        bias = bcast("x_bv")[rng].rearrange("p (q k d) -> p k q d", k=2, d=HD)[:, k]
                        for b in range(GB):
                            last = nc.vector.tensor_tensor(vx[rng, g % 2, b, :, k * (HD + 1):k * (HD + 1) + HD],
                                                           val[:, b], bias, ALU.add)
                    last.then_inc(vx_ready, 1)

            def inject(i):
                g = i // STEPS
                dve.wait_ge(b_ps, i + 1)
                if i % STEPS == 0:
                    dve.wait_ge(du_ready, g + 1)
                if i >= 2:
                    dve.wait_ge(state, i - 1)
                nc.vector.tensor_tensor(
                    dBu[:, i % 2, :, :, :], du[:, g % 2, :, :].unsqueeze(2).to_broadcast([P, NH, 2, T]),
                    pB[:, :, :].unsqueeze(1).to_broadcast([P, NH, 2, T]), ALU.mult).then_inc(dbu_ready, 1)

            def scan(g, piece):
                p, op = piece
                i = STEPS * g + p
                if op == "scan":
                    if p == 0:
                        inject(i)
                    dve.wait_ge(decay, i + 1)
                    dve.wait_ge(dbu_ready, i + 1)
                    if i >= 2:
                        dve.wait_ge(paired, i - 1)
                    nc.vector.tensor_tensor_scan(
                        hs[:, i % 2, :, :, :].rearrange("p h k t -> p (h k t)"),
                        dA[:, i % 2, :, :, :, :].rearrange("p h k b s -> p (h k b s)"),
                        dBu[:, i % 2, :, :, :].rearrange("p h k t -> p (h k t)"), 0.0, ALU.mult,
                        ALU.add).then_inc(state, 1)
                elif op == "inject":
                    if p < STEPS - 1:
                        inject(i + 1)
                else:
                    dve.wait_ge(c_ps, i + 1)
                    dve.wait_ge(state, i + 1)
                    nc.vector.tensor_tensor(
                        hs[:, i % 2, :, :, :], hs[:, i % 2, :, :, :],
                        pC[:, :, :].unsqueeze(1).to_broadcast([P, NH, 2, T]), ALU.mult).then_inc(weighted, 1)

            def shift(j):
                bank = (pX, pY)[j % 2][:, :].rearrange("p (h k) -> p h k", k=S)
                dve.wait_ge(scores, j + 1)
                nc.vector.tensor_reduce(mx[:, j % 2, :], bank, AX_X, ALU.max).then_inc(maxed, 1)
                dve.wait_ge(maxed, j + 1)
                nc.vector.tensor_tensor(sd[:, j % 2, :, :], bank, mx[:, j % 2, :].unsqueeze(2).to_broadcast([P, H // 2, S]),
                                        ALU.subtract).then_inc(shifted, 1)

            def divide(j):
                t, rows_ = (j // 2) % NT, slice((j % 2) * S, (j % 2 + 1) * S)
                pv = (pX, pY)[j % 2][rows_, 0:HP * VW].rearrange("p (h w) -> p h w", w=HD + 1)
                dve.wait_ge(pv_ps, j + 1)
                nc.vector.reciprocal(rc[rows_, :].unsqueeze(2), pv[:, :, HD:HD + 1]).then_inc(recip, 1)
                dve.wait_ge(recip, j + 1)
                nc.vector.tensor_tensor(ov[rows_, t, :, :], pv[:, :, 0:HD], rc[rows_, :].unsqueeze(2).to_broadcast([S, H, HD]),
                                        ALU.mult).then_inc(ov_ready, 1)

            def mid(g, piece):
                j = 2 * NT * g + 2 * (piece[-1] == "2" and piece[-2] == " ")
                tiles = pX[:, 0:NT * D].rearrange("p (t d) -> p t d", t=NT)
                if piece == "centre":
                    dve.wait_ge(summed, STEPS * (g + 1))
                    dve.wait_ge(mean_ps, g + 1)
                    nc.vector.tensor_tensor(yc[:, :, :], yacc[:, g % 2, :, :],
                                            pX[:, 0:T].unsqueeze(1).to_broadcast([P, NH, T]),
                                            ALU.subtract).then_inc(centred, 1)
                elif piece == "gate_y":
                    dve.wait_ge(rstd_y, g + 1)
                    for h in range(NH):
                        last = nc.vector.scalar_tensor_tensor(out=yn[:, h, :], in0=yc[:, h, :], scalar=col("norm_w", h),
                                                              in1=rsv[:, :], op0=ALU.mult, op1=ALU.mult)
                    last.then_inc(scaled, 1)
                    dve.wait_ge(scaled, g + 1)
                    for h in range(NH):
                        last = nc.vector.scalar_tensor_tensor(out=gy[:, h, :], in0=yn[:, h, :], scalar=col("norm_b", h),
                                                              in1=sz[:, g % 2, h, :], op0=ALU.add, op1=ALU.mult)
                    last.then_inc(gated, 1)
                elif piece == "x1":
                    dve.wait_ge(back_ps, g + 1)
                    nc.vector.tensor_tensor(x1[:, g % 2, :, :], X[:, g * NT:(g + 1) * NT, :], tiles,
                                            ALU.add).then_inc(x1_ready, 1)
                    dve.wait_ge(x1_ready, g + 1)
                    statistics(g, lambda t: x1[:, g % 2, t, :], st2, mv2, stats2, mean_var2)
                elif piece == "norm2":
                    normalise(g, lambda t: x1[:, g % 2, t, :], mv2, rs2, lambda t: xn2[:, t, :], mean_var2, rstd2,
                              normed2)
                    nc.vector.tensor_tensor(x1b[:, :, :], x1[:, g % 2, :, :],
                                            bcast("x_bo").unsqueeze(1).to_broadcast([P, NT, D]),
                                            ALU.add).then_inc(x1b_ready, 1)
                elif piece in ("shift 0", "shift 2"):
                    shift(j)
                elif piece in ("exp 0", "exp 2"):
                    shift(j + 1)
                elif piece == "divide 0":
                    divide(j)
                elif piece == "scores 2":
                    divide(j - 1)
                elif piece == "divide 2":
                    divide(j)
                elif piece == "divide 3":
                    divide(2 * NT * g + 3)
                elif piece == "x2":
                    dve.wait_ge(cross_ps, g + 1)
                    dve.wait_ge(x1b_ready, g + 1)
                    nc.vector.tensor_tensor(x2[:, g % 2, :, :], x1b[:, :, :], tiles, ALU.add).then_inc(x2_ready, 1)
                    dve.wait_ge(x2_ready, g + 1)
                    statistics(g, lambda t: x2[:, g % 2, t, :], st3, mv3, stats3, mean_var3)
                elif piece == "norm3":
                    normalise(g, lambda t: x2[:, g % 2, t, :], mv3, rs3, lambda t: xn3[:, t, :], mean_var3, rstd3,
                              normed3)
                    dve.wait_ge(normed3, g + 1)
                    nc.vector.tensor_tensor(x3b[:, :, :], xn3[:, :, :],
                                            bcast("f_bo").unsqueeze(1).to_broadcast([P, NT, D]),
                                            ALU.add).then_inc(x3b_ready, 1)
                elif piece == "fqk_out":
                    dve.wait_ge(fv_ps, g + 1)
                    nc.vector.tensor_copy(fv[:, :, :],
                                          pY[0:S, :].rearrange("p (b d) -> p b d", b=GB)).then_inc(fv_ready, 1)
                elif piece == "fmax":
                    dve.wait_ge(fscores, g + 1)
                    nc.vector.tensor_reduce(fm[:, :], pX[:, 0:NT * S].rearrange("p (t s) -> p t s", t=NT), AX_X,
                                            ALU.max).then_inc(fmaxed, 1)
                    dve.wait_ge(fmaxed, g + 1)
                    nc.vector.tensor_scalar(fnb[:, :], fm[:, :], -F_SCALE, None, ALU.mult).then_inc(fneg, 1)
                elif piece == "fdivide":
                    dve.wait_ge(fprobs, g + 1)
                    nc.vector.reciprocal(fr[:, :], fs[:, :]).then_inc(frecip, 1)
                    dve.wait_ge(frecip, g + 1)
                    nc.vector.tensor_tensor(fpn[:, :, :], fp[:, :, :], fr[:, :].unsqueeze(2).to_broadcast([P, NT, S]),
                                            ALU.mult).then_inc(fpn_ready, 1)
                elif piece == "x4":
                    dve.wait_ge(self_ps, g + 1)
                    dve.wait_ge(x3b_ready, g + 1)
                    nc.vector.tensor_tensor(x4[:, :, :], x3b[:, :, :], tiles, ALU.add).then_inc(x4_ready, 1)
                    dve.wait_ge(x4_ready, g + 1)
                    nc.vector.tensor_tensor(x24[:, :, :], x2[:, g % 2, :, :], x4[:, :, :], ALU.add).then_inc(x24_ready, 1)
                elif piece == "logits":
                    dve.wait_ge(gate_ps, g + 1)
                    nc.vector.tensor_tensor(gl[:, :, :], pX[:, 0:NT * E].rearrange("p (t e) -> p t e", t=NT),
                                            bcast("bg").unsqueeze(1).to_broadcast([P, NT, E]), ALU.add).then_inc(logits, 1)
                    dve.wait_ge(logits, g + 1)
                    nc.vector.tensor_reduce(gm[:, :], gl[:, :, :], AX_X, ALU.max).then_inc(gmaxed, 1)
                    dve.wait_ge(gmaxed, g + 1)
                    nc.vector.tensor_tensor(gd[:, :, :], gl[:, :, :], gm[:, :].unsqueeze(2).to_broadcast([P, NT, E]),
                                            ALU.subtract).then_inc(gshifted, 1)
                elif piece == "gate":
                    dve.wait_ge(gexp, g + 1)
                    nc.vector.tensor_reduce(gs[:, :], ge[:, :, :], AX_X, ALU.add).then_inc(gsummed, 1)
                    dve.wait_ge(gsummed, g + 1)
                    nc.vector.reciprocal(gr[:, :], gs[:, :]).then_inc(grecip, 1)
                    dve.wait_ge(grecip, g + 1)
                    nc.vector.tensor_tensor(gate[:, g % 2, :, :], ge[:, :, :],
                                            gr[:, :].unsqueeze(2).to_broadcast([P, NT, E]),
                                            ALU.mult).then_inc(gate_ready, 1)
                elif piece == "first":
                    dve.wait_ge(bias_ps, g + 1)
                    dve.wait_ge(x24_ready, g + 1)
                    nc.vector.tensor_tensor(acc[:, g, :, :], x24[:, :, :], tiles, ALU.add).then_inc(acc_first, 1)

            def add_expert(g, e):
                n = E * g + e
                dve.wait_ge(exp_ps, FT * (n + 1))
                if e:
                    dve.wait_ge(expert, n)
                else:
                    dve.wait_ge(acc_first, g + 1)
                for t in range(NT):
                    last = nc.vector.scalar_tensor_tensor(
                        out=acc[:, g, t, :], in0=pE[:, t * D:(t + 1) * D], scalar=gate[:, g % 2, t, e:e + 1],
                        in1=acc[:, g, t, :], op0=ALU.mult, op1=ALU.add)
                last.then_inc(expert, 1)

            def experts(g, f):
                if f and f % FT == 0:
                    add_expert(g, f // FT - 1)
                if f == TILES - 1:
                    add_expert(g, E - 1)

            for what, g, piece in timetable(NG):
                {"front": front, "scan": scan, "mid": mid, "experts": experts}[what](g, piece)


def kernel(**inputs):
    import numpy as _np
    import concourse.bacc as _bacc
    from concourse import mybir as _mybir
    from concourse.bass_utils import run_bass_kernel_spmd as _run

    a = {k: _np.asarray(v) for k, v in inputs.items()}

    def cols_of(v):
        return v.reshape(-1, P).T

    m, xa, f = "L0_attn_", "L0_xattn_", "L0_ffn_"
    laid = {
        "x": a["x"],
        "ctx_t": a["ctx_1024"].reshape(-1, P).T,
        "cols": _np.concatenate(
            [cols_of(a[m + n]) for n in ("conv_b", "dt_proj_b", "D_param", "norm_w", "norm_b")]
            + [a[m + "log_A"].reshape(2, P, 16).transpose(1, 0, 2).reshape(P, 32)]
            + [cols_of(a[n]) for n in (xa + "bq", xa + "bk", f + "bq", f + "bk", f + "bv")]
            + [cols_of(a[f + "b1"].reshape(-1))], axis=1),
        "row": _np.concatenate([a[m + "conv_w"].reshape(256, 4).T.reshape(-1), a[xa + "bv"], a[xa + "bo"],
                                a[f + "bo"], a[f + "bg"]])[None],
        "dt_row": a[m + "dt_proj_w"].reshape(1, 256),
        "w_mamba": _np.concatenate(
            [a[m + "in_proj_w"].T,
             a[m + "x_proj_w"].T.reshape(2, P, 33).transpose(1, 0, 2).reshape(P, 66),
             a[m + "out_proj_w"].T.reshape(2, P, P).transpose(1, 0, 2).reshape(P, 256)], axis=1),
        "w_cross": _np.concatenate([a[xa + n] for n in ("Wq", "Wk", "Wv", "Wo")], axis=1),
        "w_self": _np.concatenate([a[f + n] for n in ("Wq", "Wk", "Wv", "Wo", "Wg")], axis=1),
        "W1": a[f + "W1"],
        "W2": a[f + "W2"],
        "b2": a[f + "b2"],
    }
    nc = _bacc.Bacc("TRN2", target_bir_lowering=False, num_devices=1)
    arrays, args = {}, []
    for name, v in laid.items():
        arrays[f"in_{name}_dram"] = _np.ascontiguousarray(v)
        args.append(nc.dram_tensor(f"in_{name}_dram", v.shape, _mybir.dt.from_np(v.dtype), kind="ExternalInput").ap())
    args.append(nc.dram_tensor("out_0_dram", a["x"].shape, _mybir.dt.float32, kind="ExternalOutput").ap())
    decoder_layer(nc, *args)
    r = _run(nc, [arrays], core_ids=[0])
    return r.results[0]["out_0_dram"]
```

```python
from contextlib import ExitStack

import concourse.bass as bass
from concourse import mybir

F32 = mybir.dt.float32
BF16 = mybir.dt.bfloat16
ALU = mybir.AluOpType
ACT = mybir.ActivationFunctionType
AX_X = mybir.AxisListType.X

P = 128


def columns():
    at, out = 0, {}
    for name, n in (("conv_b", 2), ("dt_b", 2), ("D", 2), ("norm_w", 2), ("norm_b", 2), ("log_A", 32),
                    ("x_bq", 1), ("x_bk", 1), ("f_bq", 1), ("f_bk", 1), ("f_bv", 1), ("b1", 32)):
        out[name] = (at, n)
        at += n
    return out, at


def rows():
    at, out = 0, {}
    for name, n in (("conv_w", 1024), ("x_bv", 128), ("x_bo", 128), ("f_bo", 128), ("bg", 8)):
        out[name] = (at, n)
        at += n
    return out, at


BATCHES = (4, 4, 4, 4)

FRONT = (("stats", 0), ("rstd", 492), ("norm", 882), ("turn", 1343), ("pad", 1405), ("conv_0", 1460),
         ("conv_1", 1562), ("exp_u", 1573), ("cap_u", 1604), ("sig_u", 1736), ("u", 1772), ("ssm", 1821),
         ("ssm_out", 1837), ("dt", 1871), ("exp_dt", 1888), ("cap_dt", 1903), ("ln_dt", 1927), ("delta", 1939),
         ("du", 1939), ("exp_z", 1948), ("cap_z", 2001), ("sig_z", 2189), ("silu_z", 2249))
MEMORY = (("keys", 0), ("keys_out", 0), ("values", 27), ("values_out", 54))
SCAN = (((0, "scan"), 0), ((0, "inject"), 60), ((0, "read"), 60), ((1, "scan"), 232), ((1, "inject"), 338),
        ((1, "read"), 418), ((2, "scan"), 461), ((2, "inject"), 487), ((2, "read"), 514), ((3, "scan"), 564),
        ((3, "inject"), 596), ((3, "read"), 603), ((4, "scan"), 643), ((4, "inject"), 686), ((4, "read"), 786),
        ((5, "scan"), 804), ((5, "inject"), 843), ((5, "read"), 881), ((6, "scan"), 973), ((6, "inject"), 976),
        ((6, "read"), 977), ((7, "scan"), 1058), ((7, "inject"), 1134), ((7, "read"), 1134))
MID = (("mean", 0), ("centre", 6), ("square", 81), ("var", 126), ("rstd_y", 126), ("gate_y", 134), ("back", 221),
       ("x1", 247), ("rstd2", 251), ("norm2", 276), ("x1b", 305), ("turn2", 307), ("turn2_out", 310), ("query", 316),
       ("query_out", 336), ("scores 0", 371), ("scores 1", 378), ("shift 0", 405), ("shift 1", 410), ("exp 0", 413),
       ("exp 1", 444), ("turn 0", 459), ("turn 1", 464), ("turn_out 0", 464), ("turn_out 1", 465), ("apply 0", 484),
       ("apply 1", 514), ("divide 0", 523), ("divide 1", 526), ("scores 2", 543), ("scores 3", 543), ("shift 2", 566),
       ("shift 3", 566), ("exp 2", 580), ("exp 3", 595), ("turn 2", 605), ("turn 3", 605), ("turn_out 2", 605),
       ("turn_out 3", 605), ("apply 2", 649), ("apply 3", 676), ("divide 2", 696), ("divide 3", 714), ("heads", 748),
       ("heads_out", 750), ("cross", 772), ("x2", 782), ("rstd3", 814), ("norm3", 819), ("x3b", 831), ("turn3", 844),
       ("turn3_out", 850), ("fqk", 862), ("fqk_out", 876), ("fscores", 880), ("fmax", 890), ("fexp", 904),
       ("fdivide", 904), ("fturn", 932), ("fturn_out", 951), ("fapply", 961), ("fapply_out", 961), ("self", 976),
       ("x4", 983), ("x24", 993), ("turn4", 1004), ("turn4_out", 1042), ("gates", 1049), ("logits", 1049),
       ("gexp", 1051), ("gate", 1063), ("gturn", 1094), ("gturn_out", 1101), ("bias", 1149), ("first", 1158))
HIDDEN = ((0, 0), (1, 62), (2, 115), (3, 196), (4, 240), (5, 276), (6, 325), (7, 327), (8, 376), (9, 414), (10, 471),
          (11, 521), (12, 531), (13, 563), (14, 586), (15, 686), (16, 700), (17, 764), (18, 785), (19, 863),
          (20, 910), (21, 932), (22, 975), (23, 991), (24, 1012), (25, 1070), (26, 1090), (27, 1137), (28, 1154),
          (29, 1180), (30, 1234), (31, 1279))
TILES = len(HIDDEN)
THREADS = (
    ("experts", HIDDEN, (4040, 5267, 6520, 7745), (96, 98, 91, 18)),
    ("mid", MID, (2962, 4191, 5388, 6526), (101, 99, 95, 107)),
    ("scan", SCAN, (1633, 2880, 4055, 5298), (89, 95, 101, 92)),
    ("front", FRONT, (0, 814, 1973, 3210), (79, 83, 102, 101)),
    ("front", MEMORY, (2956, 4424, 5616, 6718), (74, 102, 143, 114)),
)


def timetable():
    work = []
    for rank, (what, pieces, starts, paces) in enumerate(THREADS):
        for g, batches in enumerate(BATCHES):
            for i, (piece, ticks) in enumerate(pieces):
                if what == "mid" and " " in piece and int(piece[-1]) >= batches:
                    continue
                work.append((starts[g] + ticks * paces[g] // 100, rank, g, i, what, piece))
    for _, _, g, _, what, piece in sorted(work, key=lambda entry: entry[:4]):
        yield what, g, piece


def decoder_layer(nc, x, ctx_t, cols, row, dt_row, w_mamba, w_cross, w_self, W1, W2, b2, out):
    B, S, D = x.shape
    NG = len(BATCHES)
    GB = max(BATCHES)
    T = GB * S
    NT = T // P
    FIRST = [sum(BATCHES[:g]) for g in range(NG + 1)]
    DI = 256
    NH = DI // P
    N = 16
    TAPS = 4
    PAD = TAPS - 1
    SP = S + PAD
    STEPS = N // 2
    H = 16
    HG = H // 2
    HD = D // H
    CHUNK = 32
    HP = H // 2
    VW = 2 * (HD + 1)
    E = 8
    FT = W1.shape[2] // P
    EPS = 1e-5
    MASKED = -1e30
    CAP = 1e18
    X_SCALE = float(HD) ** -0.5
    F_SCALE = float(D) ** -0.5
    COL, NCOL = columns()
    ROW, NROW = rows()

    with ExitStack() as ctx:
        def sb(name, shape, dt=F32):
            return ctx.enter_context(nc.sbuf_tensor(name, shape, dt))

        def pb(name, shape, dt=F32):
            return ctx.enter_context(nc.psum_tensor(name, shape, dt))

        def sem(name):
            return ctx.enter_context(nc.semaphore(name))

        X = sb("X", [P, B // 2, D])
        CT = sb("CT", [P, B, 2, S])
        cv = sb("cv", [P, NCOL])
        rw = sb("rw", [P, NROW])
        dtw = sb("dtw", [33, DI])
        wm = sb("wm", [P, 512 + 66 + 256])
        wc = sb("wc", [P, 4 * 128])
        ws = sb("ws", [P, 4 * 128 + E])
        w1 = sb("w1", [P, E, FT * P])
        w2 = sb("w2", [P, E * FT, D])
        b2s = sb("b2s", [E, D])
        ident = sb("ident", [P, P])
        mean_w = sb("mean_w", [P, P])
        eps = sb("eps", [P, 1])
        one = sb("one", [P, 1])
        pick = sb("pick", [96, 2 * N], BF16)
        head = sb("head", [P, HG])
        early_q = sb("early_q", [1, P], BF16)
        late_k = sb("late_k", [1, 512], BF16)
        negA = sb("negA", [P, 2 * N])
        expA = sb("expA", [P, 2 * N])
        ncb = sb("ncb", [P, NH])
        wconv = sb("wconv", [P, TAPS, DI])
        st = sb("st", [P, NG, NT, 6])
        mv = sb("mv", [P, NG, NT, 2])
        lv = sb("lv", [P, NG, NT])
        rs = sb("rs", [P, NG, NT])
        xn = sb("xn", [P, NT, D])
        xp = sb("xp", [P, B, SP])
        eu = sb("eu", [P, NH, T])
        u = sb("u", [P, 2, NH, T])
        ssm = sb("ssm", [33, 2, T])
        rem = sb("rem", [64, T])
        bc = sb("bc", [96, 2, T], BF16)
        de = sb("de", [P, NH, T])
        dlt = sb("dlt", [P, 2, NH, T])
        du = sb("du", [P, 2, NH, T])
        ez = sb("ez", [P, NH, T])
        sz = sb("sz", [P, 2, NH, T])
        yacc = sb("yacc", [P, 2, NH, T])
        dA = sb("dA", [P, 2, NH * 2 * T])
        dBu = sb("dBu", [P, 2, NH * 2 * T])
        hs = sb("hs", [P, 2, NH * 2 * T])
        pair = sb("pair", [P, NH, T])
        yc = sb("yc", [P, NH, T])
        sq = sb("sq", [P, NH, T])
        lnv = sb("lnv", [P, T])
        rsv = sb("rsv", [P, T])
        yn = sb("yn", [P, NH, T])
        gy = sb("gy", [P, NH, T])
        x1 = sb("x1", [P, 2, NT, D])
        kt = sb("kt", [P, T])
        kx = sb("kx", [P, GB, HG, S])
        vx = sb("vx", [P, 2, GB, HP, VW])
        st2 = sb("st2", [P, NG, NT, 6])
        mv2 = sb("mv2", [P, NG, NT, 2])
        lv2 = sb("lv2", [P, NG, NT])
        rs2 = sb("rs2", [P, NG, NT])
        xn2 = sb("xn2", [P, NT, D])
        x2t = sb("x2t", [P, T])
        qt = sb("qt", [P, GB, 2, S])
        x1b = sb("x1b", [P, NT, D])
        mx = sb("mx", [P, 2, H // 2])
        sd = sb("sd", [P, 2, H // 2, S])
        pt = sb("pt", [P, 2, HP // 2, P])
        rc = sb("rc", [P, H])
        ov = sb("ov", [P, NT, H, HD])
        ot = sb("ot", [P, T])
        x2 = sb("x2", [P, 2, NT, D])
        st3 = sb("st3", [P, NG, NT, 6])
        mv3 = sb("mv3", [P, NG, NT, 2])
        lv3 = sb("lv3", [P, NG, NT])
        rs3 = sb("rs3", [P, NG, NT])
        xn3 = sb("xn3", [P, NT, D])
        x3b = sb("x3b", [P, NT, D])
        x3t = sb("x3t", [P, T])
        fq = sb("fq", [P, T])
        fk = sb("fk", [P, T])
        fv = sb("fv", [S, GB, D])
        fm = sb("fm", [P, NT])
        fnb = sb("fnb", [P, NT])
        fp = sb("fp", [P, NT, S])
        fs = sb("fs", [P, NT])
        fr = sb("fr", [P, NT])
        fpn = sb("fpn", [P, NT, S])
        fpt = sb("fpt", [S, T])
        fat = sb("fat", [P, T])
        x4 = sb("x4", [P, NT, D])
        x4t = sb("x4t", [P, 2, T])
        gl = sb("gl", [P, NT, E])
        gm = sb("gm", [P, NT])
        gd = sb("gd", [P, NT, E])
        ge = sb("ge", [P, NT, E])
        gs = sb("gs", [P, NT])
        gr = sb("gr", [P, NT])
        gate = sb("gate", [P, 2, NT, E])
        gt = sb("gt", [E, T])
        x24 = sb("x24", [P, NT, D])
        hid = sb("hid", [P, 4, T])
        acc = sb("acc", [P, B // 2, D])

        pF = pb("pF", [P, 512])
        pB = pb("pB", [P, 2, T])
        pC = pb("pC", [P, 2, T])
        pX = pb("pX", [P, 512])
        pY = pb("pY", [P, 512])
        pH = pb("pH", [P, 2, 512])
        pE = pb("pE", [P, 512])

        x_in = [sem(f"x_in{g}") for g in range(NG)]
        ctx_in, vec_in, row_in, wm_in, wc_in, ws_in = (sem(n) for n in ("ctx_in", "vec_in", "row_in", "wm_in",
                                                                        "wc_in", "ws_in"))
        w1_in, w2_in, b2_in, out_done = (sem(n) for n in ("w1_in", "w2_in", "b2_in", "out_done"))
        dve_const, pool_const, pool_step, expA_ready = (sem(n) for n in (
            "dve_const", "pool_const", "pool_step", "expA_ready"))
        (stats, mean_var, ln_var, rstd, normed, normed_t, padded, inner, exp_u, sig_u, u_ready, ssm_ps, ssm_ready,
         split, dt_ps, exp_dt, dt_min, ln_dt, delta, du_ready, z_ps, exp_z, sig_z, sz_ready) = (sem(n) for n in (
            "stats", "mean_var", "ln_var", "rstd", "normed", "normed_t", "padded", "inner", "exp_u", "sig_u",
            "u_ready", "ssm_ps", "ssm_ready", "split", "dt_ps", "exp_dt", "dt_min", "ln_dt", "delta", "du_ready",
                "z_ps",
            "exp_z", "sig_z", "sz_ready"))
        split_step = sem("split_step")
        b_ps, c_ps, decay, dbu_ready, state, weighted, paired, summed, skip = (sem(n) for n in (
            "b_ps", "c_ps", "decay", "dbu_ready", "state", "weighted", "paired", "summed", "skip"))
        cap_u, ln_u, cap_z, ln_z = (sem(n) for n in ("cap_u", "ln_u", "cap_z", "ln_z"))
        mean_ps, centred, squared, var_ps, ln_y, rstd_y, scaled, gated, back_ps, x1_ready = (sem(n) for n in (
            "mean_ps", "centred", "squared", "var_ps", "ln_y", "rstd_y", "scaled", "gated", "back_ps", "x1_ready"))
        (k_ps, k_ready, kx_ready, v_ps, vx_ready, stats2, mean_var2, ln_var2, rstd2, normed2, normed2_t, x2t_ready,
         q_ps,
         q_ready, scores, maxed, shifted, probs, probs_t, pt_ready, pv_ps, recip, ov_ready, ov_t, ot_ready, cross_ps,
         x1b_ready, x2_ready) = (sem(n) for n in (
            "k_ps", "k_ready", "kx_ready", "v_ps", "vx_ready", "stats2", "mean_var2", "ln_var2", "rstd2", "normed2",
            "normed2_t", "x2t_ready", "q_ps", "q_ready", "scores", "maxed", "shifted", "probs", "probs_t", "pt_ready",
            "pv_ps", "recip", "ov_ready", "ov_t", "ot_ready", "cross_ps", "x1b_ready", "x2_ready"))
        (stats3, mean_var3, ln_var3, rstd3, normed3, x3b_ready, normed3_t, x3t_ready, fqk_ps, fqk_ready, fv_ps,
         fv_ready,
         fscores, fmaxed, fneg, fprobs, frecip, fpn_ready, fp_t, fpt_ready, fat_ps, fat_ready, self_ps, x4_ready, x4_t,
         x4t_ready) = (sem(n) for n in (
            "stats3", "mean_var3", "ln_var3", "rstd3", "normed3", "x3b_ready", "normed3_t", "x3t_ready", "fqk_ps",
            "fqk_ready", "fv_ps", "fv_ready", "fscores", "fmaxed", "fneg", "fprobs", "frecip", "fpn_ready", "fp_t",
            "fpt_ready", "fat_ps", "fat_ready", "self_ps", "x4_ready", "x4_t", "x4t_ready"))
        (gate_ps, logits, gmaxed, gshifted, gexp, gsummed, grecip, gate_ready, gate_t, gt_ready, bias_ps, x24_ready,
         acc_first, hid_ps, hid_ready, exp_ps, expert) = (sem(n) for n in (
            "gate_ps", "logits", "gmaxed", "gshifted", "gexp", "gsummed", "grecip", "gate_ready", "gate_t", "gt_ready",
            "bias_ps", "x24_ready", "acc_first", "hid_ps", "hid_ready", "exp_ps", "expert"))

        block = ctx.enter_context(nc.Block())

        def col(name, i=0, n=1):
            return cv[:, COL[name][0] + i:COL[name][0] + i + n]

        def bcast(name):
            return rw[:, ROW[name][0]:ROW[name][0] + ROW[name][1]]

        w_in_t = wm[:, 0:512]
        w_x = wm[:, 512:512 + 66].rearrange("p (h m) -> p h m", h=NH)
        w_out = wm[:, 578:578 + 256].rearrange("p (h m) -> p h m", h=NH)
        xwq, xwk, xwv, xwo = (wc[:, i * 128:(i + 1) * 128] for i in range(4))
        fwq, fwk, fwv, fwo = (ws[:, i * 128:(i + 1) * 128] for i in range(4))
        wg = ws[:, 512:512 + E]
        x_tiles = x.rearrange("b s d -> (b s) d").rearrange("(n p) d -> p n d", p=P)
        out_tiles = out.rearrange("b s d -> (b s) d").rearrange("(n p) d -> p n d", p=P)

        def tokens(g):
            return BATCHES[g] * S

        def tiles_of(g):
            return range(BATCHES[g] // 2)

        def in_x(g):
            return slice(FIRST[g] // 2, FIRST[g + 1] // 2)

        def halves(ap, g):
            return ap.rearrange("p (h t) -> p h t", h=NH)[:, :, 0:tokens(g)]

        def tiled(ap, g):
            return ap[:, 0:tokens(g)].rearrange("p (t d) -> p t d", d=D)

        def step_of(buf, i):
            t = tokens(i // STEPS)
            return buf[:, i % 2, 0:NH * 2 * t].rearrange("p (h k t) -> p h k t", h=NH, k=2)

        @block.sync
        def _(sp):
            sp.dma_start(X[:, in_x(0), :], x_tiles[:, in_x(0), :]).then_inc(x_in[0], 16)
            sp.dma_start(cv[:, :], cols).then_inc(vec_in, 16)
            sp.dma_start(wm[:, :], w_mamba).then_inc(wm_in, 16)
            sp.dma_start(rw[:, :], row.to_broadcast([P, NROW])).then_inc(row_in, 16)
            sp.dma_start(dtw[32:33, :], dt_row).then_inc(row_in, 16)
            for k in range(2):
                sp.dma_start(CT[:, :, k, :], ctx_t.rearrange("d (b s) -> d b s", b=B)).then_inc(ctx_in, 16)
            sp.dma_start(wc[:, :], w_cross).then_inc(wc_in, 16)
            for g in range(1, NG):
                sp.dma_start(X[:, in_x(g), :], x_tiles[:, in_x(g), :]).then_inc(x_in[g], 16)
            sp.dma_start(ws[:, :], w_self).then_inc(ws_in, 16)
            sp.dma_start(b2s[:, :], b2).then_inc(b2_in, 16)
            sp.dma_start(w1[:, :, :], W1.rearrange("e h f -> h e f")).then_inc(w1_in, 16)
            sp.dma_start(w2[:, :, :], W2.rearrange("e (t p) h -> p (e t) h", p=P)).then_inc(w2_in, 16)
            for g in range(NG):
                sp.wait_ge(expert, E * (g + 1))
                sp.dma_start(out_tiles[:, in_x(g), :], acc[:, in_x(g), :]).then_inc(out_done, 16)
            sp.wait_ge(out_done, 16 * NG)

        @block.gpsimd
        def _(pool):
            done = [0]

            def step(ins):
                done[0] += 1
                ins.then_inc(pool_step, 1)
                pool.wait_ge(pool_step, done[0])

            step(nc.gpsimd.memset(ident[:, :], 0.0))
            nc.gpsimd.affine_select(out=ident[:, :], in_=ident[:, :], compare_op=ALU.not_equal, fill=1.0, base=0,
                                    pattern=[[-1, P]], channel_multiplier=1).then_inc(pool_const, 1)
            step(nc.gpsimd.memset(head[:, :], 1.0))
            for k in range(2):
                part = head[k * S:(k + 1) * S, :]
                step(nc.gpsimd.affine_select(out=part, in_=part, compare_op=ALU.is_ge, fill=0.0, base=0,
                                             pattern=[[-HD, HG]], channel_multiplier=1))
                step(nc.gpsimd.affine_select(out=part, in_=part, compare_op=ALU.is_ge, fill=0.0, base=HD - 1,
                                             pattern=[[HD, HG]], channel_multiplier=-1))
            step(nc.gpsimd.memset(pick[:, :], 0.0))
            for j in range(3):
                last = nc.gpsimd.affine_select(out=pick[:, :], in_=pick[:, :], compare_op=ALU.not_equal, fill=1.0,
                                               base=-2 * N * j, pattern=[[-1, 2 * N]], channel_multiplier=1)
                if j < 2:
                    step(last)
            last.then_inc(pool_const, 1)

            def keys(g):
                pool.wait_ge(k_ready, g + 1)
                if g:
                    pool.wait_ge(scores, FIRST[g])
                for b in range(BATCHES[g]):
                    last = nc.gpsimd.tensor_tensor(
                        kx[:, b, :, :],
                        kt[:, b * S:(b + 1) * S].unsqueeze(1).to_broadcast([P, HG, S]),
                        head[:, :].unsqueeze(2).to_broadcast([P, HG, S]), ALU.mult)
                last.then_inc(kx_ready, 1)

            def scan(g, p):
                i = STEPS * g + p
                if p == 0:
                    pool.wait_ge(skip, g + 1)
                if i:
                    pool.wait_ge(summed, i)
                pool.wait_ge(weighted, i + 1)
                h, t = step_of(hs, i), tokens(g)
                nc.gpsimd.tensor_tensor(pair[:, :, 0:t], h[:, :, 0, :], h[:, :, 1, :], ALU.add).then_inc(paired, 1)
                pool.wait_ge(paired, i + 1)
                nc.gpsimd.tensor_tensor(yacc[:, g % 2, :, 0:t], yacc[:, g % 2, :, 0:t], pair[:, :, 0:t],
                                        ALU.add).then_inc(summed, 1)

            def front(g, piece):
                t = tokens(g)
                if piece == "cap_u" and g:
                    pool.wait_ge(exp_u, g + 1)
                    nc.gpsimd.tensor_scalar(eu[:, :, 0:t], eu[:, :, 0:t], CAP, None, ALU.min).then_inc(cap_u, 1)
                elif piece == "ssm":
                    pool.wait_ge(u_ready, g + 1)
                    if g >= 2:
                        pool.wait_ge(mean_ps, g - 1)
                        pool.wait_ge(centred, g - 1)
                    for h in range(NH):
                        last = nc.gpsimd.tensor_scalar(yacc[:, g % 2, h, 0:t], u[:, g % 2, h, 0:t], col("D", h), None,
                                                       ALU.mult)
                    last.then_inc(skip, 1)
                elif piece == "cap_dt" and g:
                    pool.wait_ge(exp_dt, g + 1)
                    nc.gpsimd.tensor_scalar(de[:, :, 0:t], de[:, :, 0:t], 1.0, None, ALU.min).then_inc(dt_min, 1)
                elif piece == "du" and g:
                    pool.wait_ge(delta, g + 1)
                    pool.wait_ge(u_ready, g + 1)
                    if g >= 2:
                        pool.wait_ge(dbu_ready, STEPS * (g - 1))
                    nc.gpsimd.tensor_tensor(du[:, g % 2, :, 0:t], dlt[:, g % 2, :, 0:t], u[:, g % 2, :, 0:t],
                                            ALU.mult).then_inc(du_ready, 1)
                elif piece == "cap_z" and g:
                    pool.wait_ge(exp_z, g + 1)
                    nc.gpsimd.tensor_scalar(ez[:, :, 0:t], ez[:, :, 0:t], CAP, None, ALU.min).then_inc(cap_z, 1)
                elif piece == "keys_out":
                    keys(g)

            def mid(g, piece):
                n = BATCHES[g] // 2
                if piece == "x1b":
                    pool.wait_ge(x1_ready, g + 1)
                    if g:
                        pool.wait_ge(x2_ready, g)
                    nc.gpsimd.tensor_tensor(x1b[:, 0:n, :], x1[:, g % 2, 0:n, :],
                                            bcast("x_bo").unsqueeze(1).to_broadcast([P, n, D]),
                                            ALU.add).then_inc(x1b_ready, 1)
                elif piece == "x3b":
                    pool.wait_ge(normed3, g + 1)
                    if g:
                        pool.wait_ge(x4_ready, g)
                    nc.gpsimd.tensor_tensor(x3b[:, 0:n, :], xn3[:, 0:n, :],
                                            bcast("f_bo").unsqueeze(1).to_broadcast([P, n, D]),
                                            ALU.add).then_inc(x3b_ready, 1)
                elif piece == "x24":
                    pool.wait_ge(x4_ready, g + 1)
                    if g:
                        pool.wait_ge(acc_first, g)
                    nc.gpsimd.tensor_tensor(x24[:, 0:n, :], x2[:, g % 2, 0:n, :], x4[:, 0:n, :],
                                            ALU.add).then_inc(x24_ready, 1)

            for what, g, piece in timetable():
                if what == "scan" and piece[1] == "read":
                    scan(g, piece[0])
                elif what == "front":
                    front(g, piece)
                elif what == "mid":
                    mid(g, piece)

        @block.scalar
        def _(act):
            nc.scalar.preload_act_table_set("natural_log_exp_and_others")
            act.wait_ge(vec_in, 16)
            nc.scalar.activation(expA[:, :], col("log_A", 0, 2 * N), ACT.Exp).then_inc(expA_ready, 1)
            act.wait_ge(dve_const, 1)

            def rsqrt(g, mv_, lv_, rs_, ready, ln_done, done):
                act.wait_ge(ready, g + 1)
                n = BATCHES[g] // 2
                nc.scalar.activation(lv_[:, g, 0:n], mv_[:, g, 0:n, 1], ACT.Ln, bias=eps[:, :]).then_inc(ln_done, 1)
                act.wait_ge(ln_done, g + 1)
                nc.scalar.activation(rs_[:, g, 0:n], lv_[:, g, 0:n], ACT.Exp, scale=-0.5).then_inc(done, 1)

            def front(g, piece):
                t = tokens(g)
                if piece == "rstd":
                    rsqrt(g, mv, lv, rs, mean_var, ln_var, rstd)
                elif piece == "pad":
                    act.wait_ge(normed_t, g + 1)
                    nc.scalar.activation(xp[:, FIRST[g]:FIRST[g + 1], PAD:SP],
                                         pF[:, 0:t].rearrange("p (b s) -> p b s", s=S), ACT.Copy).then_inc(padded, 1)
                elif piece == "exp_u":
                    act.wait_ge(inner, g + 1)
                    if g:
                        act.wait_ge(u_ready, g)
                    for h in range(NH):
                        last = nc.scalar.activation(eu[:, h, 0:t], halves(pF[:, :], g)[:, h, :], ACT.Exp, scale=-1.0,
                                                    bias=ncb[:, h:h + 1])
                    last.then_inc(exp_u, 1)
                elif piece == "sig_u":
                    act.wait_ge(cap_u, g + 1)
                    nc.scalar.activation(eu[:, :, 0:t], eu[:, :, 0:t], ACT.Ln, bias=one[:, :]).then_inc(ln_u, 1)
                    act.wait_ge(ln_u, g + 1)
                    nc.scalar.activation(eu[:, :, 0:t], eu[:, :, 0:t], ACT.Exp, scale=-1.0).then_inc(sig_u, 1)
                elif piece == "ssm_out":
                    act.wait_ge(ssm_ps, g + 1)
                    nc.scalar.activation(ssm[:, g % 2, 0:t], pF[0:33, 0:t], ACT.Copy).then_inc(ssm_ready, 1)
                elif piece == "exp_dt":
                    act.wait_ge(dt_ps, g + 1)
                    if g:
                        act.wait_ge(delta, g)
                    for h in range(NH):
                        last = nc.scalar.activation(de[:, h, 0:t], halves(pF[:, :], g)[:, h, :], ACT.Exp,
                                                    bias=col("dt_b", h))
                    last.then_inc(exp_dt, 1)
                elif piece == "ln_dt":
                    act.wait_ge(dt_min, g + 1)
                    nc.scalar.activation(de[:, :, 0:t], de[:, :, 0:t], ACT.Ln, bias=one[:, :]).then_inc(ln_dt, 1)
                elif piece == "exp_z":
                    act.wait_ge(z_ps, g + 1)
                    if g:
                        act.wait_ge(sz_ready, g)
                    nc.scalar.activation(ez[:, :, 0:t], halves(pF[:, :], g), ACT.Exp, scale=-1.0).then_inc(exp_z, 1)
                elif piece == "sig_z":
                    act.wait_ge(cap_z, g + 1)
                    nc.scalar.activation(ez[:, :, 0:t], ez[:, :, 0:t], ACT.Ln, bias=one[:, :]).then_inc(ln_z, 1)
                    act.wait_ge(ln_z, g + 1)
                    nc.scalar.activation(ez[:, :, 0:t], ez[:, :, 0:t], ACT.Exp, scale=-1.0).then_inc(sig_z, 1)
                elif piece == "keys_out":
                    act.wait_ge(k_ps, g + 1)
                    if g:
                        act.wait_ge(kx_ready, g)
                    nc.scalar.activation(kt[:, 0:t], pF[:, 0:t], ACT.Identity, bias=col("x_bk")).then_inc(k_ready, 1)

            def decays(g, p):
                i = STEPS * g + p
                if p == 0:
                    act.wait_ge(delta, g + 1)
                if i >= 2:
                    act.wait_ge(state, i - 1)
                for h in range(NH):
                    for k in range(2):
                        a = h * N + 2 * p + k
                        last = nc.scalar.activation(
                            step_of(dA, i)[:, h, k, :].rearrange("p (b s) -> p b s", s=S)[:, :, 1:S],
                            dlt[:, g % 2, h, 0:tokens(g)].rearrange("p (b s) -> p b s", s=S)[:, :, 1:S],
                            ACT.Exp, scale=negA[:, a:a + 1])
                last.then_inc(decay, 1)

            def scan(g, piece):
                p, op = piece
                if p == 0 and op == "scan":
                    decays(g, 0)
                if op == "inject" and p + 1 < STEPS:
                    decays(g, p + 1)

            def weights(j):
                act.wait_ge(shifted, j + 1)
                nc.scalar.activation(sd[:, j % 2, :, :], sd[:, j % 2, :, :], ACT.Exp, scale=X_SCALE).then_inc(probs, 1)

            def weights_t(j):
                act.wait_ge(probs_t, j + 1)
                nc.scalar.activation(pt[:, j % 2, :, :], (pX, pY)[j % 2][:, :].rearrange("p (h t) -> p h t", t=P),
                                     ACT.Copy).then_inc(pt_ready, 1)

            def mid(g, piece):
                t = tokens(g)
                j = FIRST[g] + int(piece[-1]) if " " in piece else None
                if piece == "square":
                    act.wait_ge(centred, g + 1)
                    nc.scalar.activation(sq[:, :, 0:t], yc[:, :, 0:t], ACT.Square).then_inc(squared, 1)
                elif piece == "rstd_y":
                    act.wait_ge(var_ps, g + 1)
                    nc.scalar.activation(lnv[:, 0:t], pX[:, 0:t], ACT.Ln, bias=eps[:, :]).then_inc(ln_y, 1)
                    act.wait_ge(ln_y, g + 1)
                    nc.scalar.activation(rsv[:, 0:t], lnv[:, 0:t], ACT.Exp, scale=-0.5).then_inc(rstd_y, 1)
                elif piece == "rstd2":
                    rsqrt(g, mv2, lv2, rs2, mean_var2, ln_var2, rstd2)
                elif piece == "turn2_out":
                    act.wait_ge(normed2_t, g + 1)
                    nc.scalar.activation(x2t[:, 0:t], pX[:, 0:t], ACT.Copy).then_inc(x2t_ready, 1)
                elif piece == "query_out":
                    act.wait_ge(q_ps, g + 1)
                    if g == 0:
                        act.wait_ge(dve_const, 4)
                    for k in range(2):
                        rng = slice(k * S, (k + 1) * S)
                        last = nc.scalar.activation(qt[rng, 0:BATCHES[g], k, :], pX[rng,
                                0:t].rearrange("p (b s) -> p b s", s=S),
                                                    ACT.Identity, bias=col("x_bq")[rng])
                    last.then_inc(q_ready, 1)
                elif piece.startswith("exp "):
                    weights(j)
                elif piece.startswith("turn_out "):
                    weights_t(j)
                elif piece == "heads_out":
                    act.wait_ge(ov_t, g + 1)
                    nc.scalar.activation(ot[:, 0:t], pX[:, 0:t], ACT.Copy).then_inc(ot_ready, 1)
                elif piece == "rstd3":
                    rsqrt(g, mv3, lv3, rs3, mean_var3, ln_var3, rstd3)
                elif piece == "turn3_out":
                    act.wait_ge(normed3_t, g + 1)
                    nc.scalar.activation(x3t[:, 0:t], pX[:, 0:t], ACT.Copy).then_inc(x3t_ready, 1)
                elif piece == "fqk_out":
                    act.wait_ge(fqk_ps, g + 1)
                    nc.scalar.activation(fq[:, 0:t], pX[:, 0:t], ACT.Identity, bias=col("f_bq"))
                    nc.scalar.activation(fk[:, 0:t], pX[:, T:T + t], ACT.Identity,
                                         bias=col("f_bk")).then_inc(fqk_ready, 1)
                elif piece == "fexp":
                    act.wait_ge(fneg, g + 1)
                    for n in tiles_of(g):
                        last = nc.scalar.activation(fp[:, n, :], pX[:, n * S:(n + 1) * S], ACT.Exp, scale=F_SCALE,
                                                    bias=fnb[:, n:n + 1], accum_out=fs[:, n:n + 1])
                    last.then_inc(fprobs, 1)
                elif piece == "fturn_out":
                    act.wait_ge(fp_t, g + 1)
                    nc.scalar.activation(fpt[:, 0:t], pY[0:S, 0:t], ACT.Copy).then_inc(fpt_ready, 1)
                elif piece == "fapply_out":
                    act.wait_ge(fat_ps, g + 1)
                    nc.scalar.activation(fat[:, 0:t], pX[:, 0:t], ACT.Identity, bias=col("f_bv")).then_inc(fat_ready, 1)
                elif piece == "turn4_out":
                    act.wait_ge(x4_t, g + 1)
                    if g >= 2:
                        act.wait_ge(hid_ps, TILES * (g - 1))
                    nc.scalar.activation(x4t[:, g % 2, 0:t], pX[:, 0:t], ACT.Copy).then_inc(x4t_ready, 1)
                elif piece == "gexp":
                    act.wait_ge(gshifted, g + 1)
                    n = BATCHES[g] // 2
                    nc.scalar.activation(ge[:, 0:n, :], gd[:, 0:n, :], ACT.Exp).then_inc(gexp, 1)
                elif piece == "gturn_out":
                    act.wait_ge(gate_t, g + 1)
                    nc.scalar.activation(gt[:, 0:t], pX[0:E, 0:t], ACT.Copy).then_inc(gt_ready, 1)

            def experts(g, f):
                i = TILES * g + f
                act.wait_ge(hid_ps, i + 1)
                if i >= 4:
                    act.wait_ge(exp_ps, i - 3)
                nc.scalar.activation(hid[:, i % 4, 0:tokens(g)], pH[:, i % 2, 0:tokens(g)], ACT.Relu,
                                     bias=col("b1", f)).then_inc(hid_ready, 1)

            for what, g, piece in timetable():
                {"front": front, "scan": scan, "mid": mid, "experts": experts}[what](g, piece)

        @block.tensor
        def _(pe):
            def front(g, piece):
                if piece == "turn":
                    if g == 0:
                        pe.wait_ge(pool_const, 1)
                    elif g == 1:
                        pe.wait_ge(sz_ready, g)
                    else:
                        pe.wait_ge(vx_ready, g - 1)
                    pe.wait_ge(normed, g + 1)
                    for t in tiles_of(g):
                        last = nc.tensor.transpose(pF[:, t * P:(t + 1) * P], xn[:, t, :], ident[:, :])
                    last.then_inc(normed_t, 1)
                elif piece in ("conv_0", "conv_1"):
                    h = int(piece[-1])
                    if h == 0:
                        if g == 0:
                            pe.wait_ge(dve_const, 2)
                        pe.wait_ge(padded, g + 1)
                    for k in range(TAPS):
                        last = nc.tensor.matmul(halves(pF[:, :], g)[:, h, :], wconv[:, k, h * P:(h + 1) * P],
                                                xp[:, FIRST[g]:FIRST[g + 1], k:k + S], start=(k == 0),
                                                    stop=(k == TAPS - 1))
                    if h == NH - 1:
                        last.then_inc(inner, 1)
                elif piece == "ssm":
                    pe.wait_ge(exp_u, g + 1)
                    pe.wait_ge(u_ready, g + 1)
                    for h in range(NH):
                        last = nc.tensor.matmul(pF[0:33, 0:tokens(g)], w_x[:, h, :], u[:, g % 2, h, 0:tokens(g)],
                                                start=(h == 0), stop=(h == NH - 1))
                    last.then_inc(ssm_ps, 1)
                elif piece == "dt":
                    if g == 0:
                        pe.wait_ge(row_in, 32)
                    pe.wait_ge(ssm_ready, g + 1)
                    for h in range(NH):
                        last = nc.tensor.matmul(halves(pF[:, :], g)[:, h, :], dtw[32:33, h * P:(h + 1) * P],
                                                ssm[32:33, g % 2, 0:tokens(g)], start=True, stop=True)
                    last.then_inc(dt_ps, 1)
                elif piece == "cap_dt":
                    pe.wait_ge(exp_dt, g + 1)
                    for h in range(NH):
                        last = nc.tensor.matmul(halves(pF[:, :], g)[:, h, :], w_in_t[:, DI + h * P:DI + (h + 1) * P],
                                                xp[:, FIRST[g]:FIRST[g + 1], PAD:SP], start=True, stop=True)
                    last.then_inc(z_ps, 1)
                elif piece == "keys":
                    if g == 0:
                        pe.wait_ge(ctx_in, 32)
                        pe.wait_ge(wc_in, 16)
                    pe.wait_ge(sz_ready, min(g + 2, NG))
                    nc.tensor.matmul(pF[:, 0:tokens(g)], xwk, CT[:, FIRST[g]:FIRST[g + 1], 0, :], start=True,
                                     stop=True).then_inc(k_ps, 1)
                elif piece == "values":
                    pe.wait_ge(k_ready, g + 1)
                    for b in range(BATCHES[g]):
                        last = nc.tensor.matmul(pF[:, b * D:(b + 1) * D], CT[:, FIRST[g] + b, :, :], xwv,
                                                start=True, stop=True)
                    last.then_inc(v_ps, 1)

            def spread_b(i):
                g, p = divmod(i, STEPS)
                if i % STEPS == 0:
                    pe.wait_ge(split, g + 1)
                if i == 0:
                    pe.wait_ge(pool_const, 2)
                else:
                    pe.wait_ge(dbu_ready, i)
                for k in range(2):
                    last = nc.tensor.matmul(pB[:, k, 0:tokens(g)], pick[:,
                                                                        2 * p + k:2 * p + k + 1].to_broadcast([96, P]),
                                            bc[:, g % 2, 0:tokens(g)], start=True, stop=True)
                last.then_inc(b_ps, 1)

            def scan(g, piece):
                p, op = piece
                i = STEPS * g + p
                if op == "scan":
                    if p == 0:
                        spread_b(i)
                    if i:
                        pe.wait_ge(weighted, i)
                    for k in range(2):
                        last = nc.tensor.matmul(pC[:, k, 0:tokens(g)],
                                                pick[:, N + 2 * p + k:N + 2 * p + k + 1].to_broadcast([96, P]),
                                                bc[:, g % 2, 0:tokens(g)], start=True, stop=True)
                    last.then_inc(c_ps, 1)
                    if p + 1 < STEPS:
                        spread_b(i + 1)

            def score(g, j):
                b = j - FIRST[g]
                bank = (pX, pY)[j % 2]
                nc.tensor.matmul(bank[:, :], early_q[0:1, :], late_k[0:1, :], start=True, stop=False,
                                 skip_group_check=True)
                nc.tensor.matmul(bank[:, :], qt[:, b, :, :], kx[:, b, :, :], start=False, stop=True,
                                 skip_group_check=True).then_inc(scores, 1)

            def turn(j):
                pe.wait_ge(probs, j + 1)
                for q in range(HP // 2):
                    last = nc.tensor.transpose((pX, pY)[j % 2][:, q * P:(q + 1) * P],
                                               sd[:, j % 2, 2 * q:2 * q + 2, :], ident[:, :])
                last.then_inc(probs_t, 1)

            def apply(g, j):
                b, rows_ = j - FIRST[g], slice((j % 2) * S, (j % 2 + 1) * S)
                pe.wait_ge(pt_ready, j + 1)
                pe.wait_ge(vx_ready, g + 1)
                for k in range(2):
                    for q in range(HG // 2):
                        at = k * (HG // 2) + q
                        last = nc.tensor.matmul((pX, pY)[j % 2][rows_, at * VW:(at + 1) * VW],
                                                pt[:, j % 2, q, k * S:(k + 1) * S], vx[:, g % 2, b, at, :],
                                                start=True, stop=True)
                last.then_inc(pv_ps, 1)

            def mid(g, piece):
                t = tokens(g)
                j = FIRST[g] + int(piece[-1]) if " " in piece else None
                if piece == "mean":
                    pe.wait_ge(summed, STEPS * (g + 1))
                    if g:
                        pe.wait_ge(acc_first, g)
                    for h in range(NH):
                        last = nc.tensor.matmul(pX[:, 0:t], mean_w[:, :], yacc[:, g % 2, h, 0:t],
                                                start=(h == 0), stop=(h == NH - 1))
                    last.then_inc(mean_ps, 1)
                elif piece == "var":
                    pe.wait_ge(centred, g + 1)
                    pe.wait_ge(squared, g + 1)
                    for h in range(NH):
                        last = nc.tensor.matmul(pX[:, 0:t], mean_w[:, :], sq[:, h, 0:t],
                                                start=(h == 0), stop=(h == NH - 1))
                    last.then_inc(var_ps, 1)
                elif piece == "back":
                    pe.wait_ge(ln_y, g + 1)
                    pe.wait_ge(gated, g + 1)
                    for t in tiles_of(g):
                        for h in range(NH):
                            last = nc.tensor.matmul(pX[:, t * D:(t + 1) * D], gy[:, h, t * P:(t + 1) * P],
                                                    w_out[:, h, :], start=(h == 0), stop=(h == NH - 1))
                    last.then_inc(back_ps, 1)
                elif piece == "turn2":
                    pe.wait_ge(x1_ready, g + 1)
                    pe.wait_ge(normed2, g + 1)
                    for t in tiles_of(g):
                        last = nc.tensor.transpose(pX[:, t * P:(t + 1) * P], xn2[:, t, :], ident[:, :])
                    last.then_inc(normed2_t, 1)
                elif piece == "query":
                    pe.wait_ge(x2t_ready, g + 1)
                    nc.tensor.matmul(pX[:, 0:t], xwq, x2t[:, 0:t], start=True, stop=True).then_inc(q_ps, 1)
                elif piece.startswith("scores "):
                    if j < FIRST[g] + 2:
                        pe.wait_ge(q_ready, g + 1)
                        pe.wait_ge(kx_ready, g + 1)
                    else:
                        pe.wait_ge(ov_ready, j - 1)
                    score(g, j)
                elif piece.startswith("turn "):
                    turn(j)
                elif piece.startswith("apply "):
                    apply(g, j)
                elif piece == "heads":
                    pe.wait_ge(ov_ready, FIRST[g + 1])
                    for t in tiles_of(g):
                        last = nc.tensor.transpose(pX[:, t * P:(t + 1) * P], ov[:, t, :, :], ident[:, :])
                    last.then_inc(ov_t, 1)
                elif piece == "cross":
                    pe.wait_ge(ot_ready, g + 1)
                    for t in tiles_of(g):
                        last = nc.tensor.matmul(pX[:, t * D:(t + 1) * D], ot[:, t * P:(t + 1) * P], xwo,
                                                start=True, stop=True)
                    last.then_inc(cross_ps, 1)
                elif piece == "turn3":
                    pe.wait_ge(x2_ready, g + 1)
                    pe.wait_ge(normed3, g + 1)
                    for t in tiles_of(g):
                        last = nc.tensor.transpose(pX[:, t * P:(t + 1) * P], xn3[:, t, :], ident[:, :])
                    last.then_inc(normed3_t, 1)
                elif piece == "fqk":
                    pe.wait_ge(x3t_ready, g + 1)
                    if g == 0:
                        pe.wait_ge(ws_in, 16)
                    nc.tensor.matmul(pX[:, 0:t], fwq, x3t[:, 0:t], start=True, stop=True)
                    nc.tensor.matmul(pX[:, T:T + t], fwk, x3t[:, 0:t], start=True, stop=True).then_inc(fqk_ps, 1)
                    for b in range(BATCHES[g]):
                        last = nc.tensor.matmul(pY[0:S, b * D:(b + 1) * D], x3t[:, b * S:(b + 1) * S], fwv,
                                                start=True, stop=True)
                    last.then_inc(fv_ps, 1)
                elif piece == "fscores":
                    pe.wait_ge(fqk_ready, g + 1)
                    for n in tiles_of(g):
                        for b in range(2):
                            c = n * P + b * S
                            last = nc.tensor.matmul(pX[b * S:(b + 1) * S, n * S:(n + 1) * S], fq[:, c:c + S],
                                                    fk[:, c:c + S], start=True, stop=True)
                    last.then_inc(fscores, 1)
                elif piece == "fturn":
                    pe.wait_ge(fv_ready, g + 1)
                    pe.wait_ge(fpn_ready, g + 1)
                    for t in tiles_of(g):
                        last = nc.tensor.transpose(pY[0:S, t * P:(t + 1) * P], fpn[:, t, :], ident[:, :])
                    last.then_inc(fp_t, 1)
                elif piece == "fapply":
                    pe.wait_ge(fpt_ready, g + 1)
                    for b in range(BATCHES[g]):
                        last = nc.tensor.matmul(pX[:, b * S:(b + 1) * S], fv[:, b, :], fpt[:, b * S:(b + 1) * S],
                                                start=True, stop=True)
                    last.then_inc(fat_ps, 1)
                elif piece == "self":
                    pe.wait_ge(fat_ready, g + 1)
                    for t in tiles_of(g):
                        last = nc.tensor.matmul(pX[:, t * D:(t + 1) * D], fat[:, t * P:(t + 1) * P], fwo,
                                                start=True, stop=True)
                    last.then_inc(self_ps, 1)
                elif piece == "turn4":
                    pe.wait_ge(x4_ready, g + 1)
                    for t in tiles_of(g):
                        last = nc.tensor.transpose(pX[:, t * P:(t + 1) * P], x4[:, t, :], ident[:, :])
                    last.then_inc(x4_t, 1)
                elif piece == "gates":
                    pe.wait_ge(x4t_ready, g + 1)
                    for t in tiles_of(g):
                        last = nc.tensor.matmul(pX[:, t * E:(t + 1) * E], x4t[:, g % 2, t * P:(t + 1) * P], wg,
                                                start=True, stop=True)
                    last.then_inc(gate_ps, 1)
                elif piece == "gturn":
                    pe.wait_ge(gate_ready, g + 1)
                    for t in tiles_of(g):
                        last = nc.tensor.transpose(pX[0:E, t * P:(t + 1) * P], gate[:, g % 2, t, :], ident[:, :])
                    last.then_inc(gate_t, 1)
                elif piece == "bias":
                    pe.wait_ge(gt_ready, g + 1)
                    if g == 0:
                        pe.wait_ge(b2_in, 16)
                    for t in tiles_of(g):
                        last = nc.tensor.matmul(pX[:, t * D:(t + 1) * D], gt[:, t * P:(t + 1) * P], b2s[:, :],
                                                start=True, stop=True)
                    last.then_inc(bias_ps, 1)

            def second(g, f):
                i = TILES * g + f
                pe.wait_ge(hid_ready, i + 1)
                n = E * g + f // FT
                if f % FT == 0 and n:
                    pe.wait_ge(expert, n)
                for t in tiles_of(g):
                    last = nc.tensor.matmul(pE[:, t * D:(t + 1) * D], hid[:, i % 4, t * P:(t + 1) * P],
                                            w2[:, f, :], start=(f % FT == 0 and t == 0), stop=(f % FT == FT - 1),
                                            skip_group_check=True)
                last.then_inc(exp_ps, 1)

            def experts(g, f):
                i = TILES * g + f
                if i == 0:
                    pe.wait_ge(w1_in, 16)
                    pe.wait_ge(w2_in, 16)
                if f == 0:
                    pe.wait_ge(x4t_ready, g + 1)
                if i >= 2:
                    pe.wait_ge(hid_ready, i - 1)
                nc.tensor.matmul(pH[:, i % 2, 0:tokens(g)], w1[:, f // FT, (f % FT) * P:(f % FT + 1) * P],
                                 x4t[:, g % 2, 0:tokens(g)], start=True, stop=True).then_inc(hid_ps, 1)
                if f:
                    second(g, f - 1)
                if f == TILES - 1:
                    second(g, f)

            for what, g, piece in timetable():
                {"front": front, "scan": scan, "mid": mid, "experts": experts}[what](g, piece)

        @block.vector
        def _(dve):
            nc.vector.memset(eps[:, :], EPS)
            nc.vector.memset(one[:, :], 1.0)
            nc.vector.memset(mean_w[:, :], 1.0 / DI)
            nc.vector.memset(early_q[0:1, :].rearrange("p (b s) -> p b s", s=S)[:, :, 0:CHUNK], 1.0)
            nc.vector.memset(early_q[0:1, :].rearrange("p (b s) -> p b s", s=S)[:, :, CHUNK:S], 0.0)
            nc.vector.memset(late_k[0:1, :].rearrange("p (b s) -> p b s", s=S)[:, :, 0:CHUNK], 0.0)
            nc.vector.memset(late_k[0:1, :].rearrange("p (b s) -> p b s", s=S)[:, :, CHUNK:S], MASKED)
            nc.vector.memset(xp[:, :, 0:PAD], 0.0)
            nc.vector.memset(dA[:, :, :].rearrange("p a (n s) -> p (a n) s", s=S)[:, :, 0:1], 0.0)
            dve.wait_ge(vec_in, 16)
            nc.vector.tensor_scalar(ncb[:, :], col("conv_b", 0, NH), -1.0, None, ALU.mult)
            dve.wait_ge(expA_ready, 1)
            nc.vector.tensor_scalar(negA[:, :], expA[:, :], -1.0, None, ALU.mult).then_inc(dve_const, 1)
            dve.wait_ge(row_in, 32)
            dve.wait_ge(wm_in, 16)
            nc.vector.tensor_tensor(wconv[:, :, :], bcast("conv_w").rearrange("p (k c) -> p k c", k=TAPS),
                                    w_in_t[:, 0:DI].unsqueeze(1).to_broadcast([P, TAPS, DI]),
                                    ALU.mult).then_inc(dve_const, 1)
            nc.vector.memset(vx[:, :, :, :, :].rearrange("p a b q w -> p (a b q w)"), 0.0).then_inc(dve_const, 1)
            dve.wait_ge(dve_const, 3)
            nc.vector.memset(qt[:, :, :, :], 0.0)
            vxf = vx[:, :, :, :, :].rearrange("p a b q w -> p (a b q) w")
            nc.vector.memset(vxf[0:S, :, HD:HD + 1], 1.0)
            nc.vector.memset(vxf[S:P, :, VW - 1:VW], 1.0).then_inc(dve_const, 1)

            def statistics(g, src, st_, mv_, s_stats, s_mv):
                for t in tiles_of(g):
                    last = nc.vector.bn_stats(st_[:, g, t, :], src(t))
                last.then_inc(s_stats, 1)
                dve.wait_ge(s_stats, g + 1)
                for t in tiles_of(g):
                    last = nc.vector.bn_aggr(mv_[:, g, t, :], st_[:, g, t, :])
                last.then_inc(s_mv, 1)

            def normalise(g, src, mv_, rs_, dst, s_mv, s_rstd, s_out):
                dve.wait_ge(s_mv, g + 1)
                dve.wait_ge(s_rstd, g + 1)
                for t in tiles_of(g):
                    last = nc.vector.tensor_scalar(dst(t), src(t), mv_[:, g, t, 0:1], rs_[:, g, t:t + 1],
                                                   ALU.subtract, ALU.mult)
                last.then_inc(s_out, 1)

            def front(g, piece):
                src, n = lambda t: X[:, FIRST[g] // 2 + t, :], tokens(g)
                if piece == "stats":
                    dve.wait_ge(x_in[g], 16)
                    statistics(g, src, st, mv, stats, mean_var)
                elif piece == "norm":
                    if g:
                        dve.wait_ge(normed_t, g)
                    normalise(g, src, mv, rs, lambda t: xn[:, t, :], mean_var, rstd, normed)
                elif piece == "cap_u" and g == 0:
                    dve.wait_ge(exp_u, g + 1)
                    nc.vector.tensor_scalar(eu[:, :, 0:n], eu[:, :, 0:n], CAP, None, ALU.min).then_inc(cap_u, 1)
                elif piece == "u":
                    dve.wait_ge(sig_u, g + 1)
                    if g >= 2:
                        dve.wait_ge(skip, g - 1)
                        dve.wait_ge(du_ready, g - 1)
                    for h in range(NH):
                        last = nc.vector.scalar_tensor_tensor(
                            out=u[:, g % 2, h, 0:n], in0=halves(pF[:, :], g)[:, h, :], scalar=col("conv_b", h),
                            in1=eu[:, h, 0:n], op0=ALU.add, op1=ALU.mult)
                    last.then_inc(u_ready, 1)
                elif piece == "dt":
                    dve.wait_ge(ssm_ready, g + 1)
                    nc.vector.tensor_copy(bc[0:32, g % 2, 0:n], ssm[0:32, g % 2, 0:n]).then_inc(split_step, 1)
                    dve.wait_ge(split_step, 3 * g + 1)
                    nc.vector.tensor_tensor(rem[32:64, 0:n], ssm[0:32, g % 2, 0:n], bc[0:32, g % 2, 0:n],
                                            ALU.subtract).then_inc(split_step, 1)
                elif piece == "exp_dt":
                    dve.wait_ge(split_step, 3 * g + 2)
                    nc.vector.tensor_copy(bc[32:64, g % 2, 0:n], rem[32:64, 0:n]).then_inc(split_step, 1)
                    dve.wait_ge(split_step, 3 * g + 3)
                    nc.vector.tensor_tensor(bc[64:96, g % 2, 0:n], rem[32:64, 0:n], bc[32:64, g % 2, 0:n],
                                            ALU.subtract).then_inc(split, 1)
                elif piece == "cap_dt" and g == 0:
                    dve.wait_ge(exp_dt, g + 1)
                    nc.vector.tensor_scalar(de[:, :, 0:n], de[:, :, 0:n], 1.0, None, ALU.min).then_inc(dt_min, 1)
                elif piece == "delta":
                    dve.wait_ge(ln_dt, g + 1)
                    nc.vector.tensor_scalar(dlt[:, g % 2, :, 0:n], de[:, :, 0:n], 0.001, 0.1, ALU.max,
                                            ALU.min).then_inc(delta, 1)
                elif piece == "du" and g == 0:
                    dve.wait_ge(delta, g + 1)
                    nc.vector.tensor_tensor(du[:, g % 2, :, 0:n], dlt[:, g % 2, :, 0:n], u[:, g % 2, :, 0:n],
                                            ALU.mult).then_inc(du_ready, 1)
                elif piece == "cap_z" and g == 0:
                    dve.wait_ge(exp_z, g + 1)
                    nc.vector.tensor_scalar(ez[:, :, 0:n], ez[:, :, 0:n], CAP, None, ALU.min).then_inc(cap_z, 1)
                elif piece == "silu_z":
                    dve.wait_ge(sig_z, g + 1)
                    nc.vector.tensor_tensor(sz[:, g % 2, :, 0:n], ez[:, :, 0:n], halves(pF[:, :], g),
                                            ALU.mult).then_inc(sz_ready, 1)
                elif piece == "values_out":
                    dve.wait_ge(v_ps, g + 1)
                    dve.wait_ge(dve_const, 4)
                    if g >= 2:
                        dve.wait_ge(pv_ps, FIRST[g - 1])
                    for k in range(2):
                        rng = slice(k * S, (k + 1) * S)
                        val = pF[rng, 0:BATCHES[g] * D].rearrange("p (n k d) -> p k n d", k=2, d=HD)[:, k]
                        bias = bcast("x_bv")[rng].rearrange("p (q k d) -> p k q d", k=2, d=HD)[:, k]
                        place = vx[rng, g % 2, 0:BATCHES[g], :, k * (HD + 1):k * (HD + 1) + HD]
                        last = nc.vector.tensor_tensor(
                            place, val.rearrange("p (b q) d -> p b q d", q=HP),
                            bias.unsqueeze(1).to_broadcast([S, BATCHES[g], HP, HD]), ALU.add)
                    last.then_inc(vx_ready, 1)

            def inject(i):
                g = i // STEPS
                t = tokens(g)
                dve.wait_ge(b_ps, i + 1)
                if i % STEPS == 0:
                    dve.wait_ge(du_ready, g + 1)
                if i >= 2:
                    dve.wait_ge(state, i - 1)
                nc.vector.tensor_tensor(
                    step_of(dBu, i), du[:, g % 2, :, 0:t].unsqueeze(2).to_broadcast([P, NH, 2, t]),
                    pB[:, :, 0:t].unsqueeze(1).to_broadcast([P, NH, 2, t]), ALU.mult).then_inc(dbu_ready, 1)

            def scan(g, piece):
                p, op = piece
                i, t = STEPS * g + p, tokens(g)
                if op == "scan":
                    if p == 0:
                        inject(i)
                    dve.wait_ge(decay, i + 1)
                    dve.wait_ge(dbu_ready, i + 1)
                    if i >= 2:
                        dve.wait_ge(paired, i - 1)
                    nc.vector.tensor_tensor_scan(
                        hs[:, i % 2, 0:NH * 2 * t], dA[:, i % 2, 0:NH * 2 * t], dBu[:, i % 2, 0:NH * 2 * t], 0.0,
                            ALU.mult,
                        ALU.add).then_inc(state, 1)
                elif op == "inject":
                    if p < STEPS - 1:
                        inject(i + 1)
                else:
                    dve.wait_ge(c_ps, i + 1)
                    dve.wait_ge(state, i + 1)
                    nc.vector.tensor_tensor(
                        step_of(hs, i), step_of(hs, i),
                        pC[:, :, 0:t].unsqueeze(1).to_broadcast([P, NH, 2, t]), ALU.mult).then_inc(weighted, 1)

            def shift(j):
                bank = (pX, pY)[j % 2][:, :].rearrange("p (h k) -> p h k", k=S)
                dve.wait_ge(scores, j + 1)
                nc.vector.tensor_reduce(mx[:, j % 2, :], bank, AX_X, ALU.max).then_inc(maxed, 1)
                dve.wait_ge(maxed, j + 1)
                nc.vector.tensor_tensor(sd[:, j % 2, :, :], bank, mx[:, j % 2, :].unsqueeze(2).to_broadcast([P,
                        H // 2, S]),
                                        ALU.subtract).then_inc(shifted, 1)

            def divide(g, j):
                t, rows_ = (j - FIRST[g]) // 2, slice((j % 2) * S, (j % 2 + 1) * S)
                pv = (pX, pY)[j % 2][rows_, 0:HP * VW].rearrange("p (h w) -> p h w", w=HD + 1)
                dve.wait_ge(pv_ps, j + 1)
                nc.vector.reciprocal(rc[rows_, :].unsqueeze(2), pv[:, :, HD:HD + 1]).then_inc(recip, 1)
                dve.wait_ge(recip, j + 1)
                nc.vector.tensor_tensor(ov[rows_, t, :, :], pv[:, :, 0:HD], rc[rows_,
                        :].unsqueeze(2).to_broadcast([S, H, HD]),
                                        ALU.mult).then_inc(ov_ready, 1)

            def mid(g, piece):
                t = tokens(g)
                j = FIRST[g] + int(piece[-1]) if " " in piece else None
                tiles, n = tiled(pX, g), BATCHES[g] // 2
                if piece == "centre":
                    dve.wait_ge(summed, STEPS * (g + 1))
                    dve.wait_ge(mean_ps, g + 1)
                    nc.vector.tensor_tensor(yc[:, :, 0:t], yacc[:, g % 2, :, 0:t],
                                            pX[:, 0:t].unsqueeze(1).to_broadcast([P, NH, t]),
                                            ALU.subtract).then_inc(centred, 1)
                elif piece == "gate_y":
                    dve.wait_ge(rstd_y, g + 1)
                    for h in range(NH):
                        last = nc.vector.scalar_tensor_tensor(out=yn[:, h, 0:t], in0=yc[:, h, 0:t],
                                                              scalar=col("norm_w", h),
                                                              in1=rsv[:, 0:t], op0=ALU.mult, op1=ALU.mult)
                    last.then_inc(scaled, 1)
                    dve.wait_ge(scaled, g + 1)
                    for h in range(NH):
                        last = nc.vector.scalar_tensor_tensor(out=gy[:, h, 0:t], in0=yn[:, h, 0:t],
                                                              scalar=col("norm_b", h),
                                                              in1=sz[:, g % 2, h, 0:t], op0=ALU.add, op1=ALU.mult)
                    last.then_inc(gated, 1)
                elif piece == "x1":
                    dve.wait_ge(back_ps, g + 1)
                    nc.vector.tensor_tensor(x1[:, g % 2, 0:n, :], X[:, in_x(g), :], tiles,
                                            ALU.add).then_inc(x1_ready, 1)
                    dve.wait_ge(x1_ready, g + 1)
                    statistics(g, lambda t: x1[:, g % 2, t, :], st2, mv2, stats2, mean_var2)
                elif piece == "norm2":
                    normalise(g, lambda t: x1[:, g % 2, t, :], mv2, rs2, lambda t: xn2[:, t, :], mean_var2, rstd2,
                              normed2)
                elif piece.startswith("shift "):
                    shift(j)
                elif piece.startswith("divide "):
                    divide(g, j)
                elif piece == "x2":
                    dve.wait_ge(cross_ps, g + 1)
                    dve.wait_ge(x1b_ready, g + 1)
                    nc.vector.tensor_tensor(x2[:, g % 2, 0:n, :], x1b[:, 0:n, :], tiles, ALU.add).then_inc(x2_ready, 1)
                    dve.wait_ge(x2_ready, g + 1)
                    statistics(g, lambda t: x2[:, g % 2, t, :], st3, mv3, stats3, mean_var3)
                elif piece == "norm3":
                    normalise(g, lambda t: x2[:, g % 2, t, :], mv3, rs3, lambda t: xn3[:, t, :], mean_var3, rstd3,
                              normed3)
                elif piece == "fqk_out":
                    dve.wait_ge(fv_ps, g + 1)
                    nc.vector.tensor_copy(fv[:, 0:2 * n, :],
                                          pY[0:S, 0:2 * n * D].rearrange("p (b d) -> p b d", d=D)).then_inc(fv_ready, 1)
                elif piece == "fmax":
                    dve.wait_ge(fscores, g + 1)
                    nc.vector.tensor_reduce(fm[:, 0:n], pX[:, 0:n * S].rearrange("p (t s) -> p t s", s=S), AX_X,
                                            ALU.max).then_inc(fmaxed, 1)
                    dve.wait_ge(fmaxed, g + 1)
                    nc.vector.tensor_scalar(fnb[:, 0:n], fm[:, 0:n], -F_SCALE, None, ALU.mult).then_inc(fneg, 1)
                elif piece == "fdivide":
                    dve.wait_ge(fprobs, g + 1)
                    nc.vector.reciprocal(fr[:, 0:n], fs[:, 0:n]).then_inc(frecip, 1)
                    dve.wait_ge(frecip, g + 1)
                    nc.vector.tensor_tensor(fpn[:, 0:n, :], fp[:, 0:n, :], fr[:, 0:n].unsqueeze(2).to_broadcast([P,
                            n, S]),
                                            ALU.mult).then_inc(fpn_ready, 1)
                elif piece == "x4":
                    dve.wait_ge(self_ps, g + 1)
                    dve.wait_ge(x3b_ready, g + 1)
                    nc.vector.tensor_tensor(x4[:, 0:n, :], x3b[:, 0:n, :], tiles, ALU.add).then_inc(x4_ready, 1)
                elif piece == "logits":
                    dve.wait_ge(gate_ps, g + 1)
                    nc.vector.tensor_tensor(gl[:, 0:n, :], pX[:, 0:n * E].rearrange("p (t e) -> p t e", e=E),
                                            bcast("bg").unsqueeze(1).to_broadcast([P, n, E]),
                                                ALU.add).then_inc(logits, 1)
                    dve.wait_ge(logits, g + 1)
                    nc.vector.tensor_reduce(gm[:, 0:n], gl[:, 0:n, :], AX_X, ALU.max).then_inc(gmaxed, 1)
                    dve.wait_ge(gmaxed, g + 1)
                    nc.vector.tensor_tensor(gd[:, 0:n, :], gl[:, 0:n, :], gm[:, 0:n].unsqueeze(2).to_broadcast([P,
                                                                                                                n, E]),
                                            ALU.subtract).then_inc(gshifted, 1)
                elif piece == "gate":
                    dve.wait_ge(gexp, g + 1)
                    nc.vector.tensor_reduce(gs[:, 0:n], ge[:, 0:n, :], AX_X, ALU.add).then_inc(gsummed, 1)
                    dve.wait_ge(gsummed, g + 1)
                    nc.vector.reciprocal(gr[:, 0:n], gs[:, 0:n]).then_inc(grecip, 1)
                    dve.wait_ge(grecip, g + 1)
                    nc.vector.tensor_tensor(gate[:, g % 2, 0:n, :], ge[:, 0:n, :],
                                            gr[:, 0:n].unsqueeze(2).to_broadcast([P, n, E]),
                                            ALU.mult).then_inc(gate_ready, 1)
                elif piece == "first":
                    dve.wait_ge(bias_ps, g + 1)
                    dve.wait_ge(x24_ready, g + 1)
                    nc.vector.tensor_tensor(acc[:, in_x(g), :], x24[:, 0:n, :], tiles, ALU.add).then_inc(acc_first, 1)

            def add_expert(g, e):
                n = E * g + e
                dve.wait_ge(exp_ps, FT * (n + 1))
                if e:
                    dve.wait_ge(expert, n)
                else:
                    dve.wait_ge(acc_first, g + 1)
                for t in tiles_of(g):
                    last = nc.vector.scalar_tensor_tensor(
                        out=acc[:, FIRST[g] // 2 + t, :], in0=pE[:, t * D:(t + 1) * D],
                        scalar=gate[:, g % 2, t, e:e + 1], in1=acc[:, FIRST[g] // 2 + t, :], op0=ALU.mult, op1=ALU.add)
                last.then_inc(expert, 1)

            def experts(g, f):
                if f and f % FT == 0:
                    add_expert(g, f // FT - 1)
                if f == TILES - 1:
                    add_expert(g, E - 1)

            for what, g, piece in timetable():
                {"front": front, "scan": scan, "mid": mid, "experts": experts}[what](g, piece)


def kernel(**inputs):
    import numpy as _np
    import concourse.bacc as _bacc
    from concourse import mybir as _mybir
    from concourse.bass_utils import run_bass_kernel_spmd as _run

    a = {k: _np.asarray(v) for k, v in inputs.items()}

    def cols_of(v):
        return v.reshape(-1, P).T

    m, xa, f = "L0_attn_", "L0_xattn_", "L0_ffn_"
    laid = {
        "x": a["x"],
        "ctx_t": a["ctx_1024"].reshape(-1, P).T,
        "cols": _np.concatenate(
            [cols_of(a[m + n]) for n in ("conv_b", "dt_proj_b", "D_param", "norm_w", "norm_b")]
            + [a[m + "log_A"].reshape(2, P, 16).transpose(1, 0, 2).reshape(P, 32)]
            + [cols_of(a[n]) for n in (xa + "bq", xa + "bk", f + "bq", f + "bk", f + "bv")]
            + [cols_of(a[f + "b1"].reshape(-1))], axis=1),
        "row": _np.concatenate([a[m + "conv_w"].reshape(256, 4).T.reshape(-1), a[xa + "bv"], a[xa + "bo"],
                                a[f + "bo"], a[f + "bg"]])[None],
        "dt_row": a[m + "dt_proj_w"].reshape(1, 256),
        "w_mamba": _np.concatenate(
            [a[m + "in_proj_w"].T,
             a[m + "x_proj_w"].T.reshape(2, P, 33).transpose(1, 0, 2).reshape(P, 66),
             a[m + "out_proj_w"].T.reshape(2, P, P).transpose(1, 0, 2).reshape(P, 256)], axis=1),
        "w_cross": _np.concatenate([a[xa + n] for n in ("Wq", "Wk", "Wv", "Wo")], axis=1),
        "w_self": _np.concatenate([a[f + n] for n in ("Wq", "Wk", "Wv", "Wo", "Wg")], axis=1),
        "W1": a[f + "W1"],
        "W2": a[f + "W2"],
        "b2": a[f + "b2"],
    }
    nc = _bacc.Bacc("TRN2", target_bir_lowering=False, num_devices=1)
    arrays, args = {}, []
    for name, v in laid.items():
        arrays[f"in_{name}_dram"] = _np.ascontiguousarray(v)
        args.append(nc.dram_tensor(f"in_{name}_dram", v.shape, _mybir.dt.from_np(v.dtype), kind="ExternalInput").ap())
    args.append(nc.dram_tensor("out_0_dram", a["x"].shape, _mybir.dt.float32, kind="ExternalOutput").ap())
    decoder_layer(nc, *args)
    r = _run(nc, [arrays], core_ids=[0])
    return r.results[0]["out_0_dram"]
```
